# Optimizing a Trainium2 kernel written in Bass

```python
import numpy as np
import jax
import jax.numpy as jnp

def _softmax(x, axis=-1):
    return jax.nn.softmax(x, axis=axis)

def _gelu(x):
    return jax.nn.gelu(x, approximate=True)

def _silu(x):
    return jax.nn.silu(x)

def _sigmoid(x):
    return jax.nn.sigmoid(x)

def _layernorm(x, axis=-1, eps=1e-05):
    m = jnp.mean(x, axis=axis, keepdims=True)
    v = jnp.var(x, axis=axis, keepdims=True)
    return (x - m) / jnp.sqrt(v + eps)

def _scatter_add(tgt, idx, src, axis=0):
    return tgt.at[idx].add(src)

def _segment_sum(src, seg, n):
    return jax.ops.segment_sum(src, seg, n)
kernel_name = 'mk_vit_tower_d1_tok_img768_r4_762eba'

def setup_inputs(seed: int=0):
    np.random.seed(seed)
    _w = jnp.asarray

    def _rec_inputs():
        import jax
        import jax.numpy as jnp
        _rk = jax.random.key(seed)
        x = 7.57192e-06 + 1.00007 * jax.random.normal(jax.random.fold_in(_rk, 1), (16, 96, 96, 3), jnp.float32)
        return x
    x = _rec_inputs()

    def _L0_tok_setup():
        import jax, jax.numpy as jnp
        import numpy as np
        PATCH = 16
        DIM = 192
        EPS = 0.001

        def _shifts(x):
            zw = jnp.zeros_like(x[:, :, :1, :])
            right = jnp.concatenate([zw, x[:, :, :-1, :]], axis=2)
            left = jnp.concatenate([x[:, :, 1:, :], zw], axis=2)
            zh = jnp.zeros_like(x[:, :1, :, :])
            down = jnp.concatenate([zh, x[:, :-1, :, :]], axis=1)
            up = jnp.concatenate([x[:, 1:, :, :], zh], axis=1)
            return [right, left, down, up]

        def _patchify(x, p):
            b, H, W, C = x.shape
            hh, ww = (H // p, W // p)
            x = x.reshape(b, hh, p, ww, p, C)
            x = x.transpose(0, 1, 3, 2, 4, 5)
            return x.reshape(b, hh * ww, p * p * C)
        key = jax.random.key(seed)
        k1, k2 = jax.random.split(key)
        b, H, Wd, C = (64, 224, 224, 3)
        F = PATCH * PATCH * 5 * C
        x = jax.random.normal(k1, (b, H, Wd, C), dtype=jnp.float32)
        gamma = jnp.ones((F,), dtype=jnp.float32)
        beta = jnp.zeros((F,), dtype=jnp.float32)
        W = jax.random.normal(k2, (F, DIM), dtype=jnp.float32)
        bb = jnp.zeros((DIM,), dtype=jnp.float32)
        return {'x': x, 'gamma': gamma, 'beta': beta, 'W': W, 'b': bb}
    _L0_tok_all = _L0_tok_setup()
    _L0_tok_in = {k: v for k, v in _L0_tok_all.items() if k in ('gamma', 'beta', 'W', 'b')}
    del _L0_tok_all

    def _L0_attn_setup():
        import jax, jax.numpy as jnp
        import numpy as np
        import math
        D_MODEL = 192
        N_STATES = 16
        D_IN = 2 * D_MODEL
        DT_RANK = math.ceil(D_MODEL / 16)
        KSIZE = 4
        BATCH, SEQ = (2, 256)

        def _mamba_forward(x, W_in, conv_w, conv_b, W_x, W_dt, b_dt, A_log, Dp, W_out):
            b, l, _ = x.shape
            xr = x @ W_in
            xi, res = jnp.split(xr, 2, axis=-1)
            xc = jnp.transpose(xi, (0, 2, 1))
            xc = jax.lax.conv_general_dilated(xc, conv_w, window_strides=(1,), padding=[(KSIZE - 1, 0)], dimension_numbers=('NCH', 'OIH', 'NCH'), feature_group_count=D_IN)
            xc = xc + conv_b[None, :, None]
            xi = jnp.transpose(xc, (0, 2, 1))
            xi = jax.nn.swish(xi)
            A = -jnp.exp(A_log)
            x_dbl = xi @ W_x
            delta, B, C = jnp.split(x_dbl, [DT_RANK, DT_RANK + N_STATES], axis=-1)
            delta = jax.nn.softplus(delta @ W_dt + b_dt)
            dA = jnp.einsum('bld,dn->bldn', delta, A)
            dB_u = jnp.einsum('bld,bld,bln->bldn', delta, xi, B)
            dA_shift = jnp.pad(dA[:, 1:], ((0, 0), (0, 1), (0, 0), (0, 0)))
            dA_cumsum = jnp.exp(jnp.flip(jnp.cumsum(jnp.flip(dA_shift, 1), axis=1), 1))
            x_ss = jnp.cumsum(dB_u * dA_cumsum, axis=1) / (dA_cumsum + 1e-12)
            y = jnp.einsum('bldn,bln->bld', x_ss, C) + xi * Dp
            return y * jax.nn.swish(res) @ W_out
        key = jax.random.key(seed)
        ks = jax.random.split(key, 8)
        s = 0.02
        x = jax.random.normal(ks[0], (BATCH, SEQ, D_MODEL), dtype=jnp.float32)
        W_in = jax.random.normal(ks[1], (D_MODEL, 2 * D_IN), dtype=jnp.float32) * s
        conv_w = jax.random.normal(ks[2], (D_IN, 1, KSIZE), dtype=jnp.float32) * s
        conv_b = jnp.zeros((D_IN,), dtype=jnp.float32)
        W_x = jax.random.normal(ks[3], (D_IN, DT_RANK + 2 * N_STATES), dtype=jnp.float32) * s
        W_dt = jax.random.normal(ks[4], (DT_RANK, D_IN), dtype=jnp.float32) * s
        b_dt = jnp.zeros((D_IN,), dtype=jnp.float32)
        A_log = jnp.log(jnp.broadcast_to(jnp.arange(1, N_STATES + 1, dtype=jnp.float32), (D_IN, N_STATES)))
        Dp = jnp.ones((D_IN,), dtype=jnp.float32)
        W_out = jax.random.normal(ks[5], (D_IN, D_MODEL), dtype=jnp.float32) * s
        return {'x': x, 'W_in': W_in, 'conv_w': conv_w, 'conv_b': conv_b, 'W_x': W_x, 'W_dt': W_dt, 'b_dt': b_dt, 'A_log': A_log, 'Dp': Dp, 'W_out': W_out}
    _L0_attn_all = _L0_attn_setup()
    _L0_attn_in = {k: v for k, v in _L0_attn_all.items() if k in ('W_in', 'conv_w', 'conv_b', 'W_x', 'W_dt', 'b_dt', 'A_log', 'Dp', 'W_out')}
    del _L0_attn_all

    def _L0_ffn_setup():
        import jax, jax.numpy as jnp
        import numpy as np
        G, E = (4, 8)
        KG, KE = (2, 2)
        D, M = (192, 768)
        SCALE = 0.02

        def _combine_weights(xf, Wg, bg, Wge, bge):
            N = xf.shape[0]
            glog = xf @ Wg + bg
            gtop, gidx = jax.lax.top_k(glog, KG)
            ggate = jax.nn.softmax(gtop, axis=-1)
            elog_all = jnp.einsum('nd,gde->nge', xf, Wge) + bge
            elog = jnp.take_along_axis(elog_all, gidx[:, :, None], axis=1)
            etop, eidx = jax.lax.top_k(elog, KE)
            egate = jax.nn.softmax(etop, axis=-1)
            w = ggate[:, :, None] * egate
            flat = gidx[:, :, None] * E + eidx
            comb = jnp.zeros((N, G * E), xf.dtype).at[jnp.arange(N)[:, None, None], flat].add(w)
            return comb
        key = jax.random.key(seed)
        ks = jax.random.split(key, 8)
        x = jax.random.normal(ks[0], (1, 128, D), jnp.float32)
        Wg = jax.random.normal(ks[1], (D, G), jnp.float32) * SCALE
        bg = jnp.zeros((G,), jnp.float32)
        Wge = jax.random.normal(ks[2], (G, D, E), jnp.float32) * SCALE
        bge = jnp.zeros((G, E), jnp.float32)
        W1 = jax.random.normal(ks[3], (G * E, D, M), jnp.float32) * SCALE
        b1 = jnp.zeros((G * E, M), jnp.float32)
        W2 = jax.random.normal(ks[4], (G * E, M, D), jnp.float32) * SCALE
        b2 = jnp.zeros((G * E, D), jnp.float32)
        return {'x': x, 'Wg': Wg, 'bg': bg, 'Wge': Wge, 'bge': bge, 'W1': W1, 'b1': b1, 'W2': W2, 'b2': b2}
    _L0_ffn_all = _L0_ffn_setup()
    _L0_ffn_in = {k: v for k, v in _L0_ffn_all.items() if k in ('Wg', 'bg', 'Wge', 'bge', 'W1', 'b1', 'W2', 'b2')}
    del _L0_ffn_all
    return {'x': x, 'L0_tok_gamma': _L0_tok_in['gamma'], 'L0_tok_beta': _L0_tok_in['beta'], 'L0_tok_W': _L0_tok_in['W'], 'L0_tok_b': _L0_tok_in['b'], 'L0_attn_W_in': _L0_attn_in['W_in'], 'L0_attn_conv_w': _L0_attn_in['conv_w'], 'L0_attn_conv_b': _L0_attn_in['conv_b'], 'L0_attn_W_x': _L0_attn_in['W_x'], 'L0_attn_W_dt': _L0_attn_in['W_dt'], 'L0_attn_b_dt': _L0_attn_in['b_dt'], 'L0_attn_A_log': _L0_attn_in['A_log'], 'L0_attn_Dp': _L0_attn_in['Dp'], 'L0_attn_W_out': _L0_attn_in['W_out'], 'L0_ffn_Wg': _L0_ffn_in['Wg'], 'L0_ffn_bg': _L0_ffn_in['bg'], 'L0_ffn_Wge': _L0_ffn_in['Wge'], 'L0_ffn_bge': _L0_ffn_in['bge'], 'L0_ffn_W1': _L0_ffn_in['W1'], 'L0_ffn_b1': _L0_ffn_in['b1'], 'L0_ffn_W2': _L0_ffn_in['W2'], 'L0_ffn_b2': _L0_ffn_in['b2']}

def reference(x, L0_tok_gamma, L0_tok_beta, L0_tok_W, L0_tok_b, L0_attn_W_in, L0_attn_conv_w, L0_attn_conv_b, L0_attn_W_x, L0_attn_W_dt, L0_attn_b_dt, L0_attn_A_log, L0_attn_Dp, L0_attn_W_out, L0_ffn_Wg, L0_ffn_bg, L0_ffn_Wge, L0_ffn_bge, L0_ffn_W1, L0_ffn_b1, L0_ffn_W2, L0_ffn_b2):
    import jax
    import jax.numpy as jnp

    def _L0_tok_ref(x, gamma, beta, W, b):
        import jax, jax.numpy as jnp
        import numpy as np
        PATCH = 16
        DIM = 192
        EPS = 0.001

        def _shifts(x):
            zw = jnp.zeros_like(x[:, :, :1, :])
            right = jnp.concatenate([zw, x[:, :, :-1, :]], axis=2)
            left = jnp.concatenate([x[:, :, 1:, :], zw], axis=2)
            zh = jnp.zeros_like(x[:, :1, :, :])
            down = jnp.concatenate([zh, x[:, :-1, :, :]], axis=1)
            up = jnp.concatenate([x[:, 1:, :, :], zh], axis=1)
            return [right, left, down, up]

        def _patchify(x, p):
            b, H, W, C = x.shape
            hh, ww = (H // p, W // p)
            x = x.reshape(b, hh, p, ww, p, C)
            x = x.transpose(0, 1, 3, 2, 4, 5)
            return x.reshape(b, hh * ww, p * p * C)
        x5 = jnp.concatenate([x] + _shifts(x), axis=-1)
        tokens = _patchify(x5, PATCH)
        mu = jnp.mean(tokens, axis=-1, keepdims=True)
        var = jnp.mean(jnp.square(tokens - mu), axis=-1, keepdims=True)
        ln = (tokens - mu) * jax.lax.rsqrt(var + EPS) * gamma + beta
        return jnp.einsum('bnf,fd->bnd', ln, W) + b

    def _L0_attn_ref(x, W_in, conv_w, conv_b, W_x, W_dt, b_dt, A_log, Dp, W_out):
        import jax, jax.numpy as jnp
        import numpy as np
        import math
        D_MODEL = 192
        N_STATES = 16
        D_IN = 2 * D_MODEL
        DT_RANK = math.ceil(D_MODEL / 16)
        KSIZE = 4
        BATCH, SEQ = (2, 256)

        def _mamba_forward(x, W_in, conv_w, conv_b, W_x, W_dt, b_dt, A_log, Dp, W_out):
            b, l, _ = x.shape
            xr = x @ W_in
            xi, res = jnp.split(xr, 2, axis=-1)
            xc = jnp.transpose(xi, (0, 2, 1))
            xc = jax.lax.conv_general_dilated(xc, conv_w, window_strides=(1,), padding=[(KSIZE - 1, 0)], dimension_numbers=('NCH', 'OIH', 'NCH'), feature_group_count=D_IN)
            xc = xc + conv_b[None, :, None]
            xi = jnp.transpose(xc, (0, 2, 1))
            xi = jax.nn.swish(xi)
            A = -jnp.exp(A_log)
            x_dbl = xi @ W_x
            delta, B, C = jnp.split(x_dbl, [DT_RANK, DT_RANK + N_STATES], axis=-1)
            delta = jax.nn.softplus(delta @ W_dt + b_dt)
            dA = jnp.einsum('bld,dn->bldn', delta, A)
            dB_u = jnp.einsum('bld,bld,bln->bldn', delta, xi, B)
            dA_shift = jnp.pad(dA[:, 1:], ((0, 0), (0, 1), (0, 0), (0, 0)))
            dA_cumsum = jnp.exp(jnp.flip(jnp.cumsum(jnp.flip(dA_shift, 1), axis=1), 1))
            x_ss = jnp.cumsum(dB_u * dA_cumsum, axis=1) / (dA_cumsum + 1e-12)
            y = jnp.einsum('bldn,bln->bld', x_ss, C) + xi * Dp
            return y * jax.nn.swish(res) @ W_out
        return _mamba_forward(x, W_in, conv_w, conv_b, W_x, W_dt, b_dt, A_log, Dp, W_out)

    def _L0_ffn_ref(x, Wg, bg, Wge, bge, W1, b1, W2, b2):
        import jax, jax.numpy as jnp
        import numpy as np
        G, E = (4, 8)
        KG, KE = (2, 2)
        D, M = (192, 768)
        SCALE = 0.02

        def _combine_weights(xf, Wg, bg, Wge, bge):
            N = xf.shape[0]
            glog = xf @ Wg + bg
            gtop, gidx = jax.lax.top_k(glog, KG)
            ggate = jax.nn.softmax(gtop, axis=-1)
            elog_all = jnp.einsum('nd,gde->nge', xf, Wge) + bge
            elog = jnp.take_along_axis(elog_all, gidx[:, :, None], axis=1)
            etop, eidx = jax.lax.top_k(elog, KE)
            egate = jax.nn.softmax(etop, axis=-1)
            w = ggate[:, :, None] * egate
            flat = gidx[:, :, None] * E + eidx
            comb = jnp.zeros((N, G * E), xf.dtype).at[jnp.arange(N)[:, None, None], flat].add(w)
            return comb
        shp = x.shape
        xf = x.reshape(-1, D)
        comb = _combine_weights(xf, Wg, bg, Wge, bge)
        h = jax.nn.gelu(jnp.einsum('nd,edm->nem', xf, W1) + b1, approximate=False)
        y = jnp.einsum('nem,emd->ned', h, W2) + b2
        out = jnp.einsum('ne,ned->nd', comb, y)
        return out.reshape(shp)
    h = _L0_tok_ref(x, L0_tok_gamma, L0_tok_beta, L0_tok_W, L0_tok_b)
    h = h + _L0_attn_ref(_layernorm(h, axis=-1), L0_attn_W_in, L0_attn_conv_w, L0_attn_conv_b, L0_attn_W_x, L0_attn_W_dt, L0_attn_b_dt, L0_attn_A_log, L0_attn_Dp, L0_attn_W_out)
    h = h + _L0_ffn_ref(_layernorm(h, axis=-1), L0_ffn_Wg, L0_ffn_bg, L0_ffn_Wge, L0_ffn_bge, L0_ffn_W1, L0_ffn_b1, L0_ffn_W2, L0_ffn_b2)
    return h

_drawn_inputs = setup_inputs


def setup_inputs(seed=0):
    import zlib

    import numpy as np

    out = dict(_drawn_inputs(seed))
    spreads = {'L0_tok_gamma': (1.0, 0.2),
     'L0_tok_beta': (0.0, 0.1),
     'L0_tok_b': (0.0, 2.0),
     'L0_attn_conv_b': (0.0, 0.8),
     'L0_attn_b_dt': (0.0, 0.8),
     'L0_attn_Dp': (1.0, 0.6),
     'L0_ffn_bg': (0.0, 2.0),
     'L0_ffn_bge': (0.0, 0.8),
     'L0_ffn_b1': (0.0, 2.0),
     'L0_ffn_b2': (0.0, 2.0)}
    factors = {'L0_attn_W_in': 8.0,
     'L0_attn_conv_w': 8.0,
     'L0_attn_W_x': 8.0,
     'L0_attn_W_dt': 8.0,
     'L0_attn_A_log': 8.0,
     'L0_attn_W_out': 8.0,
     'L0_ffn_Wg': 8.0,
     'L0_ffn_Wge': 8.0,
     'L0_ffn_W1': 8.0,
     'L0_ffn_W2': 8.0}
    for name, (base, spread) in spreads.items():
        noise = np.random.default_rng([zlib.crc32(name.encode()), seed]).standard_normal(out[name].shape)
        drawn = base * np.exp(spread * noise) if base else spread * noise
        out[name] = jnp.asarray(drawn.astype(out[name].dtype))
    for name, factor in factors.items():
        out[name] = (out[name] * factor).astype(out[name].dtype)
    return out
```

```python
from contextlib import ExitStack

import numpy as np

import concourse.bass as bass
from concourse import mybir

ALU = mybir.AluOpType
ACT = mybir.ActivationFunctionType
F32 = mybir.dt.float32
I32 = mybir.dt.int32
AX_X = mybir.AxisListType.X

BATCH, IMG, CH, PATCH = 16, 96, 3, 16
GRID = IMG // PATCH
L = GRID * GRID
N = BATCH * L
NSH = 5
F = PATCH * PATCH * NSH * CH
WIN = PATCH + 2
KC, NKC = 2 * WIN * CH, WIN // 2
D = 192
HALF_D = D // 2
DI = 2 * D
NJ = DI // 128
NST = 16
DTR = 12
KS = 4
TP = 96
NT = N // TP
HB = N // 2
G, E = 4, 8
NE = G * E
M = 768
NMC = M // 128
TOPK = 4
CAP = 128
MAX_OVER = (TOPK * N) // (CAP + 1)
NTILES = NE + MAX_OVER
LN_EPS = 1e-5
TOK_EPS = 1e-3
LOG_GUARD = float(-np.log(1e-12))

PC_CONVW = 0
PC_CONVB = PC_CONVW + NJ * KS
PC_BDT = PC_CONVB + NJ
PC_ALOG = PC_BDT + NJ
PC_D = PC_ALOG + NJ * NST
PC_WX = PC_D + NJ
XW = DTR + 2 * NST
PC_WOUT = PC_WX + NJ * XW
PC_B1 = PC_WOUT + NJ * D
PC_N = PC_B1 + NE * NMC
CC_ID = 0
CC_HALF = CC_ID + 128
CC_TRI = CC_HALF + 128
CC_LT8 = CC_TRI + TP
CC_LT4 = CC_LT8 + E * E
CC_BASE = CC_LT4 + G * G
CC_N = CC_BASE + NE + MAX_OVER
GC_G, GC_B, GC_CNT = 0, NKC * NSH, 2 * NKC * NSH
GC_N = GC_CNT + NKC

RING = 4
NG = 2
NGRP = NST // NG
STEPS = NGRP * NJ


def build_program(nc, x_t, w_sh, gb, consts, params, rows, w_in, w_dt, w_rt, w1, w2, b2, out, disp, disp_y, dbg=None):
    w1_v = w1.rearrange("e (c p) m -> e p c m", c=2)
    w2_v = w2.rearrange("e (c p) d -> e p c d", p=128)
    out_v = out.rearrange("(t p) d -> p t d", p=TP)

    with ExitStack() as ctx:
        def sb(name, shape, dt=F32):
            return ctx.enter_context(nc.sbuf_tensor(name, shape, dt))

        def sem(name):
            return ctx.enter_context(nc.semaphore(name))

        PS = ctx.enter_context(nc.psum_tensor("PS", [128, 8, 512], F32))
        PSF = PS[:].rearrange("p b c -> p (b c)")

        cst = sb("cst", [128, CC_N])
        par = sb("par", [128, PC_N])
        gbs = sb("gbs", [KC, GC_N])
        rws = sb("rws", [1, D + G + NE])
        win_s = sb("win_s", [HALF_D, 2, 2 * DI])
        wdt_s = sb("wdt_s", [DTR, DI])
        wrt_s = sb("wrt_s", [HALF_D, 2, G + NE])
        b2_s = sb("b2_s", [NE, D])
        ones = sb("ones", [128, 128])
        brow = sb("brow", [1, D])
        st = sb("st", [TP, 128])
        h1 = sb("h1", [TP, NT, D])
        h2 = sb("h2", [TP, NT, D])
        un = sb("un", [TP, NT, D])
        unT = sb("unT", [HALF_D, 2, N])
        ringw1 = sb("ringw1", [HALF_D, RING, 2, M])
        ringw2 = sb("ringw2", [128, RING, NMC, D])

        WORK = 27600
        work = sb("work", [128, WORK])
        at = [0]

        def region(shape, parts=128):
            n = int(np.prod(shape))
            v = work[0:parts, at[0]:at[0] + n]
            at[0] += n
            assert at[0] <= WORK, at[0]
            if len(shape) == 1:
                return v
            names = "abcd"[:len(shape)]
            return v.rearrange("p (" + " ".join(names) + ") -> p " + " ".join(names),
                               **{k: s for k, s in zip(names[1:], shape[1:])})

        x_s = region([NKC, N], KC)
        wsh_s = region([NKC, NSH, D], KC)
        xsq = region([NKC, N], KC)
        weff = region([NKC, D + 1], KC)
        gmu = region([NT, D], TP)
        bb_s = region([D], TP)
        at[0] = 0
        xpad = region([NJ, BATCH, L + KS - 1])
        xc = region([NJ, N])
        xi = region([NJ, N])
        sres = region([NJ, N])
        delta = region([NJ, N])
        dx = region([NJ, N])
        rsum = region([NJ * N + 1])
        mask = region([NJ * N])
        xdbl = region([N], XW)
        av = region([3, NJ * NST])
        guard = region([1])
        a_s = region([2, NG, BATCH, L])
        th_s = region([2, NG, N])
        t1_s = region([2, NG, N])
        bb_n = region([2, NG, N])
        cc_n = region([2, NG, N])
        sp_en = th_s.rearrange("p a b c -> p (a b c)")[:, 0:NJ * N].rearrange("p (j n) -> p j n", j=NJ)
        sp_ln = xc
        at[0] = 0
        zeros = None
        rl = region([NT, G + NE], TP)
        el = region([NT * G, E], TP)
        gt8 = region([NT * G, E, E], TP)
        eq8 = region([NT * G, E, E], TP)
        gt4 = region([NT, G, G], TP)
        eq4 = region([NT, G, G], TP)
        sm = region([1024], TP)
        msk = region([NT, NE], TP)
        comb = region([NT, NE], TP)
        slot = region([NT, NE], TP)
        incl = region([NT * NE], TP)
        rmask = region([NT * NE], TP)
        selk = region([NT * NE], TP)
        prod = region([NT * NE], TP)
        slotf = region([TOPK, NT], TP)
        combf = region([TOPK, NT], TP)
        combT = region([N], NE)
        ov = region([8, NE])
        ofs = region([MAX_OVER, NE])
        xg = region([RING, D])
        xgT = region([2, 2, CAP], HALF_D)
        hT = region([2, NMC, CAP])
        y_s = region([2, D])
        yg = region([NT, TOPK, D], TP)
        sloti = sb("sloti", [TP, TOPK * NT], I32)
        eidi = sb("eidi", [128, MAX_OVER + 1], I32)
        zero_s = sb("zero_s", [128, D])

        ident = cst[:, CC_ID:CC_ID + 128]
        half_ident = cst[:, CC_HALF:CC_HALF + 128]
        tri = cst[0:TP, CC_TRI:CC_TRI + TP]

        ld_gb, ld_cst, ld_par, ld_small, ld_rows = sem("ld_gb"), sem("ld_cst"), sem("ld_par"), sem("ld_small"), sem("ld_rows")
        ld_w = [sem(f"ld_w{g}") for g in range(3)]
        ld_x = [sem(f"ld_x{g}") for g in range(3)]
        ld_ring = [sem(f"ld_ring{r}") for r in range(RING)]
        ld_xg = [sem(f"ld_xg{r}") for r in range(RING)]
        disp_zero, disp_y_zero = sem("disp_zero"), sem("disp_y_zero")
        dve_own, act_own, pool_own = sem("dve_own"), sem("act_own"), sem("pool_own")
        ones_ready, weff_ready, cnt_ready, sq_ready = sem("ones_ready"), sem("weff_ready"), sem("cnt_ready"), sem("sq_ready")
        betaw_mm, brow_ready, tok_mm, g_mm, sq_mm = sem("betaw_mm"), sem("brow_ready"), sem("tok_mm"), sem("g_mm"), sem("sq_mm")
        var_ready, rstd_ready = sem("var_ready"), sem("rstd_ready")
        h_ready = sem("h_ready")
        un_ready, unT_mm, unT_ready = sem("un_ready"), sem("unT_mm"), sem("unT_ready")
        win_mm, win_read = sem("win_mm"), sem("win_read")
        conv_done, xi_ready = sem("conv_done"), sem("xi_ready")
        xdbl_mm, xdbl_ready, dl_mm, dl_read_act, dl_read_dve = (sem("xdbl_mm"), sem("xdbl_ready"), sem("dl_mm"), sem("dl_read_act"), sem("dl_read_dve"))
        en_ready, ln_ready, corr_ready, spq_ready = sem("en_ready"), sem("ln_ready"), sem("corr_ready"), sem("spq_ready")
        delta_ready, rsum_ready, dx_ready, aexp_ready, av_ready = (sem("delta_ready"), sem("rsum_ready"), sem("dx_ready"), sem("aexp_ready"), sem("av_ready"))
        azero_ready = sem("azero_ready")
        b_mm, c_mm, b_ready, c_ready = sem("b_mm"), sem("c_mm"), sem("b_ready"), sem("c_ready")
        a_ready, t1_ready, scan_done, wg_ready, p_ready, p_used = (sem("a_ready"), sem("t1_ready"), sem("scan_done"), sem("wg_ready"), sem("p_ready"), sem("p_used"))
        yd_done, y2_ready, wout_mm, h2_ready = sem("yd_done"), sem("y2_ready"), sem("wout_mm"), sem("h2_ready")
        rt_mm, rl_ready, ex_in, ex_out = sem("rt_mm"), sem("rl_ready"), sem("ex_in"), sem("ex_out")
        eq_ready, eqt_ready = sem("eq_ready"), sem("eqt_ready")
        msk_ready, cnt_mm, comb_ready, combT_mm, combT_ready, b2_mm, b2_read = (sem("msk_ready"), sem("cnt_mm"), sem("comb_ready"), sem("combT_mm"), sem("combT_ready"), sem("b2_mm"), sem("b2_read"))
        slot_ready, eid_ready, scattered = sem("slot_ready"), sem("eid_ready"), sem("scattered")
        xgT_mm, xgT_ready, h_mm, gelu_done, w2_done, y_ready = (sem("xgT_mm"), sem("xgT_ready"), sem("h_mm"), sem("gelu_done"), sem("w2_done"), sem("y_ready"))
        y_stored = [sem("y_stored0"), sem("y_stored1")]
        o_ld, o_xgT_mm, o_xgT, o_h_mm, o_gelu, o_w2, o_y, o_stored = [sem("o_" + n) for n in ("ld", "xgT_mm", "xgT", "h_mm", "gelu", "w2", "y", "stored")]
        o_yfree = sem("o_yfree")
        gathered = [sem(f"gathered{t}") for t in range(NT)]
        out_ready, out_stored = sem("out_ready"), sem("out_stored")

        def follower(engine, own):
            count = [0]

            def step(ins):
                count[0] += 1
                return ins.then_inc(own, 1)

            def settle():
                engine.wait_ge(own, count[0])

            return step, settle

        block = ctx.enter_context(nc.Block())

        @block.sync
        def _(sp):
            sp.dma_start(gbs[:], gb).then_inc(ld_gb, 16)
            for g in range(3):
                sp.dma_start(wsh_s[:, 3 * g:3 * g + 3], w_sh[:, 3 * g:3 * g + 3]).then_inc(ld_w[g], 16)
                sp.dma_start(x_s[:, 3 * g:3 * g + 3], x_t[:, 3 * g:3 * g + 3]).then_inc(ld_x[g], 16)
                if g == 0:
                    sp.dma_start(rws[:], rows).then_inc(ld_rows, 16)
                    sp.dma_start(cst[:], consts).then_inc(ld_cst, 16)
            sp.dma_start(par[:], params).then_inc(ld_par, 16)
            sp.dma_start(win_s[:], w_in.rearrange("(c p) n -> p c n", c=2)).then_inc(ld_small, 16)
            sp.dma_start(wdt_s[:], w_dt).then_inc(ld_small, 16)
            sp.dma_start(wrt_s[:], w_rt.rearrange("(c p) n -> p c n", c=2)).then_inc(ld_small, 16)
            sp.dma_start(b2_s[:], b2).then_inc(ld_small, 16)
            for r in range(RING):
                sp.dma_start(ringw1[:, r], w1_v[r]).then_inc(ld_ring[r], 16)
                sp.dma_start(ringw2[:, r], w2_v[r]).then_inc(ld_ring[r], 16)
            sp.wait_ge(ones_ready, 2)
            sp.dma_start(disp.rearrange("(q p) d -> p q d", p=CAP),
                         zero_s[:].unsqueeze(1).to_broadcast([128, NTILES, D])).then_inc(disp_zero, 16)
            sp.dma_start(disp_y[NE * CAP:, :].rearrange("(q p) d -> p q d", p=CAP),
                         zero_s[:].unsqueeze(1).to_broadcast([128, MAX_OVER, D])).then_inc(disp_y_zero, 16)

            sp.wait_ge(scattered, 16 * NT * TOPK)
            for r in range(RING):
                sp.dma_start(xg[:, r], disp[r * CAP:(r + 1) * CAP, :]).then_inc(ld_xg[r], 16)
            with sp.Fori(0, NE // RING - 1) as i:
                for r in range(RING):
                    e = i * RING + (RING + r)
                    sp.wait_ge(xgT_mm, i * RING + (r + 1))
                    sp.dma_start(xg[:, r], disp[bass.ds(e * CAP, CAP), :]).then_inc(ld_xg[r], 16)
                    sp.wait_ge(w2_done, i * RING + (r + 1))
                    sp.dma_start(ringw1[:, r], w1_v[bass.ds(e, 1)].rearrange("a p c m -> p (a c) m")).then_inc(ld_ring[r], 16)
                    sp.dma_start(ringw2[:, r], w2_v[bass.ds(e, 1)].rearrange("a p c d -> p (a c) d")).then_inc(ld_ring[r], 16)
            sp.wait_ge(eid_ready, 1)
            n_over = sp.value_load(eidi[0:1, MAX_OVER:MAX_OVER + 1], min_val=0, max_val=MAX_OVER)
            sp.wait_ge(w2_done, NE)
            with sp.Fori(0, MAX_OVER) as j:
                with sp.If(n_over > j):
                    e = sp.value_load(eidi[0:1, bass.ds(j, 1)], min_val=0, max_val=NE - 1)
                    sp.wait_ge(o_w2, j + 1)
                    sp.dma_start(xg[:, 0], disp[bass.ds(j * CAP + NE * CAP, CAP), :]).then_inc(o_ld, 16)
                    sp.dma_start(ringw1[:, 0], w1_v[bass.ds(e, 1)].rearrange("a p c m -> p (a c) m")).then_inc(o_ld, 16)
                    sp.dma_start(ringw2[:, 0], w2_v[bass.ds(e, 1)].rearrange("a p c d -> p (a c) d")).then_inc(o_ld, 16)
            for t in range(NT):
                sp.wait_ge(out_ready, t + 1)
                sp.dma_start(out_v[:, t], h1[:, t]).then_inc(out_stored, 16)
            if dbg is not None:
                sp.dma_start(dbg.rearrange("(t p) d -> p t d", p=TP), h2[:]).then_inc(out_stored, 16)
                sp.wait_ge(out_stored, 16)
            sp.wait_ge(out_stored, 16 * NT)

        @block.tensor
        def _(pe):
            def mm(o, a, b, start=True, stop=True, **k):
                return pe.matmul(o, a, b, start=start, stop=stop, **k)

            pe.wait_ge(ld_gb, 16)
            for c in range(NKC):
                if c % 3 == 0:
                    pe.wait_ge(ld_w[c // 3], 16)
                for s in range(NSH):
                    k = c * NSH + s
                    last = mm(PS[0:1, 7, 0:D], gbs[:, GC_B + k:GC_B + k + 1], wsh_s[:, c, s], k == 0, k == NKC * NSH - 1)
            last.then_inc(betaw_mm, 1)
            pe.wait_ge(cnt_ready, 1)
            for c in range(NKC):
                if c % 3 == 0:
                    pe.wait_ge(ld_x[c // 3], 16)
                pe.wait_ge(weff_ready, c + 1)
                for t in range(NT):
                    last = mm(PS[0:TP, t, 0:D + 1], x_s[:, c, t * TP:(t + 1) * TP], weff[:, c], c == 0, c == NKC - 1)
            last.then_inc(tok_mm, 1)
            pe.wait_ge(ones_ready, 1)
            for c in range(NKC):
                mm(PS[0:TP, 6, 0:D], ones[0:KC, 0:TP], weff[:, c, 0:D], c == 0, c == NKC - 1)
            pe.wait_ge(brow_ready, 1)
            mm(PS[0:TP, 6, D:2 * D], ones[0:1, 0:TP], brow[:]).then_inc(g_mm, 1)
            pe.wait_ge(sq_ready, 3)
            for t in range(NT):
                for c in range(NKC):
                    last = mm(PS[0:TP, 7, t:t + 1], xsq[:, c, t * TP:(t + 1) * TP], weff[:, c, D:D + 1], c == 0, c == NKC - 1)
            last.then_inc(sq_mm, 1)

            def transposes(done):
                pe.wait_ge(ld_cst, 16)
                for t in range(NT):
                    pe.wait_ge(un_ready, done * NT + t + 1)
                    for c in range(2):
                        last = pe.transpose(PS[0:HALF_D, 2 * c + t // 3, (t % 3) * TP:(t % 3 + 1) * TP],
                                            un[:, t, c * HALF_D:(c + 1) * HALF_D], ident[0:TP, 0:TP])
                last.then_inc(unT_mm, 1)

            pe.wait_ge(h_ready, NT)
            transposes(0)
            pe.wait_ge(ld_small, 16 * 4)
            pe.wait_ge(ld_rows, 16)
            pe.wait_ge(unT_ready, 2)
            for j in range(2 * NJ):
                if j >= 4:
                    pe.wait_ge(win_read, j - 3)
                for hf in range(2):
                    for c in range(2):
                        last = mm(PS[:, (4 + 2 * j + hf) % 8, 0:HB], win_s[:, c, j * 128:(j + 1) * 128],
                                  unT[:, c, hf * HB:(hf + 1) * HB], c == 0, c == 1)
                last.then_inc(win_mm, 1)
            pe.wait_ge(ld_par, 16)
            pe.wait_ge(win_read, 3)
            for j in range(NJ):
                pe.wait_ge(xi_ready, j + 1)
                for hf in range(2):
                    last = mm(PS[0:XW, hf, 0:HB], par[:, PC_WX + j * XW:PC_WX + (j + 1) * XW],
                              xi[:, j, hf * HB:(hf + 1) * HB], j == 0, j == NJ - 1, skip_group_check=True)
            last.then_inc(xdbl_mm, 1)
            pe.wait_ge(xdbl_ready, 1)
            pe.wait_ge(win_read, 6)
            for j in range(NJ):
                for hf in range(2):
                    last = mm(PS[:, 2 + 2 * j + hf, 0:HB], wdt_s[:, j * 128:(j + 1) * 128], xdbl[0:DTR, hf * HB:(hf + 1) * HB])
                last.then_inc(dl_mm, 1)

            def broadcast(n):
                for bank, row, read, done in ((0, DTR + n, b_ready, b_mm), (2, DTR + NST + n, c_ready, c_mm)):
                    if n:
                        pe.wait_ge(read, n)
                    elif bank == 2:
                        pe.wait_ge(dl_read_act, 1)
                        pe.wait_ge(dl_read_dve, 1)
                    for hf in range(2):
                        last = mm(PS[:, bank + hf, 0:HB], ident[0:XW, row:row + 1].to_broadcast([XW, 128]),
                                  xdbl[:, hf * HB:(hf + 1) * HB])
                    last.then_inc(done, 1)

            for n in range(NG):
                broadcast(n)
            pe.wait_ge(dl_read_act, NJ)
            pe.wait_ge(dl_read_dve, NJ)
            for s in range(STEPS):
                g, j, k = s // NJ, s % NJ, s % 2
                if j < NG and g + 1 < NGRP:
                    broadcast(NG * (g + 1) + j)
                pe.wait_ge(p_ready, s + 1)
                for n in range(NG):
                    lo = j * N
                    while lo < (j + 1) * N:
                        hi = min((j + 1) * N, (lo // 512 + 1) * 512)
                        first = s < NJ and n == 0 and lo % 512 == 0
                        last = mm(PSF[:, 4 * 512 + lo:4 * 512 + hi], half_ident, t1_s[:, k, n, lo - j * N:hi - j * N],
                                  first, s >= STEPS - NJ and n == NG - 1, skip_group_check=True)
                        lo = hi
                last.then_inc(p_used, 1)
            pe.wait_ge(y2_ready, NJ)
            for t in range(NT):
                for j in range(NJ):
                    last = mm(PS[0:TP, t, 0:D], dx[:, j, t * TP:(t + 1) * TP],
                              par[:, PC_WOUT + j * D:PC_WOUT + (j + 1) * D], j == 0, j == NJ - 1)
                last.then_inc(wout_mm, 1)
            pe.wait_ge(h2_ready, NT)
            transposes(1)
            pe.wait_ge(unT_ready, 4)
            for t in range(NT):
                o = PS[0:TP, 4, t * (G + NE):(t + 1) * (G + NE)]
                for c in range(2):
                    mm(o, unT[:, c, t * TP:(t + 1) * TP], wrt_s[:, c], c == 0, False)
                last = mm(o, ones[0:1, 0:TP], rws[0:1, D:D + G + NE], False, True)
            last.then_inc(rt_mm, 1)
            pe.wait_ge(msk_ready, 1)
            for t in range(NT):
                o = PS[0:TP, 5, t * NE:(t + 1) * NE]
                for u in range(t):
                    mm(o, ones[0:TP, 0:TP], msk[:, u], u == 0, False)
                mm(o, tri, msk[:, t], t == 0, True)
            for t in range(NT):
                last = mm(PS[:, 6, 0:NE], ones[0:TP, :], msk[:, t], t == 0, t == NT - 1)
            last.then_inc(cnt_mm, 1)
            pe.wait_ge(comb_ready, 1)
            for t in range(NT):
                last = pe.transpose(PS[0:NE, t // 3, (t % 3) * TP:(t % 3 + 1) * TP], comb[:, t], ident[0:TP, 0:TP])
            last.then_inc(combT_mm, 1)
            pe.wait_ge(combT_ready, 1)
            for t in range(NT):
                last = mm(PS[0:TP, 2 + t // 2, (t % 2) * D:(t % 2 + 1) * D], combT[:, t * TP:(t + 1) * TP], b2_s[:])
            last.then_inc(b2_mm, 1)
            pe.wait_ge(b2_read, 1)

            def expert(i, r, first):
                e = i * RING + r
                pe.wait_ge(xgT_ready, e + 1)
                pe.wait_ge(ld_ring[r], i * 32 + 32)
                for m in range(NMC):
                    if not (first and r * NMC + m < 4):
                        pe.wait_ge(gelu_done, e * NMC + (m - 3))
                    for c in range(2):
                        last = mm(PS[:, (r * NMC + m) % 4, 0:CAP], ringw1[:, r, c, m * 128:(m + 1) * 128],
                                  xgT[:, r % 2, c], c == 0, c == 1)
                    last.then_inc(h_mm, 1)

            def next_tokens(i, r):
                pe.wait_ge(ld_xg[r], i * 16 + 16)
                for c in range(2):
                    last = pe.transpose(PS[0:HALF_D, 6 + r % 2, c * CAP:(c + 1) * CAP],
                                        xg[:, r, c * HALF_D:(c + 1) * HALF_D], ident)
                last.then_inc(xgT_mm, 1)

            def output(i, r, first):
                e = i * RING + r
                if not (first and r < 2):
                    pe.wait_ge(y_ready, e - 1)
                for m in range(NMC):
                    pe.wait_ge(gelu_done, e * NMC + (m + 1))
                    last = mm(PS[:, 4 + r % 2, 0:D], hT[:, r % 2, m], ringw2[:, r, m], m == 0, m == NMC - 1)
                last.then_inc(w2_done, 1)

            def experts(i, first=False, final=False):
                for r in range(RING):
                    expert(i, r, first)
                    if r + 1 < RING:
                        next_tokens(i, r + 1)
                    elif not final:
                        next_tokens(i + 1, 0)
                    output(i, r, first)

            next_tokens(0, 0)
            experts(0, first=True)
            with pe.Fori(1, NE // RING - 1) as i:
                experts(i)
            experts(NE // RING - 1, final=True)
            pe.wait_ge(eid_ready, 1)
            n_over = pe.value_load(eidi[0:1, MAX_OVER:MAX_OVER + 1], min_val=0, max_val=MAX_OVER)
            pe.wait_ge(gelu_done, NE * NMC)
            pe.wait_ge(y_ready, NE)
            pe.sem_inc(o_w2, 1)
            with pe.Fori(0, MAX_OVER) as j:
                with pe.If(n_over > j):
                    pe.wait_ge(o_ld, j * 48 + 48)
                    for c in range(2):
                        last = pe.transpose(PS[0:HALF_D, 6, c * CAP:(c + 1) * CAP], xg[:, 0, c * HALF_D:(c + 1) * HALF_D], ident)
                    last.then_inc(o_xgT_mm, 1)
                    pe.wait_ge(o_xgT, j + 1)
                    for m in range(NMC):
                        if m >= 4:
                            pe.wait_ge(o_gelu, j * NMC + (m - 3))
                        for c in range(2):
                            last = mm(PS[:, m % 4, 0:CAP], ringw1[:, 0, c, m * 128:(m + 1) * 128], xgT[:, 0, c], c == 0, c == 1)
                        last.then_inc(o_h_mm, 1)
                    for m in range(NMC):
                        pe.wait_ge(o_gelu, j * NMC + (m + 1))
                        last = mm(PS[:, 4, 0:D], hT[:, 0, m], ringw2[:, 0, m], m == 0, m == NMC - 1)
                    last.then_inc(o_w2, 1)

        @block.scalar
        def _(act):
            step, settle = follower(act, act_own)
            for g in range(3):
                act.wait_ge(ld_x[g], 16)
                act.activation(xsq[:, 3 * g:3 * g + 3], x_s[:, 3 * g:3 * g + 3], ACT.Square).then_inc(sq_ready, 1)
            act.wait_ge(unT_mm, 1)
            act.copy(unT[:, 0].rearrange("p (h n) -> p h n", h=2), PS[0:HALF_D, 0:2, 0:HB]).then_inc(unT_ready, 1)
            act.wait_ge(azero_ready, 1)
            for j in range(NJ):
                act.wait_ge(win_mm, j + 1)
                b0 = (4 + 2 * j) % 8
                act.copy(xpad[:, j, :, KS - 1:].rearrange("p (h b) l -> p h b l", h=2),
                         PS[:, b0:b0 + 2, 0:HB].rearrange("p h (b l) -> p h b l", l=L)).then_inc(win_read, 1)
            for j in range(NJ):
                act.wait_ge(win_mm, NJ + j + 1)
                b0 = (4 + 2 * (NJ + j)) % 8
                act.activation(sres[:, j].rearrange("p (h n) -> p h n", h=2), PS[:, b0:b0 + 2, 0:HB], ACT.Silu).then_inc(win_read, 1)
            for j in range(NJ):
                act.wait_ge(conv_done, j + 1)
                act.activation(xi[:, j], xc[:, j], ACT.Silu).then_inc(xi_ready, 1)
            act.wait_ge(ld_par, 16)
            act.activation(av[:, 0], par[:, PC_ALOG:PC_ALOG + NJ * NST], ACT.Exp).then_inc(aexp_ready, 1)
            for j in range(NJ):
                act.wait_ge(dl_mm, j + 1)
                act.activation(sp_en[:, j].rearrange("p (h n) -> p h n", h=2), PS[:, 2 + 2 * j:4 + 2 * j, 0:HB], ACT.Abs,
                               bias=par[:, PC_BDT + j:PC_BDT + j + 1]).then_inc(dl_read_act, 1)
            for j in range(NJ):
                act.wait_ge(dl_read_act, j + 1)
                act.activation(sp_en[:, j], sp_en[:, j], ACT.Exp, scale=-1.0).then_inc(en_ready, 1)
            for j in range(NJ):
                act.wait_ge(en_ready, j + 1)
                act.activation(sp_ln[:, j], sp_en[:, j], ACT.Ln, bias=1.0).then_inc(ln_ready, 1)
            act.wait_ge(delta_ready, NJ)
            act.wait_ge(rsum_ready, 1)
            act.wait_ge(av_ready, 2)

            def copy_c(n):
                act.wait_ge(c_mm, n + 1)
                if n % NG == 0 and n >= 2 * NG:
                    act.wait_ge(p_ready, NJ * (n // NG - 1))
                act.copy(cc_n[:, (n // NG) % 2, n % NG].rearrange("p (h n) -> p h n", h=2), PS[:, 2:4, 0:HB]).then_inc(c_ready, 1)

            for n in range(NG):
                copy_c(n)
            s_view = rsum[:, 1:NJ * N + 1].rearrange("p (j n) -> p j n", j=NJ)
            d_view = delta.rearrange("p j (b l) -> p j b l", l=L)
            for s in range(STEPS):
                g, j, k = s // NJ, s % NJ, s % 2
                if s >= 2:
                    act.wait_ge(wg_ready, s - 1)
                for n in range(NG):
                    q = j * NST + g * NG + n
                    act.activation(a_s[:, k, n, :, 1:L], d_view[:, j, :, 1:L], ACT.Exp, scale=av[:, 1, q:q + 1])
                    last = act.activation(th_s[:, k, n], s_view[:, j], ACT.Tanh, scale=av[:, 2, q:q + 1], bias=guard[:])
                last.then_inc(a_ready, 1)
                if j < NG and g + 1 < NGRP:
                    copy_c(NG * (g + 1) + j)
            act.wait_ge(unT_mm, 2)
            act.copy(unT[:, 0].rearrange("p (h n) -> p h n", h=2), PS[0:HALF_D, 0:2, 0:HB]).then_inc(unT_ready, 1)
            act.wait_ge(ex_in, 1)
            act.activation(sm[:, 0:NT * (G + NE)], sm[:, 0:NT * (G + NE)], ACT.Exp).then_inc(ex_out, 1)

            def gelus(i, first):
                for r in range(RING):
                    e = i * RING + r
                    if not (first and r < 2):
                        act.wait_ge(w2_done, e - 1)
                    for m in range(NMC):
                        act.wait_ge(h_mm, e * NMC + (m + 1))
                        col = e * NMC + (PC_B1 + m)
                        act.activation(hT[:, r % 2, m], PS[:, (r * NMC + m) % 4, 0:CAP], ACT.Gelu,
                                       bias=par[:, bass.ds(col, 1)]).then_inc(gelu_done, 1)

            gelus(0, True)
            with act.Fori(1, NE // RING) as i:
                gelus(i, False)
            act.wait_ge(eid_ready, 1)
            n_over = act.value_load(eidi[0:1, MAX_OVER:MAX_OVER + 1], min_val=0, max_val=MAX_OVER)
            with act.Fori(0, MAX_OVER) as j:
                with act.If(n_over > j):
                    e = act.value_load(eidi[0:1, bass.ds(j, 1)], min_val=0, max_val=NE - 1)
                    act.wait_ge(o_w2, j + 1)
                    for m in range(NMC):
                        act.wait_ge(o_h_mm, j * NMC + (m + 1))
                        col = e * NMC + (PC_B1 + m)
                        act.activation(hT[:, 0, m], PS[:, m % 4, 0:CAP], ACT.Gelu,
                                       bias=par[:, bass.ds(col, 1)]).then_inc(o_gelu, 1)

        @block.gpsimd
        def _(pool):
            step, settle = follower(pool, pool_own)
            pool.memset(ones[:], 1.0).then_inc(ones_ready, 1)
            pool.memset(zero_s[:], 0.0).then_inc(ones_ready, 1)
            step(pool.memset(st[:, 64:64 + NT], -0.5))
            settle()

            def inverse_root(k):
                pool.wait_ge(var_ready, k + 1)
                pool.tensor_tensor(st[:, 32:32 + NT], st[:, 24:24 + NT], st[:, 64:64 + NT], ALU.pow).then_inc(rstd_ready, 1)

            inverse_root(0)
            inverse_root(1)
            pool.wait_ge(tok_mm, 1)
            pool.wait_ge(g_mm, 1)
            pool.wait_ge(sq_mm, 1)
            pool.wait_ge(h_ready, NT)
            pool.memset(xpad[:, :, :, 0:KS - 1], 0.0).then_inc(azero_ready, 1)
            pool.memset(a_s[:, :, :, :, 0:1].rearrange("p a b c d -> p (a b) c d"), 0.0).then_inc(azero_ready, 1)
            pool.memset(guard[:], 0.5 * LOG_GUARD).then_inc(azero_ready, 1)
            step(pool.memset(mask[:], 1.0))
            settle()
            pool.memset(mask[:].rearrange("p (b l) -> p b l", l=L)[:, :, L - 1:L], 0.0).then_inc(azero_ready, 1)
            for j in range(NJ):
                pool.wait_ge(corr_ready, j + 1)
                step(pool.tensor_tensor(dx[:, j], sp_en[:, j], dx[:, j], ALU.subtract))
                settle()
                pool.wait_ge(dl_read_dve, j + 1)
                pool.tensor_tensor(dx[:, j], dx[:, j], delta[:, j], ALU.add).then_inc(spq_ready, 1)
            for j in range(NJ):
                pool.wait_ge(delta_ready, j + 1)
                pool.tensor_tensor(dx[:, j], delta[:, j], xi[:, j], ALU.mult).then_inc(dx_ready, 1)

            def inputs(s):
                g, j, k = s // NJ, s % NJ, s % 2
                pool.wait_ge(b_ready, NG * (g + 1))
                if s >= 2:
                    pool.wait_ge(p_used, s - 1)
                pool.tensor_tensor(t1_s[:, k], dx[:, j].unsqueeze(1).to_broadcast([128, NG, N]), bb_n[:, g % 2], ALU.mult).then_inc(t1_ready, 1)

            pool.wait_ge(dx_ready, NJ)
            inputs(0)
            for s in range(STEPS):
                g, k = s // NJ, s % 2
                if s + 1 < STEPS:
                    inputs(s + 1)
                pool.wait_ge(wg_ready, s + 1)
                pool.wait_ge(c_ready, NG * (g + 1))
                pool.tensor_tensor(t1_s[:, k], t1_s[:, k], cc_n[:, g % 2], ALU.mult).then_inc(p_ready, 1)
            for j in range(NJ):
                pool.wait_ge(yd_done, j + 1)
                pool.tensor_tensor(dx[:, j], xc[:, j], sres[:, j], ALU.mult).then_inc(y2_ready, 1)
            inverse_root(2)
            pool.wait_ge(eq_ready, 1)
            pool.wait_ge(ld_cst, 16)
            pool.tensor_tensor(eq4, eq4, cst[0:TP, CC_LT4:CC_LT4 + G * G].rearrange("p (i j) -> p i j", i=G).unsqueeze(1)
                               .to_broadcast([TP, NT, G, G]), ALU.mult).then_inc(eqt_ready, 1)
            pool.wait_ge(eq_ready, 2)
            pool.tensor_tensor(eq8, eq8, cst[0:TP, CC_LT8:CC_LT8 + E * E].rearrange("p (i j) -> p i j", i=E).unsqueeze(1)
                               .to_broadcast([TP, NT * G, E, E]), ALU.mult).then_inc(eqt_ready, 1)
            pool.wait_ge(disp_zero, 16)
            for k in range(TOPK):
                pool.wait_ge(slot_ready, k + 1)
                for t in range(NT):
                    pool.indirect_dma_start(disp[:], bass.IndirectOffsetOnAxis(ap=sloti[:, k * NT + t:k * NT + t + 1], axis=0),
                                            un[:, t], None).then_inc(scattered, 16)

            def stores(i):
                for r in range(RING):
                    e = i * RING + r
                    pool.wait_ge(y_ready, e + 1)
                    pool.dma_start(disp_y[bass.ds(e * CAP, CAP), :], y_s[:, r % 2]).then_inc(y_stored[r % 2], 16)

            with pool.Fori(0, NE // RING) as i:
                stores(i)
            pool.wait_ge(eid_ready, 1)
            n_over = pool.value_load(eidi[0:1, MAX_OVER:MAX_OVER + 1], min_val=0, max_val=MAX_OVER)
            for b in range(2):
                pool.wait_ge(y_stored[b], 8 * NE)
            pool.wait_ge(disp_y_zero, 16)
            pool.sem_inc(o_yfree, 1)
            with pool.Fori(0, MAX_OVER) as j:
                with pool.If(n_over > j):
                    pool.wait_ge(o_y, j + 1)
                    pool.dma_start(disp_y[bass.ds(j * CAP + NE * CAP, CAP), :], y_s[:, 0]).then_inc(o_stored, 16)
                    pool.wait_ge(o_stored, j * 16 + 16)
                    pool.sem_inc(o_yfree, 1)
            for t in range(NT):
                for k in range(TOPK):
                    pool.indirect_dma_start(yg[:, t, k], None, disp_y[:],
                                            bass.IndirectOffsetOnAxis(ap=sloti[:, k * NT + t:k * NT + t + 1], axis=0)).then_inc(gathered[t], 16)

        @block.vector
        def _(dve):
            step, settle = follower(dve, dve_own)
            mean, ex2, var, rstd, nm = (st[:, 0:NT], st[:, 8:8 + NT], st[:, 24:24 + NT], st[:, 32:32 + NT], st[:, 40:40 + NT])
            bst = st[:, 72:72 + 6]
            mv = st[:, 80:80 + 2 * NT]

            dve.wait_ge(ld_gb, 16)
            dve.tensor_copy(weff[:, :, D], gbs[:, GC_CNT:GC_CNT + NKC]).then_inc(cnt_ready, 1)
            for g in range(3):
                dve.wait_ge(ld_w[g], 16)
                for s in range(NSH):
                    settle()
                    for c in range(3 * g, 3 * g + 3):
                        k = GC_G + c * NSH + s
                        if s == 0:
                            step(dve.tensor_scalar(weff[:, c, 0:D], wsh_s[:, c, 0], gbs[:, k:k + 1], None, ALU.mult))
                        else:
                            ins = dve.scalar_tensor_tensor(out=weff[:, c, 0:D], in0=wsh_s[:, c, s], scalar=gbs[:, k:k + 1],
                                                           in1=weff[:, c, 0:D], op0=ALU.mult, op1=ALU.add)
                            if s == NSH - 1:
                                ins.then_inc(weff_ready, 1)
                            else:
                                step(ins)
            dve.wait_ge(betaw_mm, 1)
            dve.wait_ge(ld_rows, 16)
            dve.tensor_tensor(brow[:], PS[0:1, 7, 0:D], rws[0:1, 0:D], ALU.add).then_inc(brow_ready, 1)
            dve.wait_ge(g_mm, 1)
            step(dve.tensor_copy(bb_s, PS[0:TP, 6, D:2 * D]))
            dve.wait_ge(tok_mm, 1)
            step(dve.tensor_scalar(mean, PS[0:TP, 0:NT, D], 1.0 / F, None, ALU.mult))
            settle()
            step(dve.tensor_tensor(ex2, mean, mean, ALU.mult))
            dve.wait_ge(sq_mm, 1)
            settle()
            step(dve.scalar_tensor_tensor(out=var, in0=PS[0:TP, 7, 0:NT], scalar=1.0 / F, in1=ex2, op0=ALU.mult, op1=ALU.subtract))
            settle()
            dve.tensor_scalar(var, var, TOK_EPS, None, ALU.add).then_inc(var_ready, 1)
            dve.wait_ge(rstd_ready, 1)
            step(dve.scalar_tensor_tensor(out=nm, in0=mean, scalar=-1.0, in1=rstd, op0=ALU.mult, op1=ALU.mult))
            settle()
            for t in range(NT):
                step(dve.scalar_tensor_tensor(out=gmu[:, t], in0=PS[0:TP, 6, 0:D], scalar=nm[:, t:t + 1], in1=bb_s, op0=ALU.mult, op1=ALU.add))
            settle()
            for t in range(NT):
                dve.scalar_tensor_tensor(out=h1[:, t], in0=PS[0:TP, t, 0:D], scalar=rstd[:, t:t + 1], in1=gmu[:, t],
                                         op0=ALU.mult, op1=ALU.add).then_inc(h_ready, 1)

            def layernorm(src, ready, k):
                dve.wait_ge(ready, NT)
                bs6 = st[:, 92:92 + 36].rearrange("p (t s) -> p t s", s=6)
                for t in range(NT):
                    step(dve.bn_stats(bs6[:, t], src[:, t]))
                settle()
                for t in range(NT):
                    step(dve.bn_aggr(mv[:, 2 * t:2 * t + 2], bs6[:, t]))
                settle()
                mvv = mv.rearrange("p (t s) -> p t s", s=2)
                dve.tensor_scalar(var, mvv[:, :, 1], LN_EPS, None, ALU.add).then_inc(var_ready, 1)
                dve.wait_ge(rstd_ready, k + 1)
                for t in range(NT):
                    dve.tensor_scalar(un[:, t], src[:, t], mv[:, 2 * t:2 * t + 1], rstd[:, t:t + 1],
                                      ALU.subtract, ALU.mult).then_inc(un_ready, 1)
                dve.wait_ge(unT_mm, k)
                dve.tensor_copy(unT[:, 1].rearrange("p (h n) -> p h n", h=2), PS[0:HALF_D, 2:4, 0:HB]).then_inc(unT_ready, 1)

            layernorm(h1, h_ready, 1)
            dve.wait_ge(ld_par, 16)
            xcb = xc.rearrange("p j (b l) -> p j b l", l=L)
            for j in range(NJ):
                dve.wait_ge(win_read, j + 1)
                for k in range(KS):
                    w = par[:, PC_CONVW + j * KS + k:PC_CONVW + j * KS + k + 1]
                    src = xpad[:, j, :, k:k + L]
                    settle()
                    if k == 0:
                        step(dve.tensor_scalar(xcb[:, j], src, w, par[:, PC_CONVB + j:PC_CONVB + j + 1], ALU.mult, ALU.add))
                    else:
                        ins = dve.scalar_tensor_tensor(out=xcb[:, j], in0=src, scalar=w, in1=xcb[:, j], op0=ALU.mult, op1=ALU.add)
                        if k == KS - 1:
                            ins.then_inc(conv_done, 1)
                        else:
                            step(ins)
            dve.wait_ge(aexp_ready, 1)
            dve.tensor_scalar(av[:, 1], av[:, 0], -1.0, None, ALU.mult).then_inc(av_ready, 1)
            dve.tensor_scalar(av[:, 2], av[:, 0], -0.5, None, ALU.mult).then_inc(av_ready, 1)
            dve.wait_ge(xdbl_mm, 1)
            dve.tensor_copy(xdbl.rearrange("p (h n) -> p h n", h=2), PS[0:XW, 0:2, 0:HB]).then_inc(xdbl_ready, 1)
            for j in range(NJ):
                dve.wait_ge(dl_read_act, j + 1)
                dve.tensor_scalar(delta[:, j].rearrange("p (h n) -> p h n", h=2), PS[:, 2 + 2 * j:4 + 2 * j, 0:HB],
                                  par[:, PC_BDT + j:PC_BDT + j + 1], 0.0, ALU.add, ALU.max).then_inc(dl_read_dve, 1)
            for j in range(NJ):
                dve.wait_ge(en_ready, j + 1)
                dve.tensor_scalar(dx[:, j], sp_en[:, j], 1.0, 1.0, ALU.add, ALU.subtract).then_inc(corr_ready, 1)
            for j in range(NJ):
                dve.wait_ge(ln_ready, j + 1)
                dve.wait_ge(spq_ready, j + 1)
                dve.tensor_tensor(delta[:, j], sp_ln[:, j], dx[:, j], ALU.add).then_inc(delta_ready, 1)

            def copy_b(n):
                dve.wait_ge(b_mm, n + 1)
                if n % NG == 0 and n >= 2 * NG:
                    dve.wait_ge(t1_ready, NJ * (n // NG - 1))
                dve.tensor_copy(bb_n[:, (n // NG) % 2, n % NG].rearrange("p (h n) -> p h n", h=2), PS[:, 0:2, 0:HB]).then_inc(b_ready, 1)

            for n in range(NG):
                copy_b(n)
            dve.wait_ge(azero_ready, 4)
            dve.wait_ge(delta_ready, NJ)
            step(dve.tensor_tensor_scan(rsum[:, 0:NJ * N][:, ::-1], mask[:, ::-1], delta.rearrange("p j n -> p (j n)")[:, ::-1],
                                        0.0, ALU.mult, ALU.add))
            settle()
            dve.memset(rsum[:, L:NJ * N + 1:L], 0.0).then_inc(rsum_ready, 1)
            for s in range(STEPS + 1):
                k = s % 2
                if s < STEPS:
                    dve.wait_ge(a_ready, s + 1)
                    dve.wait_ge(t1_ready, s + 1)
                    dve.tensor_tensor_scan(t1_s[:, k].rearrange("p n l -> p (n l)"), a_s[:, k].rearrange("p n b l -> p (n b l)"),
                                           t1_s[:, k].rearrange("p n l -> p (n l)"), 0.0, ALU.mult, ALU.add).then_inc(scan_done, 1)
                if s >= 1:
                    o = 1 - k
                    dve.wait_ge(scan_done, s)
                    dve.scalar_tensor_tensor(out=t1_s[:, o], in0=th_s[:, o], scalar=1.0, in1=t1_s[:, o],
                                             op0=ALU.add, op1=ALU.mult).then_inc(wg_ready, 1)
                if s % NJ < NG and s // NJ + 1 < NGRP and s < STEPS:
                    copy_b(NG * (s // NJ + 1) + s % NJ)
            dve.wait_ge(p_used, STEPS)
            for j in range(NJ):
                dve.scalar_tensor_tensor(out=xc[:, j], in0=xi[:, j], scalar=par[:, PC_D + j:PC_D + j + 1],
                                         in1=PSF[:, 4 * 512 + j * N:4 * 512 + (j + 1) * N], op0=ALU.mult, op1=ALU.add).then_inc(yd_done, 1)
            for t in range(NT):
                dve.wait_ge(wout_mm, t + 1)
                dve.tensor_tensor(h2[:, t], PS[0:TP, t, 0:D], h1[:, t], ALU.add).then_inc(h2_ready, 1)
            layernorm(h2, h2_ready, 2)

            dve.wait_ge(rt_mm, 1)
            lg = PS[0:TP, 4, 0:NT * (G + NE)].rearrange("p (t c) -> p t c", t=NT)
            step(dve.tensor_copy(rl, lg))
            settle()
            step(dve.tensor_copy(el.rearrange("p (t g) e -> p t g e", t=NT), rl[:, :, G:].rearrange("p t (g e) -> p t g e", g=G)))
            gl = rl[:, :, 0:G]
            dve.tensor_tensor(eq4, gl.unsqueeze(2).to_broadcast([TP, NT, G, G]), gl.unsqueeze(3).to_broadcast([TP, NT, G, G]),
                              ALU.is_equal).then_inc(eq_ready, 1)
            settle()
            dve.tensor_tensor(eq8, el.unsqueeze(2).to_broadcast([TP, NT * G, E, E]), el.unsqueeze(3).to_broadcast([TP, NT * G, E, E]),
                              ALU.is_equal).then_inc(eq_ready, 1)
            step(dve.tensor_tensor(gt4, gl.unsqueeze(2).to_broadcast([TP, NT, G, G]), gl.unsqueeze(3).to_broadcast([TP, NT, G, G]), ALU.is_gt))
            step(dve.tensor_tensor(gt8, el.unsqueeze(2).to_broadcast([TP, NT * G, E, E]), el.unsqueeze(3).to_broadcast([TP, NT * G, E, E]), ALU.is_gt))
            exg, exe = sm[:, 0:NT * G], sm[:, NT * G:NT * (G + NE)]
            mxg, mxe = sm[:, 256:256 + NT], sm[:, 264:264 + NT * G]
            step(dve.tensor_reduce(mxg, gl, AX_X, ALU.max))
            step(dve.tensor_reduce(mxe, el, AX_X, ALU.max))
            settle()
            exg3, exe3 = exg.rearrange("p (t g) -> p t g", g=G), exe.rearrange("p (q e) -> p q e", e=E)
            step(dve.tensor_tensor(exg3, gl, mxg.unsqueeze(2).to_broadcast([TP, NT, G]), ALU.subtract))
            dve.tensor_tensor(exe3, el, mxe.unsqueeze(2).to_broadcast([TP, NT * G, E]), ALU.subtract).then_inc(ex_in, 1)
            settle()
            dve.wait_ge(eqt_ready, 2)
            step(dve.tensor_tensor(gt4, gt4, eq4, ALU.add))
            step(dve.tensor_tensor(gt8, gt8, eq8, ALU.add))
            settle()
            rkg, rke = sm[:, 296:296 + NT * G], sm[:, 320:320 + NT * NE]
            step(dve.tensor_reduce(rkg.rearrange("p (t g) -> p t g", g=G), gt4, AX_X, ALU.add))
            step(dve.tensor_reduce(rke.rearrange("p (q e) -> p q e", e=E), gt8, AX_X, ALU.add))
            settle()
            step(dve.tensor_scalar(sm[:, 296:320 + NT * NE], sm[:, 296:320 + NT * NE], 1.5, None, ALU.is_lt))
            settle()
            mskq = msk.rearrange("p t (g e) -> p (t g) e", g=G)
            rke3 = rke.rearrange("p (q e) -> p q e", e=E)
            dve.tensor_tensor(mskq, rke3, rkg.unsqueeze(2).to_broadcast([TP, NT * G, E]), ALU.mult).then_inc(msk_ready, 1)
            dve.wait_ge(ex_out, 1)
            step(dve.tensor_tensor(exg, exg, rkg, ALU.mult))
            step(dve.tensor_tensor(exe, exe, rke, ALU.mult))
            settle()
            smg, sme = sm[:, 520:520 + NT], sm[:, 528:528 + NT * G]
            step(dve.tensor_reduce(smg, exg3, AX_X, ALU.add))
            step(dve.tensor_reduce(sme, exe3, AX_X, ALU.add))
            settle()
            step(dve.reciprocal(smg, smg))
            step(dve.reciprocal(sme, sme))
            settle()
            sme3 = sme.rearrange("p (t g) -> p t g", g=G)
            step(dve.tensor_tensor(exg3, exg3, smg.unsqueeze(2).to_broadcast([TP, NT, G]), ALU.mult))
            settle()
            step(dve.tensor_tensor(sme3, sme3, exg3, ALU.mult))
            settle()
            combq = comb.rearrange("p t (g e) -> p (t g) e", g=G)
            dve.tensor_tensor(combq, exe3, sme.unsqueeze(2).to_broadcast([TP, NT * G, E]), ALU.mult).then_inc(comb_ready, 1)
            step(dve.memset(rmask, 1.0))
            settle()
            step(dve.memset(rmask[:, 0:NT * NE:NE], 0.0))
            dve.wait_ge(msk_ready, 1)
            settle()
            mskf = msk.rearrange("p t e -> p (t e)")
            step(dve.tensor_tensor_scan(incl, rmask, mskf, 0.0, ALU.mult, ALU.add))
            dve.wait_ge(cnt_mm, 1)
            cnt = PS[:, 6, 0:NE]
            step(dve.tensor_scalar(ov[:, 0], cnt, float(CAP), None, ALU.is_gt))
            for q in range(2, (N + CAP - 1) // CAP):
                settle()
                step(dve.scalar_tensor_tensor(out=ov[:, 0], in0=cnt, scalar=float(q * CAP), in1=ov[:, 0], op0=ALU.is_gt, op1=ALU.add))
            step(dve.memset(ov[:, 1], 1.0))
            settle()
            step(dve.tensor_tensor_scan(ov[:, 2], ov[:, 1], ov[:, 0], 0.0, ALU.mult, ALU.add))
            settle()
            step(dve.tensor_tensor(ov[:, 3], ov[:, 2], ov[:, 0], ALU.subtract))
            settle()
            step(dve.tensor_scalar(ov[:, 4], ov[:, 3], float(CAP), float((NE - 1) * CAP), ALU.mult, ALU.add))
            settle()
            base = cst[:, CC_BASE:CC_BASE + NE]
            step(dve.tensor_tensor(ov[:, 5], ov[:, 4], base, ALU.subtract))
            pos = PS[0:TP, 5, 0:NT * NE].rearrange("p (t e) -> p t e", t=NT)
            sl3 = selk.rearrange("p (t e) -> p t e", t=NT)
            step(dve.tensor_scalar(sl3, pos, float(CAP) - 0.5, None, ALU.is_gt))
            step(dve.tensor_tensor(slot, pos, base[0:TP].unsqueeze(1).to_broadcast([TP, NT, NE]), ALU.add))
            settle()
            step(dve.tensor_tensor(sl3, sl3, ov[0:TP, 5].unsqueeze(1).to_broadcast([TP, NT, NE]), ALU.mult))
            settle()
            step(dve.tensor_tensor(slot, slot, sl3, ALU.add))
            step(dve.tensor_tensor(ofs, ov[:, 2].unsqueeze(1).to_broadcast([128, MAX_OVER, NE]),
                                   cst[:, CC_BASE + NE:CC_N].unsqueeze(2).to_broadcast([128, MAX_OVER, NE]), ALU.is_le))
            settle()
            step(dve.tensor_reduce(ov[:, 6, 0:MAX_OVER], ofs, AX_X, ALU.add))
            step(dve.tensor_copy(ov[:, 6, MAX_OVER:MAX_OVER + 1], ov[:, 2, NE - 1:NE]))
            settle()
            step(dve.tensor_scalar(ov[:, 6, 0:MAX_OVER], ov[:, 6, 0:MAX_OVER], float(NE - 1), None, ALU.min))
            settle()
            dve.tensor_copy(eidi[:], ov[:, 6, 0:MAX_OVER + 1]).then_inc(eid_ready, 1)
            slotq = slot.rearrange("p t e -> p (t e)")
            combf_ = comb.rearrange("p t e -> p (t e)")
            dve.wait_ge(comb_ready, 1)
            for k in range(TOPK):
                settle()
                step(dve.scalar_tensor_tensor(out=selk, in0=incl, scalar=float(k + 1), in1=mskf, op0=ALU.is_equal, op1=ALU.mult))
                settle()
                step(dve.tensor_tensor(prod, selk, slotq, ALU.mult))
                settle()
                step(dve.tensor_reduce(slotf[:, k], prod.rearrange("p (t e) -> p t e", t=NT), AX_X, ALU.add))
                settle()
                dve.tensor_copy(sloti[:, k * NT:(k + 1) * NT], slotf[:, k]).then_inc(slot_ready, 1)
                step(dve.tensor_tensor(selk, selk, combf_, ALU.mult))
                settle()
                step(dve.tensor_reduce(combf[:, k], selk.rearrange("p (t e) -> p t e", t=NT), AX_X, ALU.add))
            dve.wait_ge(combT_mm, 1)
            dve.tensor_copy(combT.rearrange("p (h n) -> p h n", h=2), PS[0:NE, 0:2, 0:HB]).then_inc(combT_ready, 1)
            dve.wait_ge(b2_mm, 1)
            dve.tensor_tensor(h1[:].rearrange("p (a b) d -> p a b d", b=2), PS[0:TP, 2:5, 0:2 * D].rearrange("p a (b d) -> p a b d", b=2),
                              h2[:].rearrange("p (a b) d -> p a b d", b=2), ALU.add).then_inc(b2_read, 1)

            def token_copy(i, r, first):
                e = i * RING + r
                dve.wait_ge(xgT_mm, e + 1)
                if not (first and r < 2):
                    dve.wait_ge(h_mm, (e - 1) * NMC)
                dve.tensor_copy(xgT[:, r % 2], PS[0:HALF_D, 6 + r % 2, 0:2 * CAP].rearrange("p (c n) -> p c n", c=2)).then_inc(xgT_ready, 1)

            def output_copy(i, r, first):
                e = i * RING + r
                dve.wait_ge(w2_done, e + 1)
                if not (first and r < 2):
                    dve.wait_ge(y_stored[r % 2], i * (RING * 8) + (r // 2) * 16)
                dve.tensor_copy(y_s[:, r % 2], PS[:, 4 + r % 2, 0:D]).then_inc(y_ready, 1)

            def copies(i, first=False, final=False):
                for r in range(RING):
                    if r + 1 < RING:
                        token_copy(i, r + 1, first)
                    elif not final:
                        token_copy(i + 1, 0, False)
                    output_copy(i, r, first)

            token_copy(0, 0, True)
            copies(0, first=True)
            with dve.Fori(1, NE // RING - 1) as i:
                copies(i)
            copies(NE // RING - 1, final=True)
            n_over = dve.value_load(eidi[0:1, MAX_OVER:MAX_OVER + 1], min_val=0, max_val=MAX_OVER)
            for b in range(2):
                dve.wait_ge(y_stored[b], 8 * NE)
            with dve.Fori(0, MAX_OVER) as j:
                with dve.If(n_over > j):
                    dve.wait_ge(o_xgT_mm, j + 1)
                    dve.tensor_copy(xgT[:, 0], PS[0:HALF_D, 6, 0:2 * CAP].rearrange("p (c n) -> p c n", c=2)).then_inc(o_xgT, 1)
                    dve.wait_ge(o_yfree, j + 1)
                    dve.wait_ge(o_w2, j + 2)
                    dve.tensor_copy(y_s[:, 0], PS[:, 4, 0:D]).then_inc(o_y, 1)
            settle()
            dve.wait_ge(b2_read, 1)
            for t in range(NT):
                dve.wait_ge(gathered[t], 16 * TOPK)
                for k in range(TOPK):
                    settle()
                    ins = dve.scalar_tensor_tensor(out=h1[:, t], in0=yg[:, t, k], scalar=combf[:, k, t:t + 1], in1=h1[:, t],
                                                   op0=ALU.mult, op1=ALU.add)
                    if k == TOPK - 1:
                        ins.then_inc(out_ready, 1)
                    else:
                        step(ins)


DEBUG = False


def _layouts(x, gamma, beta, W):
    xp = np.pad(x, ((0, 0), (1, 1), (1, 1), (0, 0)))
    rows = (np.arange(GRID) * PATCH)[:, None] + np.arange(WIN)[None, :]
    p = xp[:, rows][:, :, :, rows]
    p = p.transpose(2, 4, 5, 0, 1, 3).reshape(NKC, KC, N).transpose(1, 0, 2)
    moves = ((0, 0), (0, 1), (0, -1), (1, 0), (-1, 0))

    def place(a):
        a = a.reshape(PATCH, PATCH, NSH, CH, -1)
        o = np.zeros((NSH, WIN, WIN, CH, a.shape[-1]), a.dtype)
        for s, (dy, dx) in enumerate(moves):
            o[s, 1 - dy:1 - dy + PATCH, 1 - dx:1 - dx + PATCH] = a[:, :, s]
        o = o.reshape(NSH, NKC, KC, -1)
        return o.transpose(2, 1, 0, 3)

    cnt = place(np.ones((F, 1), np.float32)).sum(2)[:, :, 0]
    gb = np.concatenate([place(gamma).reshape(KC, -1), place(beta).reshape(KC, -1), cnt], 1)
    return p, place(W), gb


def _constants():
    c = np.zeros((128, CC_N), np.float32)
    c[:, CC_ID:CC_ID + 128] = np.eye(128)
    c[:, CC_HALF:CC_HALF + 128] = 0.5 * np.eye(128)
    c[:TP, CC_TRI:CC_TRI + TP] = np.triu(np.ones((TP, TP)), 1)
    c[:, CC_LT8:CC_LT8 + E * E] = np.tril(np.ones((E, E)), -1).reshape(-1)
    c[:, CC_LT4:CC_LT4 + G * G] = np.tril(np.ones((G, G)), -1).reshape(-1)
    c[:, CC_BASE:CC_BASE + NE] = np.arange(NE) * CAP
    c[:, CC_BASE + NE:CC_N] = np.arange(MAX_OVER)
    return c


def kernel(**inputs):
    import numpy as _np
    import concourse.bacc as _bacc
    from concourse import mybir as _mybir
    from concourse.bass_utils import run_bass_kernel_spmd as _run

    v = {k: _np.asarray(a) for k, a in inputs.items()}

    def chunked(a):
        return a.reshape(NJ, 128, -1).transpose(1, 0, 2).reshape(128, -1)

    x_t, w_sh, gb = _layouts(v["x"], v["L0_tok_gamma"], v["L0_tok_beta"], v["L0_tok_W"])
    params = _np.concatenate(
        [chunked(v["L0_attn_" + k]) for k in ("conv_w", "conv_b", "b_dt", "A_log", "Dp", "W_x", "W_out")]
        + [v["L0_ffn_b1"].reshape(NE, NMC, 128).transpose(2, 0, 1).reshape(128, -1)], 1)
    rows = _np.concatenate([v["L0_tok_b"], v["L0_ffn_bg"], v["L0_ffn_bge"].reshape(-1)])[None]
    w_rt = _np.concatenate([v["L0_ffn_Wg"], v["L0_ffn_Wge"].transpose(1, 0, 2).reshape(D, NE)], 1)
    given = {"x_t": x_t, "w_sh": w_sh, "gb": gb, "consts": _constants(), "params": params, "rows": rows,
             "w_in": v["L0_attn_W_in"], "w_dt": v["L0_attn_W_dt"], "w_rt": w_rt,
             "w1": v["L0_ffn_W1"], "w2": v["L0_ffn_W2"], "b2": v["L0_ffn_b2"]}
    nc = _bacc.Bacc("TRN2", target_bir_lowering=False, num_devices=1)
    arrays, args = {}, []
    for name, a in given.items():
        a = _np.ascontiguousarray(a)
        arrays[f"in_{name}"] = a
        args.append(nc.dram_tensor(f"in_{name}", a.shape, _mybir.dt.from_np(a.dtype), kind="ExternalInput").ap())
    o = nc.dram_tensor("out_0", (N, D), _mybir.dt.float32, kind="ExternalOutput").ap()
    disp = nc.dram_tensor("disp", (NTILES * CAP, D), _mybir.dt.float32).ap()
    disp_y = nc.dram_tensor("disp_y", (NTILES * CAP, D), _mybir.dt.float32).ap()
    dbg = nc.dram_tensor("out_1", (N, D), _mybir.dt.float32, kind="ExternalOutput").ap() if DEBUG else None
    build_program(nc, *args, o, disp, disp_y, dbg)
    r = _run(nc, [arrays], core_ids=[0])
    return r.results[0]["out_0"].reshape(BATCH, L, D)
```

```python
from contextlib import ExitStack

import numpy as np

import concourse.bass as bass
from concourse import mybir

ALU = mybir.AluOpType
ACT = mybir.ActivationFunctionType
F32 = mybir.dt.float32
I32 = mybir.dt.int32
BF16 = mybir.dt.bfloat16
AX_X = mybir.AxisListType.X

BATCH, IMG, CH, PATCH = 16, 96, 3, 16
GRID = IMG // PATCH
L = GRID * GRID
N = BATCH * L
NSH = 5
F = PATCH * PATCH * NSH * CH
WIN = PATCH + 2
KC, NKC = 2 * WIN * CH, WIN // 2
D = 192
HALF_D = D // 2
DI = 2 * D
NJ = DI // 128
NST = 16
DTR = 12
KS = 4
TP = 96
NT = N // TP
HB = N // 2
G, E = 4, 8
NE = G * E
M = 768
NMC = M // 128
TOPK = 4
CAP = 128
MAX_OVER = (TOPK * N) // (CAP + 1)
LN_EPS = 1e-5
TOK_EPS = 1e-3
LOG_GUARD = float(-np.log(1e-12))

RING = 4
OVER = 6
OVER_ROUNDS = -(-MAX_OVER // OVER)
OVER_PAD = OVER * OVER_ROUNDS
NR = 6

PC_CONVW = 0
PC_CONVB = PC_CONVW + NJ * KS
PC_BDT = PC_CONVB + NJ
PC_ALOG = PC_BDT + NJ
PC_D = PC_ALOG + NJ * NST
PC_WX = PC_D + NJ
XW = DTR + 2 * NST
PC_WOUT = PC_WX + NJ * XW
PC_B1 = PC_WOUT + NJ * D
PC_N = PC_B1 + NE * NMC
CC_ID = 0
CC_HALF = CC_ID + 128
CC_TRI = CC_HALF + 128
CC_LT8 = CC_TRI + TP
CC_LT4 = CC_LT8 + E * E
CC_J = CC_LT4 + G * G
CC_JC = CC_J + OVER_PAD
CC_IOTA = CC_JC + OVER_PAD
CC_TOK = CC_IOTA + CAP
CC_SPARE = CC_TOK + 2 * NT
CC_N = CC_SPARE + 2
GC_G, GC_B, GC_CNT = 0, NKC * NSH, 2 * NKC * NSH
GC_N = GC_CNT + NKC

NG = 2
NGRP = NST // NG
STEPS = NGRP * NJ


def build_program(nc, x_t, w_sh, gb, consts, params, rows, w_in, w_dt, w_rt, w1, w2, b2, out, xn, bc, dbg=None):
    w1_v = w1.rearrange("e (c p) m -> e p c m", c=2)
    w2_v = w2.rearrange("e (c p) d -> e p c d", p=128)
    out_v = out[0:N].rearrange("(t p) d -> p t d", p=TP)

    with ExitStack() as ctx:
        def sb(name, shape, dt=F32):
            return ctx.enter_context(nc.sbuf_tensor(name, shape, dt))

        def sem(name):
            return ctx.enter_context(nc.semaphore(name))

        PS = ctx.enter_context(nc.psum_tensor("PS", [128, 8, 512], F32))
        PSF = PS[:].rearrange("p b c -> p (b c)")

        cst = sb("cst", [128, CC_N])
        par = sb("par", [128, PC_N])
        gbs = sb("gbs", [KC, GC_N])
        rws = sb("rws", [1, D + G + NE])
        win_s = sb("win_s", [HALF_D, 2, 2 * DI])
        wdt_s = sb("wdt_s", [DTR, DI])
        wrt_s = sb("wrt_s", [HALF_D, 2, G + NE])
        b2_s = sb("b2_s", [NE, D])
        ones = sb("ones", [128, 128])
        brow = sb("brow", [1, D])
        st = sb("st", [TP, 128])
        h1 = sb("h1", [TP, NT, D])
        h2 = sb("h2", [TP, NT, D])
        un = sb("un", [TP, NT, D])
        unT = sb("unT", [HALF_D, 2, N])
        ringw1 = sb("ringw1", [HALF_D, RING, 2, M])
        ringw2 = sb("ringw2", [128, RING, NMC, D])

        WORK = 29100
        work = sb("work", [128, WORK])
        at = [0]

        def region(shape, parts=128):
            n = int(np.prod(shape))
            v = work[0:parts, at[0]:at[0] + n]
            at[0] += n
            assert at[0] <= WORK, at[0]
            if len(shape) == 1:
                return v
            names = "abcd"[:len(shape)]
            return v.rearrange("p (" + " ".join(names) + ") -> p " + " ".join(names),
                               **{k: s for k, s in zip(names[1:], shape[1:])})

        x_s = region([NKC, N], KC)
        wsh_s = region([NKC, NSH, D], KC)
        xsq = region([NKC, N], KC)
        weff = region([NKC, D + 1], KC)
        gmu = region([NT, D], TP)
        bb_s = region([D], TP)
        at[0] = 0
        xpad = region([NJ, BATCH, L + KS - 1])
        xc = region([NJ, N])
        xi = region([NJ, N])
        sres = region([NJ, N])
        delta = region([NJ, N])
        dx = region([NJ, N])
        rsum = region([NJ * N + 1])
        xdbl = region([N], XW)
        av = region([3, NJ * NST])
        guard = region([1])
        a_s = region([2, NG, BATCH, L])
        th_s = region([2, NG, N])
        t1_s = region([2, NG, N])
        w_s = region([2, NG, N])
        p_s = region([2, NG, N])
        bb_n = region([2, NG, N])
        cc_n = region([2, NG, N])
        mask = p_s.rearrange("p a b c -> p (a b c)")[:, 0:NJ * N]
        sp_en = th_s.rearrange("p a b c -> p (a b c)")[:, 0:NJ * N].rearrange("p (j n) -> p j n", j=NJ)
        sp_ln = xc
        at[0] = 0
        zeros = None
        rl = region([NT, G + NE], TP)
        el = region([NT * G, E], TP)
        gt8 = region([NT * G, E, E], TP)
        eq8 = region([NT * G, E, E], TP)
        gt4 = region([NT, G, G], TP)
        eq4 = region([NT, G, G], TP)
        sm = region([1024], TP)
        msk = region([NT, NE], TP)
        comb = region([NT, NE], TP)
        posm = region([NT, NE], TP)
        oposm = region([NT, NE], TP)
        rest = region([NT, NE], TP)
        combT = region([N], NE)
        ov = region([7, NE])
        ofs = region([OVER_PAD, NE])
        tmp6 = region([OVER, NT], TP)
        calc = region([RING + OVER, 4])
        xg = region([RING, D])
        xgT = region([2, 2, CAP], HALF_D)
        hT = region([2, NMC, CAP])
        y_s = region([2, D])
        oh = region([RING, NT * CAP // 2], TP).rearrange("p r c -> p (r c)").bitcast(BF16).rearrange("p (r t c) -> p r t c", r=RING, t=NT)
        oxg = region([OVER, D])
        oxgT = region([OVER, 2, CAP], HALF_D)
        ooh = region([OVER, NT * CAP // 2], TP).rearrange("p r c -> p (r c)").bitcast(BF16).rearrange("p (r t c) -> p r t c", r=OVER, t=NT)
        facts = sb("facts", [TP, NT, NE, NR], BF16)
        idx = sb("idx", [128, RING + OVER], I32)
        wgt = sb("wgt", [128, RING + OVER])
        eidi = sb("eidi", [128, OVER_PAD + 1], I32)
        zero_s = sb("zero_s", [128, D])

        ident = cst[:, CC_ID:CC_ID + 128]
        half_ident = cst[:, CC_HALF:CC_HALF + 128]
        tri = cst[0:TP, CC_TRI:CC_TRI + TP]

        ld_gb, ld_cst, ld_par, ld_small, ld_rows = sem("ld_gb"), sem("ld_cst"), sem("ld_par"), sem("ld_small"), sem("ld_rows")
        ld_w = [sem(f"ld_w{g}") for g in range(3)]
        ld_x = [sem(f"ld_x{g}") for g in range(3)]
        ld_ring = [sem(f"ld_ring{r}") for r in range(RING)]
        ld_xg = [sem(f"ld_xg{r}") for r in range(RING)]
        spare_zero, xn_stored, out_init = sem("spare_zero"), sem("xn_stored"), sem("out_init")
        dve_own, act_own, pool_own = sem("dve_own"), sem("act_own"), sem("pool_own")
        ones_ready, weff_ready, cnt_ready, sq_ready = sem("ones_ready"), sem("weff_ready"), sem("cnt_ready"), sem("sq_ready")
        betaw_mm, brow_ready, tok_mm, g_mm, sq_mm = sem("betaw_mm"), sem("brow_ready"), sem("tok_mm"), sem("g_mm"), sem("sq_mm")
        var_ready, rstd_ready = sem("var_ready"), sem("rstd_ready")
        h_ready = sem("h_ready")
        un_ready, unT_mm, unT_ready = sem("un_ready"), sem("unT_mm"), sem("unT_ready")
        win_mm, win_read = sem("win_mm"), sem("win_read")
        conv_done, xi_ready = sem("conv_done"), sem("xi_ready")
        xdbl_mm, xdbl_ready, dl_mm, dl_read_act, dl_read_dve = (sem("xdbl_mm"), sem("xdbl_ready"), sem("dl_mm"), sem("dl_read_act"), sem("dl_read_dve"))
        en_ready, ln_ready, corr_ready, spq_ready = sem("en_ready"), sem("ln_ready"), sem("corr_ready"), sem("spq_ready")
        delta_ready, rsum_ready, dx_ready, aexp_ready, av_ready = (sem("delta_ready"), sem("rsum_ready"), sem("dx_ready"), sem("aexp_ready"), sem("av_ready"))
        azero_ready = sem("azero_ready")
        bc_stored = sem("bc_stored")
        b_ready, c_ready = [[sem(f"{n}_ready{k}") for k in range(2)] for n in "bc"]
        a_ready, t1_ready, scan_done, wg_ready, p_dve, p_pool, p_used = (sem("a_ready"), sem("t1_ready"), sem("scan_done"), sem("wg_ready"), sem("p_dve"), sem("p_pool"), sem("p_used"))
        yd_done, y2_ready, wout_mm, h2_ready = sem("yd_done"), sem("y2_ready"), sem("wout_mm"), sem("h2_ready")
        rt_mm, rl_ready, ex_in, ex_out = sem("rt_mm"), sem("rl_ready"), sem("ex_in"), sem("ex_out")
        eq_ready, eqt_ready = sem("eq_ready"), sem("eqt_ready")
        msk_ready, cnt_mm, comb_ready, combT_mm, combT_ready, b2_mm, b2_read = (sem("msk_ready"), sem("cnt_mm"), sem("comb_ready"), sem("combT_mm"), sem("combT_ready"), sem("b2_mm"), sem("b2_read"))
        numbers_ready, facts_ready, eid_ready = sem("numbers_ready"), sem("facts_ready"), sem("eid_ready")
        oh_ready, idx_mm, idx_ready, slots_own = sem("oh_ready"), sem("idx_mm"), sem("idx_ready"), sem("slots_own")
        cnt_read, pool_turns = sem("cnt_read"), sem("pool_turns")
        xgT_mm, xgT_ready, h_mm, gelu_done, w2_done, y_ready = (sem("xgT_mm"), sem("xgT_ready"), sem("h_mm"), sem("gelu_done"), sem("w2_done"), sem("y_ready"))
        added = sem("added")
        o_oh, o_idx_mm, o_idx, o_xgT_mm, o_xgT, o_h_mm, o_gelu, o_w2, o_y, o_added, o_from, o_own = [
            sem("o_" + n) for n in ("oh", "idx_mm", "idx", "xgT_mm", "xgT", "h_mm", "gelu", "w2", "y", "added", "from", "own")]
        o_ld_ring = [sem(f"o_ld_ring{r}") for r in range(RING)]
        o_ld_xg = [sem(f"o_ld_xg{q}") for q in range(OVER)]

        def follower(engine, own):
            count = [0]

            def step(ins):
                count[0] += 1
                return ins.then_inc(own, 1)

            def settle():
                engine.wait_ge(own, count[0])

            return step, settle

        def on_pool(s):
            return s % 4 == 3

        def wait_product(engine, s):
            own = sum(on_pool(u) == on_pool(s) for u in range(s + 1))
            engine.wait_ge(p_pool if on_pool(s) else p_dve, own)

        def product(engine, s, done):
            g, j, k = s // NJ, s % NJ, s % 2
            engine.wait_ge(wg_ready, s + 1)
            engine.wait_ge(c_ready[g % 2], 16 * (g // 2 + 1))
            if s >= 2:
                engine.wait_ge(p_used, s - 1)
            engine.tensor_tensor(p_s[:, k], w_s[:, k], cc_n[:, g % 2], ALU.mult).then_inc(done, 1)

        def over_pair(r):
            return range(r * OVER // (RING - 1), (r + 1) * OVER // (RING - 1))

        def over_count(engine):
            return engine.value_load(eidi[0:1, OVER_PAD:OVER_PAD + 1], min_val=0, max_val=MAX_OVER)

        block = ctx.enter_context(nc.Block())

        @block.sync
        def _(sp):
            sp.dma_start(gbs[:], gb).then_inc(ld_gb, 16)
            for g in range(3):
                sp.dma_start(wsh_s[:, 3 * g:3 * g + 3], w_sh[:, 3 * g:3 * g + 3]).then_inc(ld_w[g], 16)
                sp.dma_start(x_s[:, 3 * g:3 * g + 3], x_t[:, 3 * g:3 * g + 3]).then_inc(ld_x[g], 16)
                if g == 0:
                    sp.dma_start(rws[:], rows).then_inc(ld_rows, 16)
                    sp.dma_start(cst[:], consts).then_inc(ld_cst, 16)
            sp.dma_start(par[:], params).then_inc(ld_par, 16)
            sp.dma_start(win_s[:], w_in.rearrange("(c p) n -> p c n", c=2)).then_inc(ld_small, 16)
            sp.dma_start(wdt_s[:], w_dt).then_inc(ld_small, 16)
            sp.dma_start(wrt_s[:], w_rt.rearrange("(c p) n -> p c n", c=2)).then_inc(ld_small, 16)
            sp.dma_start(b2_s[:], b2).then_inc(ld_small, 16)
            for r in range(RING):
                sp.dma_start(ringw1[:, r], w1_v[r]).then_inc(ld_ring[r], 16)
                sp.dma_start(ringw2[:, r], w2_v[r]).then_inc(ld_ring[r], 16)
            sp.wait_ge(ones_ready, 2)
            sp.dma_start(xn[N:N + CAP], zero_s[:]).then_inc(spare_zero, 16)
            sp.dma_start(out[N:N + CAP], zero_s[:]).then_inc(spare_zero, 16)
            sp.wait_ge(xdbl_ready, 1)
            sp.dma_start(bc, xdbl[DTR:XW, :]).then_inc(bc_stored, 16)
            sp.wait_ge(bc_stored, 16)
            for g in range(NGRP):
                if g >= 2:
                    sp.wait_ge(t1_ready, NJ * (g - 1))
                sp.dma_start(bb_n[:, g % 2], bc[g * NG:(g + 1) * NG, :].unsqueeze(0).to_broadcast([128, NG, N])).then_inc(b_ready[g % 2], 16)
                if g >= 2:
                    for s in range(NJ * (g - 2), NJ * (g - 1)):
                        wait_product(sp, s)
                sp.dma_start(cc_n[:, g % 2], bc[NST + g * NG:NST + (g + 1) * NG, :].unsqueeze(0).to_broadcast([128, NG, N])).then_inc(c_ready[g % 2], 16)

            sp.wait_ge(un_ready, 2 * NT)
            sp.dma_start(xn[0:N].rearrange("(t p) d -> p t d", p=TP), un[:]).then_inc(xn_stored, 16)
            sp.wait_ge(b2_read, 1)
            sp.dma_start(out_v, h1[:]).then_inc(out_init, 16)
            with sp.Fori(0, NE // RING - 1) as i:
                for r in range(RING):
                    e = i * RING + (RING + r)
                    sp.wait_ge(w2_done, i * RING + (r + 1))
                    sp.dma_start(ringw1[:, r], w1_v[bass.ds(e, 1)].rearrange("a p c m -> p (a c) m")).then_inc(ld_ring[r], 16)
                    sp.dma_start(ringw2[:, r], w2_v[bass.ds(e, 1)].rearrange("a p c d -> p (a c) d")).then_inc(ld_ring[r], 16)
            sp.wait_ge(eid_ready, 1)
            n_over = over_count(sp)

            def over_weights(i, q, first):
                with sp.If(n_over > i * OVER + q):
                    e = sp.value_load(eidi[0:1, bass.ds(i * OVER + q, 1)], min_val=0, max_val=NE - 1)
                    if first and q < RING:
                        sp.wait_ge(w2_done, NE - RING + 1 + q)
                    elif q >= RING:
                        sp.wait_ge(o_w2, i * OVER + (q - RING + 1))
                    else:
                        before = q + RING if q + RING < OVER else q
                        sp.wait_ge(o_w2, i * OVER + (before + 1 - OVER))
                    r = q % RING
                    sp.dma_start(ringw1[:, r], w1_v[bass.ds(e, 1)].rearrange("a p c m -> p (a c) m")).then_inc(o_ld_ring[r], 16)
                    sp.dma_start(ringw2[:, r], w2_v[bass.ds(e, 1)].rearrange("a p c d -> p (a c) d")).then_inc(o_ld_ring[r], 16)

            for q in range(OVER):
                over_weights(0, q, True)
            with sp.Fori(1, OVER_ROUNDS) as i:
                with sp.If(n_over > i * OVER):
                    for q in range(OVER):
                        over_weights(i, q, False)
            sp.wait_ge(spare_zero, 32)
            sp.wait_ge(added, 16 * NE)

        @block.tensor
        def _(pe):
            def mm(o, a, b, start=True, stop=True, **k):
                return pe.matmul(o, a, b, start=start, stop=stop, **k)

            pe.wait_ge(ld_gb, 16)
            for c in range(NKC):
                if c % 3 == 0:
                    pe.wait_ge(ld_w[c // 3], 16)
                for s in range(NSH):
                    k = c * NSH + s
                    last = mm(PS[0:1, 7, 0:D], gbs[:, GC_B + k:GC_B + k + 1], wsh_s[:, c, s], k == 0, k == NKC * NSH - 1)
            last.then_inc(betaw_mm, 1)
            pe.wait_ge(cnt_ready, 1)
            for c in range(NKC):
                if c % 3 == 0:
                    pe.wait_ge(ld_x[c // 3], 16)
                pe.wait_ge(weff_ready, c + 1)
                for t in range(NT):
                    last = mm(PS[0:TP, t, 0:D + 1], x_s[:, c, t * TP:(t + 1) * TP], weff[:, c], c == 0, c == NKC - 1)
            last.then_inc(tok_mm, 1)
            pe.wait_ge(ones_ready, 1)
            for c in range(NKC):
                mm(PS[0:TP, 6, 0:D], ones[0:KC, 0:TP], weff[:, c, 0:D], c == 0, c == NKC - 1)
            pe.wait_ge(brow_ready, 1)
            mm(PS[0:TP, 6, D:2 * D], ones[0:1, 0:TP], brow[:]).then_inc(g_mm, 1)
            pe.wait_ge(sq_ready, 3)
            for t in range(NT):
                for c in range(NKC):
                    last = mm(PS[0:TP, 7, t:t + 1], xsq[:, c, t * TP:(t + 1) * TP], weff[:, c, D:D + 1], c == 0, c == NKC - 1)
            last.then_inc(sq_mm, 1)

            def transposes(done):
                pe.wait_ge(ld_cst, 16)
                for t in range(NT):
                    pe.wait_ge(un_ready, done * NT + t + 1)
                    for c in range(2):
                        last = pe.transpose(PS[0:HALF_D, 2 * c + t // 3, (t % 3) * TP:(t % 3 + 1) * TP],
                                            un[:, t, c * HALF_D:(c + 1) * HALF_D], ident[0:TP, 0:TP])
                last.then_inc(unT_mm, 1)

            pe.wait_ge(h_ready, NT)
            transposes(0)
            pe.wait_ge(ld_small, 16 * 4)
            pe.wait_ge(ld_rows, 16)
            pe.wait_ge(unT_ready, 2)
            for j in range(2 * NJ):
                if j >= 4:
                    pe.wait_ge(win_read, j - 3)
                for hf in range(2):
                    for c in range(2):
                        last = mm(PS[:, (4 + 2 * j + hf) % 8, 0:HB], win_s[:, c, j * 128:(j + 1) * 128],
                                  unT[:, c, hf * HB:(hf + 1) * HB], c == 0, c == 1)
                last.then_inc(win_mm, 1)
            pe.wait_ge(ld_par, 16)
            pe.wait_ge(win_read, 3)
            for j in range(NJ):
                pe.wait_ge(xi_ready, j + 1)
                for hf in range(2):
                    last = mm(PS[0:XW, hf, 0:HB], par[:, PC_WX + j * XW:PC_WX + (j + 1) * XW],
                              xi[:, j, hf * HB:(hf + 1) * HB], j == 0, j == NJ - 1, skip_group_check=True)
            last.then_inc(xdbl_mm, 1)
            pe.wait_ge(xdbl_ready, 1)
            pe.wait_ge(win_read, 6)
            for j in range(NJ):
                for hf in range(2):
                    last = mm(PS[:, 2 + 2 * j + hf, 0:HB], wdt_s[:, j * 128:(j + 1) * 128], xdbl[0:DTR, hf * HB:(hf + 1) * HB])
                last.then_inc(dl_mm, 1)

            pe.wait_ge(dl_read_act, NJ)
            pe.wait_ge(dl_read_dve, NJ)
            for s in range(STEPS):
                g, j, k = s // NJ, s % NJ, s % 2
                wait_product(pe, s)
                for n in range(NG):
                    lo = j * N
                    while lo < (j + 1) * N:
                        hi = min((j + 1) * N, (lo // 512 + 1) * 512)
                        first = s < NJ and n == 0 and lo % 512 == 0
                        last = mm(PSF[:, 4 * 512 + lo:4 * 512 + hi], half_ident, p_s[:, k, n, lo - j * N:hi - j * N],
                                  first, s >= STEPS - NJ and n == NG - 1, skip_group_check=True)
                        lo = hi
                last.then_inc(p_used, 1)
            pe.wait_ge(y2_ready, NJ)
            for t in range(NT):
                for j in range(NJ):
                    last = mm(PS[0:TP, t, 0:D], dx[:, j, t * TP:(t + 1) * TP],
                              par[:, PC_WOUT + j * D:PC_WOUT + (j + 1) * D], j == 0, j == NJ - 1)
                last.then_inc(wout_mm, 1)
            pe.wait_ge(h2_ready, NT)
            transposes(1)
            pe.wait_ge(unT_ready, 4)
            for t in range(NT):
                o = PS[0:TP, 4, t * (G + NE):(t + 1) * (G + NE)]
                for c in range(2):
                    mm(o, unT[:, c, t * TP:(t + 1) * TP], wrt_s[:, c], c == 0, False)
                last = mm(o, ones[0:1, 0:TP], rws[0:1, D:D + G + NE], False, True)
            last.then_inc(rt_mm, 1)
            pe.wait_ge(msk_ready, 1)
            for t in range(NT):
                o = PS[0:TP, 5, t * NE:(t + 1) * NE]
                for u in range(t):
                    mm(o, ones[0:TP, 0:TP], msk[:, u], u == 0, False)
                mm(o, tri, msk[:, t], t == 0, True)
            for t in range(NT):
                last = mm(PS[:, 6, 0:NE], ones[0:TP, :], msk[:, t], t == 0, t == NT - 1)
            last.then_inc(cnt_mm, 1)
            def combine_bias():
                pe.wait_ge(comb_ready, 1)
                for t in range(NT):
                    last = pe.transpose(PS[0:NE, t // 3, (t % 3) * TP:(t % 3 + 1) * TP], comb[:, t], ident[0:TP, 0:TP])
                last.then_inc(combT_mm, 1)
                pe.wait_ge(combT_ready, 1)
                for t in range(NT):
                    last = mm(PS[0:TP, 2 + t // 2, (t % 2) * D:(t % 2 + 1) * D], combT[:, t * TP:(t + 1) * TP], b2_s[:])
                last.then_inc(b2_mm, 1)
                pe.wait_ge(b2_read, 1)

            def facts_of(hot, q, e):
                for t in range(NT):
                    last = mm(PS[:, 7, q * 8:q * 8 + NR], hot[:, t], facts[:, t, e].rearrange("p a r -> p (a r)"),
                              t == 0, t == NT - 1)
                return last

            def next_facts(i, r, first):
                e = i * RING + r
                q = (r + RING - 1) % RING
                pe.wait_ge(oh_ready, e + RING)
                pe.wait_ge(idx_ready, e + 1)
                if first and r >= 1:
                    over_facts(0, over_pair(r - 1))
                facts_of(oh[:, q], q, bass.ds(e + (RING - 1), 1)).then_inc(idx_mm, 1)

            def hidden(i, r, first):
                e = i * RING + r
                pe.wait_ge(xgT_ready, e + 1)
                pe.wait_ge(ld_ring[r], i * 32 + 32)
                for m in range(NMC):
                    if not (first and r * NMC + m < 4):
                        pe.wait_ge(gelu_done, e * NMC + (m - 3))
                    for c in range(2):
                        last = mm(PS[:, (r * NMC + m) % 4, 0:CAP], ringw1[:, r, c, m * 128:(m + 1) * 128],
                                  xgT[:, r % 2, c], c == 0, c == 1)
                    last.then_inc(h_mm, 1)

            def tokens(i, r):
                pe.wait_ge(ld_xg[r], i * 16 + 16)
                for c in range(2):
                    last = pe.transpose(PS[0:HALF_D, 6, c * CAP:(c + 1) * CAP], xg[:, r, c * HALF_D:(c + 1) * HALF_D], ident)
                last.then_inc(xgT_mm, 1)

            def output(i, r, first):
                e = i * RING + r
                if not (first and r < 2):
                    pe.wait_ge(y_ready, e - 1)
                for m in range(NMC):
                    pe.wait_ge(gelu_done, e * NMC + (m + 1))
                    last = mm(PS[:, 4 + r % 2, 0:D], hT[:, r % 2, m], ringw2[:, r, m], m == 0, m == NMC - 1)
                last.then_inc(w2_done, 1)

            def experts(i, first=False, final=False):
                for r in range(RING):
                    hidden(i, r, first)
                    if final and r == 2:
                        pe.wait_ge(o_xgT, 1)
                    if r + 1 < RING:
                        tokens(i, r + 1)
                    elif not final:
                        tokens(i + 1, 0)
                    if not (final and r >= 1):
                        next_facts(i, r, first)
                    output(i, r, first)
                    if first and r < RING - 1:
                        if r == 0:
                            pe.wait_ge(eid_ready, 1)
                        for q in over_pair(r):
                            over_expert(0, q)
                    if final and r >= 1:
                        for q in over_pair(r - 1):
                            over_tokens(0, q, True)

            experts_of = {}

            def over_expert(i, q):
                experts_of[q] = pe.value_load(eidi[0:1, bass.ds(i * OVER + q, 1)], min_val=0, max_val=NE - 1)

            def over_facts(i, tiles):
                pe.wait_ge(o_oh, i * OVER + (tiles[-1] + 1))
                for q in tiles:
                    last = facts_of(ooh[:, q], RING + q, bass.ds(experts_of[q], 1))
                if tiles[-1] == OVER - 1:
                    last.then_inc(o_idx_mm, 1)

            def over_tokens(i, q, first):
                pe.wait_ge(o_ld_xg[q], i * 16 + 16)
                if q >= 2:
                    pe.wait_ge(o_xgT, i * OVER + (q - 1))
                    if first and q == 2:
                        pe.wait_ge(xgT_ready, NE)
                elif first and q == 0:
                    pe.wait_ge(xgT_ready, NE - 1)
                elif first:
                    pe.wait_ge(idx_ready, NE - RING + 2)
                elif q == 1:
                    pe.wait_ge(o_idx, i + 1)
                for c in range(2):
                    last = pe.transpose(PS[0:HALF_D, 6 + q % 2, c * CAP:(c + 1) * CAP], oxg[:, q, c * HALF_D:(c + 1) * HALF_D], ident)
                last.then_inc(o_xgT_mm, 1)

            def over_tile(i, q, first):
                r = q % RING
                uses = 2 if r + RING < OVER else 1
                with pe.If(n_over > i * OVER + q):
                    pe.wait_ge(o_xgT, i * OVER + (q + 1))
                    pe.wait_ge(o_ld_ring[r], i * (32 * uses) + (64 if q >= RING else 32))
                    for m in range(NMC):
                        c4 = q * NMC + m
                        if not first or c4 >= 4:
                            pe.wait_ge(o_gelu, i * (OVER * NMC) + (c4 - 3))
                        elif c4 == 0:
                            pe.wait_ge(gelu_done, NE * NMC)
                        for c in range(2):
                            last = mm(PS[:, c4 % 4, 0:CAP], ringw1[:, r, c, m * 128:(m + 1) * 128], oxgT[:, q, c], c == 0, c == 1)
                        last.then_inc(o_h_mm, 1)
                    if first and q < 2:
                        pe.wait_ge(y_ready, NE)
                    else:
                        pe.wait_ge(o_y, i * OVER + (q - 1))
                    for m in range(NMC):
                        pe.wait_ge(o_gelu, i * (OVER * NMC) + (q * NMC + m + 1))
                        last = mm(PS[:, 4 + q % 2, 0:D], hT[:, q % 2, m], ringw2[:, r, m], m == 0, m == NMC - 1)
                    last.then_inc(o_w2, 1)

            pe.wait_ge(facts_ready, 3)
            pe.wait_ge(numbers_ready, 3)
            pe.wait_ge(oh_ready, RING - 1)
            for e in range(RING - 1):
                last = facts_of(oh[:, e], e, slice(e, e + 1))
            last.then_inc(idx_mm, 1)
            combine_bias()
            pe.wait_ge(cnt_read, 1)
            tokens(0, 0)
            experts(0, first=True)
            n_over = over_count(pe)
            with pe.Fori(1, NE // RING - 1) as i:
                experts(i)
            experts(NE // RING - 1, final=True)
            for q in range(OVER):
                over_tile(0, q, True)
            with pe.Fori(1, OVER_ROUNDS) as i:
                with pe.If(n_over > i * OVER):
                    for q in range(OVER):
                        over_expert(i, q)
                    over_facts(i, range(OVER))
                    for q in range(OVER):
                        over_tokens(i, q, False)
                    for q in range(OVER):
                        over_tile(i, q, False)

        @block.scalar
        def _(act):
            step, settle = follower(act, act_own)
            for g in range(3):
                act.wait_ge(ld_x[g], 16)
                act.activation(xsq[:, 3 * g:3 * g + 3], x_s[:, 3 * g:3 * g + 3], ACT.Square).then_inc(sq_ready, 1)
            act.wait_ge(unT_mm, 1)
            act.copy(unT[:, 0].rearrange("p (h n) -> p h n", h=2), PS[0:HALF_D, 0:2, 0:HB]).then_inc(unT_ready, 1)
            act.wait_ge(azero_ready, 1)
            for j in range(NJ):
                act.wait_ge(win_mm, j + 1)
                b0 = (4 + 2 * j) % 8
                act.copy(xpad[:, j, :, KS - 1:].rearrange("p (h b) l -> p h b l", h=2),
                         PS[:, b0:b0 + 2, 0:HB].rearrange("p h (b l) -> p h b l", l=L)).then_inc(win_read, 1)
            for j in range(NJ):
                act.wait_ge(win_mm, NJ + j + 1)
                b0 = (4 + 2 * (NJ + j)) % 8
                act.activation(sres[:, j].rearrange("p (h n) -> p h n", h=2), PS[:, b0:b0 + 2, 0:HB], ACT.Silu).then_inc(win_read, 1)
            for j in range(NJ):
                act.wait_ge(conv_done, j + 1)
                act.activation(xi[:, j], xc[:, j], ACT.Silu).then_inc(xi_ready, 1)
            act.wait_ge(ld_par, 16)
            act.activation(av[:, 0], par[:, PC_ALOG:PC_ALOG + NJ * NST], ACT.Exp).then_inc(aexp_ready, 1)
            for j in range(NJ):
                act.wait_ge(dl_mm, j + 1)
                act.activation(sp_en[:, j].rearrange("p (h n) -> p h n", h=2), PS[:, 2 + 2 * j:4 + 2 * j, 0:HB], ACT.Abs,
                               bias=par[:, PC_BDT + j:PC_BDT + j + 1]).then_inc(dl_read_act, 1)
            for j in range(NJ):
                act.wait_ge(dl_read_act, j + 1)
                act.activation(sp_en[:, j], sp_en[:, j], ACT.Exp, scale=-1.0).then_inc(en_ready, 1)
            for j in range(NJ):
                act.wait_ge(en_ready, j + 1)
                act.activation(sp_ln[:, j], sp_en[:, j], ACT.Ln, bias=1.0).then_inc(ln_ready, 1)
            act.wait_ge(delta_ready, NJ)
            act.wait_ge(rsum_ready, 1)
            act.wait_ge(av_ready, 2)

            s_view = rsum[:, 1:NJ * N + 1].rearrange("p (j n) -> p j n", j=NJ)
            d_view = delta.rearrange("p j (b l) -> p j b l", l=L)
            for s in range(STEPS):
                g, j, k = s // NJ, s % NJ, s % 2
                if s >= 2:
                    act.wait_ge(wg_ready, s - 1)
                for n in range(NG):
                    q = j * NST + g * NG + n
                    act.activation(a_s[:, k, n, :, 1:L], d_view[:, j, :, 1:L], ACT.Exp, scale=av[:, 1, q:q + 1])
                    last = act.activation(th_s[:, k, n], s_view[:, j], ACT.Tanh, scale=av[:, 2, q:q + 1], bias=guard[:])
                last.then_inc(a_ready, 1)
            act.wait_ge(unT_mm, 2)
            act.copy(unT[:, 0].rearrange("p (h n) -> p h n", h=2), PS[0:HALF_D, 0:2, 0:HB]).then_inc(unT_ready, 1)
            act.wait_ge(ex_in, 1)
            act.activation(sm[:, 0:NT * (G + NE)], sm[:, 0:NT * (G + NE)], ACT.Exp).then_inc(ex_out, 1)

            def gelus(i, first):
                for r in range(RING):
                    e = i * RING + r
                    if not (first and r < 2):
                        act.wait_ge(w2_done, e - 1)
                    for m in range(NMC):
                        act.wait_ge(h_mm, e * NMC + (m + 1))
                        col = e * NMC + (PC_B1 + m)
                        act.activation(hT[:, r % 2, m], PS[:, (r * NMC + m) % 4, 0:CAP], ACT.Gelu,
                                       bias=par[:, bass.ds(col, 1)]).then_inc(gelu_done, 1)

            gelus(0, True)
            act.wait_ge(eid_ready, 1)
            n_over = over_count(act)
            with act.Fori(1, NE // RING) as i:
                gelus(i, False)

            def over_gelus(i, q, first):
                with act.If(n_over > i * OVER + q):
                    e = act.value_load(eidi[0:1, bass.ds(i * OVER + q, 1)], min_val=0, max_val=NE - 1)
                    if first and q < 2:
                        act.wait_ge(w2_done, NE - 1 + q)
                    else:
                        act.wait_ge(o_w2, i * OVER + (q - 1))
                    for m in range(NMC):
                        act.wait_ge(o_h_mm, i * (OVER * NMC) + (q * NMC + m + 1))
                        act.activation(hT[:, q % 2, m], PS[:, (q * NMC + m) % 4, 0:CAP], ACT.Gelu,
                                       bias=par[:, bass.ds(e * NMC + (PC_B1 + m), 1)]).then_inc(o_gelu, 1)

            for q in range(OVER):
                over_gelus(0, q, True)
            with act.Fori(1, OVER_ROUNDS) as i:
                with act.If(n_over > i * OVER):
                    for q in range(OVER):
                        over_gelus(i, q, False)

        @block.gpsimd
        def _(pool):
            step, settle = follower(pool, pool_own)
            pool.memset(ones[:], 1.0).then_inc(ones_ready, 1)
            pool.memset(zero_s[:], 0.0).then_inc(ones_ready, 1)
            step(pool.memset(st[:, 64:64 + NT], -0.5))
            settle()
            pool.wait_ge(ld_cst, 16)
            for c in range(2):
                pool.tensor_copy(facts[:, :, :, c], cst[0:TP, CC_TOK + c * NT:CC_TOK + (c + 1) * NT].unsqueeze(2)
                                 .to_broadcast([TP, NT, NE])).then_inc(numbers_ready, 1)
            pool.memset(facts[:, :, :, 2], 1.0).then_inc(numbers_ready, 1)

            def inverse_root(k):
                pool.wait_ge(var_ready, k + 1)
                pool.tensor_tensor(st[:, 32:32 + NT], st[:, 24:24 + NT], st[:, 64:64 + NT], ALU.pow).then_inc(rstd_ready, 1)

            inverse_root(0)
            inverse_root(1)
            pool.wait_ge(tok_mm, 1)
            pool.wait_ge(g_mm, 1)
            pool.wait_ge(sq_mm, 1)
            pool.wait_ge(h_ready, NT)
            pool.memset(xpad[:, :, :, 0:KS - 1], 0.0).then_inc(azero_ready, 1)
            pool.memset(a_s[:, :, :, :, 0:1].rearrange("p a b c d -> p (a b) c d"), 0.0).then_inc(azero_ready, 1)
            pool.memset(guard[:], 0.5 * LOG_GUARD).then_inc(azero_ready, 1)
            step(pool.memset(mask[:], 1.0))
            settle()
            pool.memset(mask[:].rearrange("p (b l) -> p b l", l=L)[:, :, L - 1:L], 0.0).then_inc(azero_ready, 1)
            for j in range(NJ):
                pool.wait_ge(corr_ready, j + 1)
                step(pool.tensor_tensor(dx[:, j], sp_en[:, j], dx[:, j], ALU.subtract))
                settle()
                pool.wait_ge(dl_read_dve, j + 1)
                pool.tensor_tensor(dx[:, j], dx[:, j], delta[:, j], ALU.add).then_inc(spq_ready, 1)
            for j in range(NJ):
                pool.wait_ge(delta_ready, j + 1)
                pool.tensor_tensor(dx[:, j], delta[:, j], xi[:, j], ALU.mult).then_inc(dx_ready, 1)

            def inputs(s):
                g, j, k = s // NJ, s % NJ, s % 2
                if j == 0:
                    pool.wait_ge(b_ready[g % 2], 16 * (g // 2 + 1))
                if s >= 2:
                    pool.wait_ge(scan_done, s - 1)
                pool.tensor_tensor(t1_s[:, k], dx[:, j].unsqueeze(1).to_broadcast([128, NG, N]), bb_n[:, g % 2], ALU.mult).then_inc(t1_ready, 1)

            pool.wait_ge(dx_ready, NJ)
            inputs(0)
            for s in range(STEPS):
                if s + 1 < STEPS:
                    inputs(s + 1)
                if on_pool(s):
                    product(pool, s, p_pool)
            for j in range(NJ):
                pool.wait_ge(yd_done, j + 1)
                pool.tensor_tensor(dx[:, j], xc[:, j], sres[:, j], ALU.mult).then_inc(y2_ready, 1)
            inverse_root(2)
            pool.wait_ge(eq_ready, 1)
            pool.wait_ge(ld_cst, 16)
            pool.tensor_tensor(eq4, eq4, cst[0:TP, CC_LT4:CC_LT4 + G * G].rearrange("p (i j) -> p i j", i=G).unsqueeze(1)
                               .to_broadcast([TP, NT, G, G]), ALU.mult).then_inc(eqt_ready, 1)
            pool.wait_ge(eq_ready, 2)
            pool.tensor_tensor(eq8, eq8, cst[0:TP, CC_LT8:CC_LT8 + E * E].rearrange("p (i j) -> p i j", i=E).unsqueeze(1)
                               .to_broadcast([TP, NT * G, E, E]), ALU.mult).then_inc(eqt_ready, 1)
            pool.wait_ge(spare_zero, 32)
            pool.wait_ge(xn_stored, 16)

            def gather(tile, col, done):
                pool.sem_inc(pool_turns, 1)
                pool.indirect_dma_start(tile, None, xn[:], bass.IndirectOffsetOnAxis(ap=idx[:, col:col + 1], axis=0)).then_inc(done, 16)

            def add(src, col, done):
                pool.sem_inc(pool_turns, 1)
                pool.indirect_dma_start(out[:], bass.IndirectOffsetOnAxis(ap=idx[:, col:col + 1], axis=0), src, None,
                                        compute_op=ALU.add).then_inc(done, 16)

            def expert_io(i, first=False, final=False):
                for r in range(RING):
                    e = i * RING + r
                    pool.wait_ge(y_ready, e + 1)
                    if not (first and r == 0):
                        pool.wait_ge(added, e * 16)
                    add(y_s[:, r % 2], r, added)
                    if not (final and r >= 1):
                        q = (r + RING - 1) % RING
                        pool.wait_ge(idx_ready, e + 2)
                        gather(xg[:, q], q, ld_xg[q])
                    if final and r < 2:
                        over_gathers(0, r * OVER // 2, (r + 1) * OVER // 2)

            def over_gathers(i, lo, hi):
                pool.wait_ge(o_idx, i + 1)
                for q in range(lo, hi):
                    gather(oxg[:, q], RING + q, o_ld_xg[q])

            def over_adds(i, first):
                for q in range(OVER):
                    with pool.If(n_over > i * OVER + q):
                        pool.wait_ge(o_y, i * OVER + (q + 1))
                        if first and q == 0:
                            pool.wait_ge(added, 16 * NE)
                        add(y_s[:, q % 2], RING + q, o_added)
                        pool.wait_ge(o_added, i * (16 * OVER) + 16 * (q + 1))

            pool.wait_ge(idx_ready, 1)
            for e in range(RING - 1):
                gather(xg[:, e], e, ld_xg[e])
            pool.wait_ge(out_init, 16)
            expert_io(0, first=True)
            with pool.Fori(1, NE // RING - 1) as i:
                expert_io(i)
            pool.wait_ge(eid_ready, 1)
            n_over = over_count(pool)
            expert_io(NE // RING - 1, final=True)
            over_adds(0, True)
            with pool.Fori(1, OVER_ROUNDS) as i:
                with pool.If(n_over > i * OVER):
                    over_gathers(i, 0, OVER)
                    over_adds(i, False)

        @block.vector
        def _(dve):
            step, settle = follower(dve, dve_own)
            mean, ex2, var, rstd, nm = (st[:, 0:NT], st[:, 8:8 + NT], st[:, 24:24 + NT], st[:, 32:32 + NT], st[:, 40:40 + NT])
            bst = st[:, 72:72 + 6]
            mv = st[:, 80:80 + 2 * NT]

            dve.wait_ge(ld_gb, 16)
            dve.tensor_copy(weff[:, :, D], gbs[:, GC_CNT:GC_CNT + NKC]).then_inc(cnt_ready, 1)
            for g in range(3):
                dve.wait_ge(ld_w[g], 16)
                for s in range(NSH):
                    settle()
                    for c in range(3 * g, 3 * g + 3):
                        k = GC_G + c * NSH + s
                        if s == 0:
                            step(dve.tensor_scalar(weff[:, c, 0:D], wsh_s[:, c, 0], gbs[:, k:k + 1], None, ALU.mult))
                        else:
                            ins = dve.scalar_tensor_tensor(out=weff[:, c, 0:D], in0=wsh_s[:, c, s], scalar=gbs[:, k:k + 1],
                                                           in1=weff[:, c, 0:D], op0=ALU.mult, op1=ALU.add)
                            if s == NSH - 1:
                                ins.then_inc(weff_ready, 1)
                            else:
                                step(ins)
            dve.wait_ge(betaw_mm, 1)
            dve.wait_ge(ld_rows, 16)
            dve.tensor_tensor(brow[:], PS[0:1, 7, 0:D], rws[0:1, 0:D], ALU.add).then_inc(brow_ready, 1)
            dve.wait_ge(g_mm, 1)
            step(dve.tensor_copy(bb_s, PS[0:TP, 6, D:2 * D]))
            dve.wait_ge(tok_mm, 1)
            step(dve.tensor_scalar(mean, PS[0:TP, 0:NT, D], 1.0 / F, None, ALU.mult))
            settle()
            step(dve.tensor_tensor(ex2, mean, mean, ALU.mult))
            dve.wait_ge(sq_mm, 1)
            settle()
            step(dve.scalar_tensor_tensor(out=var, in0=PS[0:TP, 7, 0:NT], scalar=1.0 / F, in1=ex2, op0=ALU.mult, op1=ALU.subtract))
            settle()
            dve.tensor_scalar(var, var, TOK_EPS, None, ALU.add).then_inc(var_ready, 1)
            dve.wait_ge(rstd_ready, 1)
            step(dve.scalar_tensor_tensor(out=nm, in0=mean, scalar=-1.0, in1=rstd, op0=ALU.mult, op1=ALU.mult))
            settle()
            for t in range(NT):
                step(dve.scalar_tensor_tensor(out=gmu[:, t], in0=PS[0:TP, 6, 0:D], scalar=nm[:, t:t + 1], in1=bb_s, op0=ALU.mult, op1=ALU.add))
            settle()
            for t in range(NT):
                dve.scalar_tensor_tensor(out=h1[:, t], in0=PS[0:TP, t, 0:D], scalar=rstd[:, t:t + 1], in1=gmu[:, t],
                                         op0=ALU.mult, op1=ALU.add).then_inc(h_ready, 1)

            def layernorm(src, ready, k):
                dve.wait_ge(ready, NT)
                bs6 = st[:, 92:92 + 36].rearrange("p (t s) -> p t s", s=6)
                for t in range(NT):
                    step(dve.bn_stats(bs6[:, t], src[:, t]))
                settle()
                for t in range(NT):
                    step(dve.bn_aggr(mv[:, 2 * t:2 * t + 2], bs6[:, t]))
                settle()
                mvv = mv.rearrange("p (t s) -> p t s", s=2)
                dve.tensor_scalar(var, mvv[:, :, 1], LN_EPS, None, ALU.add).then_inc(var_ready, 1)
                dve.wait_ge(rstd_ready, k + 1)
                for t in range(NT):
                    dve.tensor_scalar(un[:, t], src[:, t], mv[:, 2 * t:2 * t + 1], rstd[:, t:t + 1],
                                      ALU.subtract, ALU.mult).then_inc(un_ready, 1)
                dve.wait_ge(unT_mm, k)
                dve.tensor_copy(unT[:, 1].rearrange("p (h n) -> p h n", h=2), PS[0:HALF_D, 2:4, 0:HB]).then_inc(unT_ready, 1)

            layernorm(h1, h_ready, 1)
            dve.wait_ge(ld_par, 16)
            xcb = xc.rearrange("p j (b l) -> p j b l", l=L)
            for j in range(NJ):
                dve.wait_ge(win_read, j + 1)
                for k in range(KS):
                    w = par[:, PC_CONVW + j * KS + k:PC_CONVW + j * KS + k + 1]
                    src = xpad[:, j, :, k:k + L]
                    settle()
                    if k == 0:
                        step(dve.tensor_scalar(xcb[:, j], src, w, par[:, PC_CONVB + j:PC_CONVB + j + 1], ALU.mult, ALU.add))
                    else:
                        ins = dve.scalar_tensor_tensor(out=xcb[:, j], in0=src, scalar=w, in1=xcb[:, j], op0=ALU.mult, op1=ALU.add)
                        if k == KS - 1:
                            ins.then_inc(conv_done, 1)
                        else:
                            step(ins)
            dve.wait_ge(aexp_ready, 1)
            dve.tensor_scalar(av[:, 1], av[:, 0], -1.0, None, ALU.mult).then_inc(av_ready, 1)
            dve.tensor_scalar(av[:, 2], av[:, 0], -0.5, None, ALU.mult).then_inc(av_ready, 1)
            dve.wait_ge(xdbl_mm, 1)
            dve.tensor_copy(xdbl.rearrange("p (h n) -> p h n", h=2), PS[0:XW, 0:2, 0:HB]).then_inc(xdbl_ready, 1)
            for j in range(NJ):
                dve.wait_ge(dl_read_act, j + 1)
                dve.tensor_scalar(delta[:, j].rearrange("p (h n) -> p h n", h=2), PS[:, 2 + 2 * j:4 + 2 * j, 0:HB],
                                  par[:, PC_BDT + j:PC_BDT + j + 1], 0.0, ALU.add, ALU.max).then_inc(dl_read_dve, 1)
            for j in range(NJ):
                dve.wait_ge(en_ready, j + 1)
                dve.tensor_scalar(dx[:, j], sp_en[:, j], 1.0, 1.0, ALU.add, ALU.subtract).then_inc(corr_ready, 1)
            for j in range(NJ):
                dve.wait_ge(ln_ready, j + 1)
                dve.wait_ge(spq_ready, j + 1)
                dve.tensor_tensor(delta[:, j], sp_ln[:, j], dx[:, j], ALU.add).then_inc(delta_ready, 1)

            dve.wait_ge(azero_ready, 4)
            dve.wait_ge(delta_ready, NJ)
            step(dve.tensor_tensor_scan(rsum[:, 0:NJ * N][:, ::-1], mask[:, ::-1], delta.rearrange("p j n -> p (j n)")[:, ::-1],
                                        0.0, ALU.mult, ALU.add))
            settle()
            dve.memset(rsum[:, L:NJ * N + 1:L], 0.0).then_inc(rsum_ready, 1)
            def guarded(s):
                k = s % 2
                dve.wait_ge(scan_done, s + 1)
                dve.scalar_tensor_tensor(out=w_s[:, k], in0=th_s[:, k], scalar=1.0, in1=w_s[:, k],
                                         op0=ALU.add, op1=ALU.mult).then_inc(wg_ready, 1)

            for s in range(STEPS + 1):
                k = s % 2
                if s >= 1:
                    guarded(s - 1)
                if s < STEPS:
                    dve.wait_ge(a_ready, s + 1)
                    dve.wait_ge(t1_ready, s + 1)
                    if s >= 2:
                        wait_product(dve, s - 2)
                    dve.tensor_tensor_scan(w_s[:, k].rearrange("p n l -> p (n l)"), a_s[:, k].rearrange("p n b l -> p (n b l)"),
                                           t1_s[:, k].rearrange("p n l -> p (n l)"), 0.0, ALU.mult, ALU.add).then_inc(scan_done, 1)
                if s >= 1 and not on_pool(s - 1):
                    product(dve, s - 1, p_dve)
            dve.wait_ge(p_used, STEPS)
            for j in range(NJ):
                dve.scalar_tensor_tensor(out=xc[:, j], in0=xi[:, j], scalar=par[:, PC_D + j:PC_D + j + 1],
                                         in1=PSF[:, 4 * 512 + j * N:4 * 512 + (j + 1) * N], op0=ALU.mult, op1=ALU.add).then_inc(yd_done, 1)
            for t in range(NT):
                dve.wait_ge(wout_mm, t + 1)
                dve.tensor_tensor(h2[:, t], PS[0:TP, t, 0:D], h1[:, t], ALU.add).then_inc(h2_ready, 1)
            layernorm(h2, h2_ready, 2)

            dve.wait_ge(rt_mm, 1)
            lg = PS[0:TP, 4, 0:NT * (G + NE)].rearrange("p (t c) -> p t c", t=NT)
            step(dve.tensor_copy(rl, lg))
            settle()
            step(dve.tensor_copy(el.rearrange("p (t g) e -> p t g e", t=NT), rl[:, :, G:].rearrange("p t (g e) -> p t g e", g=G)))
            gl = rl[:, :, 0:G]
            dve.tensor_tensor(eq4, gl.unsqueeze(2).to_broadcast([TP, NT, G, G]), gl.unsqueeze(3).to_broadcast([TP, NT, G, G]),
                              ALU.is_equal).then_inc(eq_ready, 1)
            settle()
            dve.tensor_tensor(eq8, el.unsqueeze(2).to_broadcast([TP, NT * G, E, E]), el.unsqueeze(3).to_broadcast([TP, NT * G, E, E]),
                              ALU.is_equal).then_inc(eq_ready, 1)
            step(dve.tensor_tensor(gt4, gl.unsqueeze(2).to_broadcast([TP, NT, G, G]), gl.unsqueeze(3).to_broadcast([TP, NT, G, G]), ALU.is_gt))
            step(dve.tensor_tensor(gt8, el.unsqueeze(2).to_broadcast([TP, NT * G, E, E]), el.unsqueeze(3).to_broadcast([TP, NT * G, E, E]), ALU.is_gt))
            exg, exe = sm[:, 0:NT * G], sm[:, NT * G:NT * (G + NE)]
            mxg, mxe = sm[:, 256:256 + NT], sm[:, 264:264 + NT * G]
            step(dve.tensor_reduce(mxg, gl, AX_X, ALU.max))
            step(dve.tensor_reduce(mxe, el, AX_X, ALU.max))
            settle()
            exg3, exe3 = exg.rearrange("p (t g) -> p t g", g=G), exe.rearrange("p (q e) -> p q e", e=E)
            step(dve.tensor_tensor(exg3, gl, mxg.unsqueeze(2).to_broadcast([TP, NT, G]), ALU.subtract))
            dve.tensor_tensor(exe3, el, mxe.unsqueeze(2).to_broadcast([TP, NT * G, E]), ALU.subtract).then_inc(ex_in, 1)
            settle()
            dve.wait_ge(eqt_ready, 2)
            step(dve.tensor_tensor(gt4, gt4, eq4, ALU.add))
            step(dve.tensor_tensor(gt8, gt8, eq8, ALU.add))
            settle()
            rkg, rke = sm[:, 296:296 + NT * G], sm[:, 320:320 + NT * NE]
            step(dve.tensor_reduce(rkg.rearrange("p (t g) -> p t g", g=G), gt4, AX_X, ALU.add))
            step(dve.tensor_reduce(rke.rearrange("p (q e) -> p q e", e=E), gt8, AX_X, ALU.add))
            settle()
            step(dve.tensor_scalar(sm[:, 296:320 + NT * NE], sm[:, 296:320 + NT * NE], 1.5, None, ALU.is_lt))
            settle()
            mskq = msk.rearrange("p t (g e) -> p (t g) e", g=G)
            rke3 = rke.rearrange("p (q e) -> p q e", e=E)
            dve.tensor_tensor(mskq, rke3, rkg.unsqueeze(2).to_broadcast([TP, NT * G, E]), ALU.mult).then_inc(msk_ready, 1)
            dve.wait_ge(ex_out, 1)
            step(dve.tensor_tensor(exg, exg, rkg, ALU.mult))
            step(dve.tensor_tensor(exe, exe, rke, ALU.mult))
            settle()
            smg, sme = sm[:, 520:520 + NT], sm[:, 528:528 + NT * G]
            step(dve.tensor_reduce(smg, exg3, AX_X, ALU.add))
            step(dve.tensor_reduce(sme, exe3, AX_X, ALU.add))
            settle()
            step(dve.reciprocal(smg, smg))
            step(dve.reciprocal(sme, sme))
            settle()
            sme3 = sme.rearrange("p (t g) -> p t g", g=G)
            step(dve.tensor_tensor(exg3, exg3, smg.unsqueeze(2).to_broadcast([TP, NT, G]), ALU.mult))
            settle()
            step(dve.tensor_tensor(sme3, sme3, exg3, ALU.mult))
            settle()
            combq = comb.rearrange("p t (g e) -> p (t g) e", g=G)
            dve.tensor_tensor(combq, exe3, sme.unsqueeze(2).to_broadcast([TP, NT * G, E]), ALU.mult).then_inc(comb_ready, 1)
            dve.wait_ge(msk_ready, 1)
            step(dve.tensor_scalar(posm, msk, 1e6, 1e6, ALU.mult, ALU.subtract))
            dve.wait_ge(cnt_mm, 1)
            settle()
            step(dve.tensor_tensor(posm, PS[0:TP, 5, 0:NT * NE].rearrange("p (t e) -> p t e", t=NT), posm, ALU.add))
            dve.tensor_copy(ov[:, 6], PS[:, 6, 0:NE]).then_inc(cnt_read, 1)
            dve.wait_ge(comb_ready, 1)
            dve.tensor_copy(facts[:, :, :, 3], comb).then_inc(facts_ready, 1)
            dve.wait_ge(facts_ready, 1)
            step(dve.tensor_tensor(rest, comb, facts[:, :, :, 3], ALU.subtract))
            settle()
            dve.tensor_copy(facts[:, :, :, 4], rest).then_inc(facts_ready, 1)
            dve.wait_ge(facts_ready, 2)
            step(dve.tensor_tensor(rest, rest, facts[:, :, :, 4], ALU.subtract))
            settle()
            dve.tensor_copy(facts[:, :, :, 5], rest).then_inc(facts_ready, 1)

            iota = cst[0:TP, CC_IOTA:CC_IOTA + CAP]

            def one_hot(o, pos):
                return dve.tensor_tensor(o, pos.to_broadcast([TP, NT, CAP]), iota.unsqueeze(1).to_broadcast([TP, NT, CAP]), ALU.is_equal)

            def slots(lo, hi, psum_lo, own, base):
                f = PS[:, 7, psum_lo * 8:(psum_lo + hi - lo) * 8].rearrange("p (q r) -> p q r", r=8)
                k = calc[:, lo:hi]
                dve.tensor_copy(k[:, :, 1:4], f[:, :, 1:4]).then_inc(own, 1)
                dve.wait_ge(own, base + 1)
                dve.scalar_tensor_tensor(out=k[:, :, 0:1], in0=f[:, :, 0:1], scalar=32.0, in1=k[:, :, 1:2],
                                         op0=ALU.mult, op1=ALU.add).then_inc(own, 1)
                dve.tensor_tensor(k[:, :, 3:4], f[:, :, 4:5], k[:, :, 3:4], ALU.add).then_inc(own, 1)
                dve.wait_ge(own, base + 3)
                dve.scalar_tensor_tensor(out=k[:, :, 0:1], in0=k[:, :, 2:3], scalar=cst[:, CC_SPARE + 1:CC_SPARE + 2],
                                         in1=k[:, :, 0:1], op0=ALU.mult, op1=ALU.add).then_inc(own, 1)
                dve.tensor_tensor(wgt[:, lo:hi].unsqueeze(2), f[:, :, 5:6], k[:, :, 3:4], ALU.add).then_inc(own, 1)
                dve.wait_ge(own, base + 5)
                return dve.tensor_scalar(idx[:, lo:hi].unsqueeze(2), k[:, :, 0:1], cst[:, CC_SPARE:CC_SPARE + 1], None, ALU.add)

            settle()
            for e in range(RING):
                one_hot(oh[:, e], posm[:, :, e:e + 1]).then_inc(oh_ready, 1)
            dve.wait_ge(idx_mm, 1)
            slots(0, RING - 1, 0, slots_own, 0).then_inc(idx_ready, 1)
            dve.wait_ge(combT_mm, 1)
            dve.tensor_copy(combT.rearrange("p (h n) -> p h n", h=2), PS[0:NE, 0:2, 0:HB]).then_inc(combT_ready, 1)
            dve.wait_ge(b2_mm, 1)
            dve.tensor_tensor(h1[:].rearrange("p (a b) d -> p a b d", b=2), PS[0:TP, 2:5, 0:2 * D].rearrange("p a (b d) -> p a b d", b=2),
                              h2[:].rearrange("p (a b) d -> p a b d", b=2), ALU.add).then_inc(b2_read, 1)
            def token_copy(i, r, first):
                e = i * RING + r
                dve.wait_ge(xgT_mm, e + 1)
                dve.tensor_copy(xgT[:, r % 2], PS[0:HALF_D, 6, 0:2 * CAP].rearrange("p (c n) -> p c n", c=2)).then_inc(xgT_ready, 1)

            def output_copy(i, r, first):
                e = i * RING + r
                dve.wait_ge(w2_done, e + 1)
                if not (first and r < 2):
                    dve.wait_ge(added, (e - 1) * 16)
                dve.tensor_scalar(y_s[:, r % 2], PS[:, 4 + r % 2, 0:D], wgt[:, r:r + 1], None, ALU.mult).then_inc(y_ready, 1)

            def copies(i, first=False, final=False):
                for r in range(RING):
                    e = i * RING + r
                    if r + 1 < RING:
                        token_copy(i, r + 1, first)
                    elif not final:
                        token_copy(i + 1, 0, False)
                    if not final:
                        dve.wait_ge(idx_mm, max(1, e - 1) if first else e - 1)
                        pos = posm[:, :, e + RING:e + RING + 1] if first else posm[:, :, bass.ds(e + RING, 1)]
                        one_hot(oh[:, r], pos).then_inc(oh_ready, 1)
                    if first and r < RING - 1:
                        for q in over_pair(r):
                            over_hot(0, q)
                    output_copy(i, r, first)
                    if first and r == RING - 1:
                        over_slots(0, True)
                    if final and r >= 1:
                        for q in over_pair(r - 1):
                            over_token_copy(0, q)
                    if not (final and r >= 1):
                        q = (r + RING - 1) % RING
                        dve.wait_ge(idx_mm, e + 2)
                        if not (first and r == 0):
                            dve.wait_ge(added, e * 16)
                        slots(q, q + 1, q, slots_own, e * 5 + 5).then_inc(idx_ready, 1)

            def over_hot(i, q):
                e = dve.value_load(eidi[0:1, bass.ds(i * OVER + q, 1)], min_val=0, max_val=NE - 1)
                dve.tensor_scalar(tmp6[:, q].unsqueeze(2), oposm[:, :, bass.ds(e, 1)], cst[0:TP, bass.ds(i * OVER + (CC_JC + q), 1)],
                                  None, ALU.subtract).then_inc(o_from, 1)
                dve.wait_ge(o_from, i * OVER + (q + 1))
                one_hot(ooh[:, q], tmp6[:, q].unsqueeze(2)).then_inc(o_oh, 1)

            def over_slots(i, first):
                dve.wait_ge(o_idx_mm, i + 1)
                if not first:
                    dve.wait_ge(o_added, i * (16 * OVER))
                slots(RING, RING + OVER, RING, o_own, i * 5).then_inc(o_idx, 1)

            def over_token_copy(i, q):
                dve.wait_ge(o_xgT_mm, i * OVER + (q + 1))
                dve.tensor_copy(oxgT[:, q], PS[0:HALF_D, 6 + q % 2, 0:2 * CAP].rearrange("p (c n) -> p c n", c=2)).then_inc(o_xgT, 1)

            def over_outputs(i, first):
                for q in range(OVER):
                    with dve.If(n_over > i * OVER + q):
                        dve.wait_ge(o_w2, i * OVER + (q + 1))
                        if first and q < 2:
                            dve.wait_ge(added, 16 * (NE - 1 + q))
                        else:
                            dve.wait_ge(o_added, i * (16 * OVER) + 16 * (q - 1))
                        dve.tensor_scalar(y_s[:, q % 2], PS[:, 4 + q % 2, 0:D], wgt[:, RING + q:RING + q + 1], None, ALU.mult).then_inc(o_y, 1)

            token_copy(0, 0, True)
            dve.wait_ge(cnt_read, 1)
            cnt = ov[:, 6]
            step(dve.tensor_scalar(ov[:, 0], cnt, float(CAP), None, ALU.is_gt))
            for q in range(2, (N + CAP - 1) // CAP):
                settle()
                step(dve.scalar_tensor_tensor(out=ov[:, 0], in0=cnt, scalar=float(q * CAP), in1=ov[:, 0], op0=ALU.is_gt, op1=ALU.add))
            step(dve.memset(ov[:, 1], 1.0))
            settle()
            step(dve.tensor_tensor_scan(ov[:, 2], ov[:, 1], ov[:, 0], 0.0, ALU.mult, ALU.add))
            settle()
            step(dve.tensor_tensor(ov[:, 3], ov[:, 2], ov[:, 0], ALU.subtract))
            step(dve.tensor_tensor(ofs, ov[:, 2].unsqueeze(1).to_broadcast([128, OVER_PAD, NE]),
                                   cst[:, CC_J:CC_J + OVER_PAD].unsqueeze(2).to_broadcast([128, OVER_PAD, NE]), ALU.is_le))
            settle()
            step(dve.tensor_scalar(ov[:, 4], ov[:, 3], float(CAP), float(CAP), ALU.mult, ALU.subtract))
            step(dve.tensor_reduce(ov[:, 5, 0:OVER_PAD], ofs, AX_X, ALU.add))
            step(dve.tensor_copy(ov[:, 5, OVER_PAD:OVER_PAD + 1], ov[:, 2, NE - 1:NE]))
            settle()
            step(dve.tensor_tensor(oposm, posm, ov[0:TP, 4].unsqueeze(1).to_broadcast([TP, NT, NE]), ALU.add))
            step(dve.tensor_scalar(ov[:, 5, 0:OVER_PAD], ov[:, 5, 0:OVER_PAD], float(NE - 1), None, ALU.min))
            settle()
            dve.tensor_copy(eidi[:], ov[:, 5, 0:OVER_PAD + 1]).then_inc(eid_ready, 1)

            dve.wait_ge(eid_ready, 1)
            n_over = over_count(dve)
            copies(0, first=True)
            with dve.Fori(1, NE // RING - 1) as i:
                copies(i)
            copies(NE // RING - 1, final=True)
            over_outputs(0, True)
            with dve.Fori(1, OVER_ROUNDS) as i:
                with dve.If(n_over > i * OVER):
                    for q in range(OVER):
                        over_hot(i, q)
                    over_slots(i, False)
                    for q in range(OVER):
                        over_token_copy(i, q)
                    over_outputs(i, False)


DEBUG = False


def _layouts(x, gamma, beta, W):
    xp = np.pad(x, ((0, 0), (1, 1), (1, 1), (0, 0)))
    rows = (np.arange(GRID) * PATCH)[:, None] + np.arange(WIN)[None, :]
    p = xp[:, rows][:, :, :, rows]
    p = p.transpose(2, 4, 5, 0, 1, 3).reshape(NKC, KC, N).transpose(1, 0, 2)
    moves = ((0, 0), (0, 1), (0, -1), (1, 0), (-1, 0))

    def place(a):
        a = a.reshape(PATCH, PATCH, NSH, CH, -1)
        o = np.zeros((NSH, WIN, WIN, CH, a.shape[-1]), a.dtype)
        for s, (dy, dx) in enumerate(moves):
            o[s, 1 - dy:1 - dy + PATCH, 1 - dx:1 - dx + PATCH] = a[:, :, s]
        o = o.reshape(NSH, NKC, KC, -1)
        return o.transpose(2, 1, 0, 3)

    cnt = place(np.ones((F, 1), np.float32)).sum(2)[:, :, 0]
    gb = np.concatenate([place(gamma).reshape(KC, -1), place(beta).reshape(KC, -1), cnt], 1)
    return p, place(W), gb


def _constants():
    c = np.zeros((128, CC_N), np.float32)
    c[:, CC_ID:CC_ID + 128] = np.eye(128)
    c[:, CC_HALF:CC_HALF + 128] = 0.5 * np.eye(128)
    c[:TP, CC_TRI:CC_TRI + TP] = np.triu(np.ones((TP, TP)), 1)
    c[:, CC_LT8:CC_LT8 + E * E] = np.tril(np.ones((E, E)), -1).reshape(-1)
    c[:, CC_LT4:CC_LT4 + G * G] = np.tril(np.ones((G, G)), -1).reshape(-1)
    c[:, CC_J:CC_J + OVER_PAD] = np.arange(OVER_PAD)
    c[:, CC_JC:CC_JC + OVER_PAD] = np.arange(OVER_PAD) * CAP
    c[:, CC_IOTA:CC_IOTA + CAP] = np.arange(CAP)
    number = np.arange(NT)[None, :] * TP + np.arange(TP)[:, None]
    c[:TP, CC_TOK:CC_TOK + NT] = number // 32
    c[:TP, CC_TOK + NT:CC_TOK + 2 * NT] = number % 32
    c[:, CC_SPARE] = N + np.arange(128)
    c[:, CC_SPARE + 1] = -c[:, CC_SPARE]
    return c


def kernel(**inputs):
    import numpy as _np
    import concourse.bacc as _bacc
    from concourse import mybir as _mybir
    from concourse.bass_utils import run_bass_kernel_spmd as _run

    v = {k: _np.asarray(a) for k, a in inputs.items()}

    def chunked(a):
        return a.reshape(NJ, 128, -1).transpose(1, 0, 2).reshape(128, -1)

    x_t, w_sh, gb = _layouts(v["x"], v["L0_tok_gamma"], v["L0_tok_beta"], v["L0_tok_W"])
    params = _np.concatenate(
        [chunked(v["L0_attn_" + k]) for k in ("conv_w", "conv_b", "b_dt", "A_log", "Dp", "W_x", "W_out")]
        + [v["L0_ffn_b1"].reshape(NE, NMC, 128).transpose(2, 0, 1).reshape(128, -1)], 1)
    rows = _np.concatenate([v["L0_tok_b"], v["L0_ffn_bg"], v["L0_ffn_bge"].reshape(-1)])[None]
    w_rt = _np.concatenate([v["L0_ffn_Wg"], v["L0_ffn_Wge"].transpose(1, 0, 2).reshape(D, NE)], 1)
    given = {"x_t": x_t, "w_sh": w_sh, "gb": gb, "consts": _constants(), "params": params, "rows": rows,
             "w_in": v["L0_attn_W_in"], "w_dt": v["L0_attn_W_dt"], "w_rt": w_rt,
             "w1": v["L0_ffn_W1"], "w2": v["L0_ffn_W2"], "b2": v["L0_ffn_b2"]}
    nc = _bacc.Bacc("TRN2", target_bir_lowering=False, num_devices=1)
    arrays, args = {}, []
    for name, a in given.items():
        a = _np.ascontiguousarray(a)
        arrays[f"in_{name}"] = a
        args.append(nc.dram_tensor(f"in_{name}", a.shape, _mybir.dt.from_np(a.dtype), kind="ExternalInput").ap())
    o = nc.dram_tensor("out_0", (N + CAP, D), _mybir.dt.float32, kind="ExternalOutput").ap()
    xn = nc.dram_tensor("xn", (N + CAP, D), _mybir.dt.float32).ap()
    dbg = nc.dram_tensor("out_1", (N, D), _mybir.dt.float32, kind="ExternalOutput").ap() if DEBUG else None
    bc = nc.dram_tensor("bc", (2 * NST, N), _mybir.dt.float32).ap()
    build_program(nc, *args, o, xn, bc, dbg)
    r = _run(nc, [arrays], core_ids=[0])
    return r.results[0]["out_0"][:N].reshape(BATCH, L, D)
```

```python
from contextlib import ExitStack

import numpy as np

import concourse.bass as bass
from concourse import mybir

ALU = mybir.AluOpType
ACT = mybir.ActivationFunctionType
F32 = mybir.dt.float32
I32 = mybir.dt.int32
BF16 = mybir.dt.bfloat16
AX_X = mybir.AxisListType.X

BATCH, IMG, CH, PATCH = 16, 96, 3, 16
GRID = IMG // PATCH
L = GRID * GRID
N = BATCH * L
NSH = 5
F = PATCH * PATCH * NSH * CH
WIN = PATCH + 2
KC, NKC = 2 * WIN * CH, WIN // 2
LOADS = ((0, 1), (1, 3), (3, 6), (6, NKC))
WIDE = 3
D = 192
HALF_D = D // 2
DI = 2 * D
NJ = DI // 128
NST = 16
DTR = 12
KS = 4
TP = 96
NT = N // TP
HB = N // 2
G, E = 4, 8
NE = G * E
M = 768
NMC = M // 128
TOPK = 4
CAP = 128
MAX_OVER = (TOPK * N) // (CAP + 1)
LN_EPS = 1e-5
TOK_EPS = 1e-3
LOG_GUARD = float(-np.log(1e-12))

RING = 4
OVER = 6
OVER_ROUNDS = -(-MAX_OVER // OVER)
OVER_PAD = OVER * OVER_ROUNDS
NR = 6

PC_CONVW = 0
PC_CONVB = PC_CONVW + NJ * KS
PC_BDT = PC_CONVB + NJ
PC_ALOG = PC_BDT + NJ
PC_D = PC_ALOG + NJ * NST
PC_WX = PC_D + NJ
XW = DTR + 2 * NST
PC_WOUT = PC_WX + NJ * XW
PC_B1 = PC_WOUT + NJ * D
PC_N = PC_B1 + NE * NMC
CC_ID = 0
CC_HALF = CC_ID + 128
CC_TRI = CC_HALF + 128
CC_RST = CC_TRI + TP
CC_J = CC_RST + NT * (G + NE)
CC_JC = CC_J + OVER_PAD
CC_IOTA = CC_JC + OVER_PAD
CC_TOK = CC_IOTA + CAP
CC_SPARE = CC_TOK + 2 * NT
CC_N = CC_SPARE + 2
GC_G, GC_B, GC_CNT = 0, NKC * NSH, 2 * NKC * NSH
GC_ROOT = GC_CNT + NKC
GC_N = GC_ROOT + NKC

NG = 2
NGRP = NST // NG
STEPS = NGRP * NJ
PD = 864


def build_program(nc, x_t, w_sh, gb, consts, params, rows, w_in, w_dt, w_rt, w1, w2, b2, out, xn, bc):
    w1_v = w1.rearrange("e (c p) m -> e p c m", c=2)
    w2_v = w2.rearrange("e (c p) d -> e p c d", p=128)
    out_v = out[0:N].rearrange("(t p) d -> p t d", p=TP)

    with ExitStack() as ctx:
        def sb(name, shape, dt=F32):
            return ctx.enter_context(nc.sbuf_tensor(name, shape, dt))

        def sem(name):
            return ctx.enter_context(nc.semaphore(name))

        PS = ctx.enter_context(nc.psum_tensor("PS", [128, 8, 512], F32))
        PSF = PS[:].rearrange("p b c -> p (b c)")

        cst = sb("cst", [128, CC_N])
        par = sb("par", [128, PC_N])
        gbs = sb("gbs", [KC, GC_N])
        rws = sb("rws", [1, D])
        win_s = sb("win_s", [HALF_D, 2, 2 * DI])
        wdt_s = sb("wdt_s", [DTR, DI])
        wrt_s = sb("wrt_s", [HALF_D, 2, G + NE])
        b2_s = sb("b2_s", [NE, D])
        ones = sb("ones", [128, 128])
        st = sb("st", [TP, 128])
        h1 = sb("h1", [TP, NT, D])
        h2 = sb("h2", [TP, NT, D])
        un = sb("un", [TP, NT, D])
        unT = sb("unT", [HALF_D, 2, N])
        ringw1 = sb("ringw1", [HALF_D, RING, 2, M])
        ringw2 = sb("ringw2", [128, RING, NMC, D])

        WORK = 29100
        work = sb("work", [128, WORK])
        at = [0]

        def region(shape, parts=128):
            n = int(np.prod(shape))
            v = work[0:parts, at[0]:at[0] + n]
            at[0] += n
            assert at[0] <= WORK, at[0]
            if len(shape) == 1:
                return v
            names = "abcd"[:len(shape)]
            return v.rearrange("p (" + " ".join(names) + ") -> p " + " ".join(names),
                               **{k: s for k, s in zip(names[1:], shape[1:])})

        x_s = region([NKC, N], KC)
        wsh_s = region([NKC, NSH, D], KC)
        xsq = region([NKC, N], KC)
        weff = region([NKC, D + 1], KC)
        u = region([NT, D], TP)
        gcol = region([D], TP)
        bb_s = region([D], TP)
        bsum = region([WIDE, D], KC)
        bprod = region([NSH, WIDE, D], KC)
        at[0] = 0
        xc = region([NJ, N])
        xi = region([NJ, N])
        sres = region([NJ, N])
        delta = region([NJ, N])
        dx = region([NJ, N])
        skip = region([NJ, N])
        rsum = region([NJ, N + 1])
        xdbl = region([N], XW)
        av = region([3, NJ * NST])
        guard = region([1])
        a_s = region([2, NG, BATCH, L])
        th_s = region([2, NG, N])
        t1_s = region([2, NG, N])
        w_s = region([2, NG, N])
        p_s = region([2, NG, N])
        bb_n = region([2, NG, N])
        cc_n = region([2, NG, N])
        mask = p_s[:, 0, 0]
        sp_en = th_s.rearrange("p a b c -> p (a b c)")[:, 0:NJ * N].rearrange("p (j n) -> p j n", j=NJ)
        sp_ln = xc
        at[0] = 0
        rl = region([NT, G + NE], TP)
        rl2 = region([NT, G + NE], TP)
        top = region([2, NT, G + NE], TP)
        tie = region([NT, G + NE], TP)
        ex = region([NT, G + NE], TP)
        mx = region([2, NT * (1 + G)], TP)
        sums = region([NT * (1 + G)], TP)
        comb = region([NT, NE], TP)
        posm = region([NT, NE], TP)
        oposm = region([NT, NE], TP)
        rest = region([NT, NE], TP)
        combT = region([N], NE)
        ov = region([7, NE])
        ofs = region([OVER_PAD, NE])
        opos = region([OVER, NT], TP)
        calc = region([RING + OVER, 4])
        xg = region([RING, D])
        xgT = region([2, 2, CAP], HALF_D)
        hT = region([2, NMC, CAP])
        y_s = region([2, D])
        oh = region([RING, NT * CAP // 2], TP).rearrange("p r c -> p (r c)").bitcast(BF16).rearrange("p (r t c) -> p r t c", r=RING, t=NT)
        oxg = region([OVER, D])
        oxgT = region([OVER, 2, CAP], HALF_D)
        ooh = region([OVER, NT * CAP // 2], TP).rearrange("p r c -> p (r c)").bitcast(BF16).rearrange("p (r t c) -> p r t c", r=OVER, t=NT)
        facts = sb("facts", [TP, NT, NE, NR], BF16)
        idx = sb("idx", [128, RING + OVER], I32)
        wgt = sb("wgt", [128, RING + OVER])
        eidi = sb("eidi", [128, OVER_PAD + 1], I32)
        zero_s = sb("zero_s", [128, D])
        msk = sb("msk", [TP, NT, NE], BF16)
        ones_b = sb("ones_b", [TP, 128], BF16)
        tri_b = sb("tri_b", [TP, TP], BF16)
        warm = sb("warm", [1, 1])
        rbias = sb("rbias", [TP, G + NE])

        ident = cst[:, CC_ID:CC_ID + 128]
        half_ident = cst[:, CC_HALF:CC_HALF + 128]
        tri = cst[0:TP, CC_TRI:CC_TRI + TP]

        ld_gb, ld_cst, ld_par, ld_small, ld_rows = sem("ld_gb"), sem("ld_cst"), sem("ld_par"), sem("ld_small"), sem("ld_rows")
        ld_w = [sem(f"ld_w{g}") for g in range(len(LOADS))]
        ld_x = [sem(f"ld_x{g}") for g in range(len(LOADS))]
        ld_ring = [sem(f"ld_ring{r}") for r in range(RING)]
        ld_xg = [sem(f"ld_xg{r}") for r in range(RING)]
        spare_zero, xn_stored, out_init = sem("spare_zero"), sem("xn_stored"), sem("out_init")
        dve_own, warm_done, pool_own = sem("dve_own"), sem("warm_done"), sem("pool_own")
        ones_ready, weff_ready, cnt_ready, sq_ready = sem("ones_ready"), sem("weff_ready"), sem("cnt_ready"), sem("sq_ready")
        bprod_ready, bsum_ready, sq_sum, tok_mm, g_mm, sq_mm = sem("bprod_ready"), sem("bsum_ready"), sem("sq_sum"), sem("tok_mm"), sem("g_mm"), sem("sq_mm")
        var_ready, rstd_ready = sem("var_ready"), sem("rstd_ready")
        h_ready = sem("h_ready")
        un_ready, unT_mm, unT_low, unT_high = sem("un_ready"), sem("unT_mm"), sem("unT_low"), sem("unT_high")
        win_mm, conv_done, gate_ready, tap_ready, xi_ready = sem("win_mm"), sem("conv_done"), sem("gate_ready"), sem("tap_ready"), sem("xi_ready")
        xdbl_mm, xdbl_ready, dl_mm, dl_read_act, dl_read_dve = (sem("xdbl_mm"), sem("xdbl_ready"), sem("dl_mm"), sem("dl_read_act"), sem("dl_read_dve"))
        en_ready, ln_ready, corr_ready, spq_ready = sem("en_ready"), sem("ln_ready"), sem("corr_ready"), sem("spq_ready")
        delta_ready, rsum_ready, dx_ready, aexp_ready, av_ready = (sem("delta_ready"), sem("rsum_ready"), sem("dx_ready"), sem("aexp_ready"), sem("av_ready"))
        azero_ready = sem("azero_ready")
        bc_stored = sem("bc_stored")
        b_ready, c_ready = [[sem(f"{n}_ready{k}") for k in range(2)] for n in "bc"]
        a_ready, t1_ready, scan_done, wg_ready, p_dve, p_pool, p_used = (sem("a_ready"), sem("t1_ready"), sem("scan_done"), sem("wg_ready"), sem("p_dve"), sem("p_pool"), sem("p_used"))
        skip_ready, y2_ready, wout_mm, h2_ready = sem("skip_ready"), sem("y2_ready"), sem("wout_mm"), sem("h2_ready")
        rt_mm, ex_in, ex_out = sem("rt_mm"), sem("ex_in"), sem("ex_out")
        tri_ready = sem("tri_ready")
        msk_ready, cnt_mm, comb_ready, combT_mm, combT_ready, b2_mm, b2_read = (sem("msk_ready"), sem("cnt_mm"), sem("comb_ready"), sem("combT_mm"), sem("combT_ready"), sem("b2_mm"), sem("b2_read"))
        numbers_ready, facts_ready, eid_ready = sem("numbers_ready"), sem("facts_ready"), sem("eid_ready")
        oh_ready, idx_mm, idx_ready, slots_own = sem("oh_ready"), sem("idx_mm"), sem("idx_ready"), sem("slots_own")
        cnt_read, pool_turns = sem("cnt_read"), sem("pool_turns")
        xgT_mm, xgT_ready, h_mm, gelu_done, w2_done, y_ready = (sem("xgT_mm"), sem("xgT_ready"), sem("h_mm"), sem("gelu_done"), sem("w2_done"), sem("y_ready"))
        added = sem("added")
        o_oh, o_idx_mm, o_idx, o_xgT_mm, o_xgT, o_h_mm, o_gelu, o_w2, o_y, o_added, o_from, o_own = [
            sem("o_" + n) for n in ("oh", "idx_mm", "idx", "xgT_mm", "xgT", "h_mm", "gelu", "w2", "y", "added", "from", "own")]
        o_ld_ring = [sem(f"o_ld_ring{r}") for r in range(RING)]
        o_ld_xg = [sem(f"o_ld_xg{q}") for q in range(OVER)]

        def follower(engine, own):
            count = [0]

            def step(ins):
                count[0] += 1
                return ins.then_inc(own, 1)

            def settle():
                engine.wait_ge(own, count[0])

            return step, settle

        def wait_product(engine, s):
            engine.wait_ge(p_dve, s + 1)
            engine.wait_ge(p_pool, s + 1)

        def product(engine, s, lo, hi, done):
            g, k = s // NJ, s % 2
            engine.wait_ge(wg_ready, s + 1)
            engine.wait_ge(c_ready[g % 2], 16 * (g // 2 + 1))
            if s >= 2:
                engine.wait_ge(p_used, s - 1)
            flat = [v.rearrange("p n l -> p (n l)")[:, lo:hi] for v in (p_s[:, k], w_s[:, k], cc_n[:, g % 2])]
            engine.tensor_tensor(*flat, ALU.mult).then_inc(done, 1)

        def over_pair(r):
            return range(r * OVER // (RING - 1), (r + 1) * OVER // (RING - 1))

        def over_half(h):
            return range(h * OVER // 2, (h + 1) * OVER // 2)

        def over_count(engine):
            return engine.value_load(eidi[0:1, OVER_PAD:OVER_PAD + 1], min_val=0, max_val=MAX_OVER)

        WIN_BANK = (4, 6, 0)
        DL_BANK = (4, 6, 2)

        block = ctx.enter_context(nc.Block())

        @block.sync
        def _(sp):
            sp.dma_start(gbs[:], gb).then_inc(ld_gb, 16)
            for g, (lo, hi) in enumerate(LOADS):
                sp.dma_start(wsh_s[:, lo:hi], w_sh[:, lo:hi]).then_inc(ld_w[g], 16)
                sp.dma_start(x_s[:, lo:hi], x_t[:, lo:hi]).then_inc(ld_x[g], 16)
                if g == 1:
                    sp.dma_start(rws[:], rows[:, 0:D]).then_inc(ld_rows, 16)
            sp.dma_start(cst[:], consts).then_inc(ld_cst, 16)
            sp.dma_start(par[:], params).then_inc(ld_par, 16)
            sp.dma_start(win_s[:], w_in.rearrange("(c p) n -> p c n", c=2)).then_inc(ld_small, 16)
            sp.dma_start(wdt_s[:], w_dt).then_inc(ld_small, 16)
            sp.dma_start(wrt_s[:], w_rt.rearrange("(c p) n -> p c n", c=2)).then_inc(ld_small, 16)
            sp.dma_start(b2_s[:], b2).then_inc(ld_small, 16)
            sp.dma_start(rbias[:], rows[:, D:].to_broadcast([TP, G + NE])).then_inc(ld_small, 16)
            for r in range(RING):
                sp.dma_start(ringw1[:, r], w1_v[r]).then_inc(ld_ring[r], 16)
                sp.dma_start(ringw2[:, r], w2_v[r]).then_inc(ld_ring[r], 16)
            sp.wait_ge(ones_ready, 2)
            sp.dma_start(xn[N:N + CAP], zero_s[:]).then_inc(spare_zero, 16)
            sp.dma_start(out[N:N + CAP], zero_s[:]).then_inc(spare_zero, 16)
            sp.wait_ge(xdbl_ready, 1)
            sp.dma_start(bc, xdbl[DTR:XW, :]).then_inc(bc_stored, 16)
            sp.wait_ge(bc_stored, 16)
            for g in range(NGRP):
                if g >= 2:
                    sp.wait_ge(t1_ready, NJ * (g - 1))
                sp.dma_start(bb_n[:, g % 2], bc[g * NG:(g + 1) * NG, :].unsqueeze(0).to_broadcast([128, NG, N])).then_inc(b_ready[g % 2], 16)
                if g >= 2:
                    wait_product(sp, NJ * (g - 1) - 1)
                sp.dma_start(cc_n[:, g % 2], bc[NST + g * NG:NST + (g + 1) * NG, :].unsqueeze(0).to_broadcast([128, NG, N])).then_inc(c_ready[g % 2], 16)

            sp.wait_ge(un_ready, 2 * NT)
            sp.dma_start(xn[0:N].rearrange("(t p) d -> p t d", p=TP), un[:]).then_inc(xn_stored, 16)
            sp.wait_ge(b2_read, 1)
            sp.dma_start(out_v, h1[:]).then_inc(out_init, 16)
            with sp.Fori(0, NE // RING - 1) as i:
                for r in range(RING):
                    e = i * RING + (RING + r)
                    sp.wait_ge(w2_done, i * RING + (r + 1))
                    sp.dma_start(ringw1[:, r], w1_v[bass.ds(e, 1)].rearrange("a p c m -> p (a c) m")).then_inc(ld_ring[r], 16)
                    sp.dma_start(ringw2[:, r], w2_v[bass.ds(e, 1)].rearrange("a p c d -> p (a c) d")).then_inc(ld_ring[r], 16)
            sp.wait_ge(eid_ready, 1)
            n_over = over_count(sp)

            def over_weights(i, q, first):
                with sp.If(n_over > i * OVER + q):
                    e = sp.value_load(eidi[0:1, bass.ds(i * OVER + q, 1)], min_val=0, max_val=NE - 1)
                    if first and q < RING:
                        sp.wait_ge(w2_done, NE - RING + 1 + q)
                    elif q >= RING:
                        sp.wait_ge(o_w2, i * OVER + (q - RING + 1))
                    else:
                        before = q + RING if q + RING < OVER else q
                        sp.wait_ge(o_w2, i * OVER + (before + 1 - OVER))
                    r = q % RING
                    sp.dma_start(ringw1[:, r], w1_v[bass.ds(e, 1)].rearrange("a p c m -> p (a c) m")).then_inc(o_ld_ring[r], 16)
                    sp.dma_start(ringw2[:, r], w2_v[bass.ds(e, 1)].rearrange("a p c d -> p (a c) d")).then_inc(o_ld_ring[r], 16)

            for q in range(OVER):
                over_weights(0, q, True)
            with sp.Fori(1, OVER_ROUNDS) as i:
                with sp.If(n_over > i * OVER):
                    for q in range(OVER):
                        over_weights(i, q, False)
            sp.wait_ge(spare_zero, 32)
            sp.wait_ge(added, 16 * NE)

        @block.tensor
        def _(pe):
            def mm(o, a, b, start=True, stop=True, **k):
                return pe.matmul(o, a, b, start=start, stop=stop, **k)

            pe.wait_ge(cnt_ready, 1)
            pe.wait_ge(ones_ready, 1)

            def token_mm(c, t):
                return mm(PS[0:TP, t, 0:D + 1], x_s[:, c, t * TP:(t + 1) * TP], weff[:, c], c == 0, c == NKC - 1)

            for g, (lo, hi) in enumerate(LOADS):
                for c in range(lo, hi):
                    pe.wait_ge(weff_ready, c + 1)
                    last = mm(PS[0:TP, 6, 0:D], ones[0:KC, 0:TP], weff[:, c, 0:D], c == 0, c == NKC - 1)
                if hi == NKC:
                    last.then_inc(g_mm, 1)
                pe.wait_ge(ld_x[g], 16)
                if hi < NKC:
                    for c in range(lo, hi):
                        for t in range(NT):
                            token_mm(c, t)
            for t in range(NT):
                for c in range(lo, hi):
                    last = token_mm(c, t)
                last.then_inc(tok_mm, 1)
            pe.wait_ge(bsum_ready, len(LOADS) * NSH)
            for k in range(WIDE):
                mm(PS[0:TP, 7, 0:D], ones[0:KC, 0:TP], bsum[:, k], k == 0, False)
            pe.wait_ge(ld_rows, 16)
            mm(PS[0:TP, 7, 0:D], ones[0:1, 0:TP], rws[0:1, 0:D], False, True)
            pe.wait_ge(sq_sum, NKC - 1)
            for t in range(NT):
                last = mm(PS[0:TP, 7, D + t:D + t + 1], xsq[:, 0, t * TP:(t + 1) * TP], ones[0:KC, 0:1])
            last.then_inc(sq_mm, 1)

            def transposes(done):
                pe.wait_ge(ld_cst, 16)
                for t in range(NT):
                    pe.wait_ge(un_ready, done * NT + t + 1)
                    for c in range(2):
                        last = pe.transpose(PS[0:HALF_D, 2 * c + t // 3, (t % 3) * TP:(t % 3 + 1) * TP],
                                            un[:, t, c * HALF_D:(c + 1) * HALF_D], ident[0:TP, 0:TP])
                    if t % 3 == 2:
                        last.then_inc(unT_mm, 1)

            pe.wait_ge(h_ready, NT)
            transposes(0)
            pe.wait_ge(ld_small, 16 * 5)
            pe.wait_ge(ld_par, 16)

            def w_in(j):
                if j >= NJ:
                    pe.wait_ge(conv_done, j - NJ + 1)
                for hf in range(2):
                    if j == 0:
                        pe.wait_ge(unT_low, hf + 1)
                        pe.wait_ge(unT_high, hf + 1)
                    for c in range(2):
                        last = mm(PS[:, WIN_BANK[j % NJ] + hf, 0:HB], win_s[:, c, j * 128:(j + 1) * 128],
                                  unT[:, c, hf * HB:(hf + 1) * HB], c == 0, c == 1)
                last.then_inc(win_mm, 1)

            def w_x(j):
                pe.wait_ge(xi_ready, j + 1)
                for hf in range(2):
                    last = mm(PS[0:XW, 2 + hf, 0:HB], par[:, PC_WX + j * XW:PC_WX + (j + 1) * XW],
                              xi[:, j, hf * HB:(hf + 1) * HB], j == 0, j == NJ - 1, skip_group_check=True)
                return last

            for j in range(NJ + 1):
                w_in(j)
            w_x(0)
            w_in(NJ + 1)
            w_x(1)
            w_x(2).then_inc(xdbl_mm, 1)
            w_in(NJ + 2)
            pe.wait_ge(xdbl_ready, 1)
            for j in range(NJ):
                if j < NJ - 1:
                    pe.wait_ge(gate_ready, j + 1)
                for hf in range(2):
                    last = mm(PS[:, DL_BANK[j] + hf, 0:HB], wdt_s[:, j * 128:(j + 1) * 128], xdbl[0:DTR, hf * HB:(hf + 1) * HB])
                last.then_inc(dl_mm, 1)

            pe.wait_ge(gate_ready, NJ)
            pe.wait_ge(dl_read_act, NJ)
            pe.wait_ge(dl_read_dve, NJ)
            pe.wait_ge(skip_ready, NJ)

            def w_out(src, j, t, start, stop):
                return mm(PS[0:TP, t // 2, (t % 2) * D:(t % 2 + 1) * D], src[:, j, t * TP:(t + 1) * TP],
                          par[:, PC_WOUT + j * D:PC_WOUT + (j + 1) * D], start, stop, skip_group_check=True)

            for t in range(NT):
                for j in range(NJ):
                    w_out(skip, j, t, j == 0 and t % 2 == 0, False)
            for s in range(STEPS):
                g, j, k = s // NJ, s % NJ, s % 2
                wait_product(pe, s)
                for n in range(NG):
                    lo = j * N
                    while lo < (j + 1) * N:
                        hi = min((j + 1) * N, (lo // 512 + 1) * 512)
                        first = s < NJ and n == 0 and lo % 512 == 0
                        last = mm(PSF[:, 4 * 512 + lo:4 * 512 + hi], half_ident, p_s[:, k, n, lo - j * N:hi - j * N],
                                  first, s >= STEPS - NJ and n == NG - 1, skip_group_check=True)
                        lo = hi
                last.then_inc(p_used, 1)
            for j in range(NJ):
                pe.wait_ge(y2_ready, j + 1)
                for t in range(NT):
                    last = w_out(dx, j, t, False, j == NJ - 1)
                    if j == NJ - 1 and t % 2 == 1:
                        last.then_inc(wout_mm, 1)
            pe.wait_ge(h2_ready, NT)
            transposes(1)
            for t in range(NT):
                pe.wait_ge(unT_low, 2 + t // 3 + 1)
                pe.wait_ge(unT_high, 2 + t // 3 + 1)
                o = PS[0:TP, 4, t * (G + NE):(t + 1) * (G + NE)]
                for c in range(2):
                    last = mm(o, unT[:, c, t * TP:(t + 1) * TP], wrt_s[:, c], c == 0, c == 1)
            last.then_inc(rt_mm, 1)
            pe.wait_ge(msk_ready, 1)
            pe.wait_ge(tri_ready, 2)
            for k in range(1, NT + 1):
                mm(PS[:, 5, k * NE:(NT + 1) * NE], ones_b[:], msk[:, 0:NT + 1 - k].rearrange("p t e -> p (t e)"), k == 1, False,
                   skip_group_check=True)
            mm(PS[0:TP, 5, 0:NT * NE], tri_b[:], msk[:].rearrange("p t e -> p (t e)"), False, True,
               skip_group_check=True).then_inc(cnt_mm, 1)

            pe.wait_ge(comb_ready, 1)
            for t in range(NT):
                last = pe.transpose(PS[0:NE, t // 3, (t % 3) * TP:(t % 3 + 1) * TP], comb[:, t], ident[0:TP, 0:TP])
            last.then_inc(combT_mm, 1)

            def combine_bias(tiles):
                for t in tiles:
                    last = mm(PS[0:TP, 2 + t // 2, (t % 2) * D:(t % 2 + 1) * D], combT[:, t * TP:(t + 1) * TP], b2_s[:])
                if tiles[-1] == NT - 1:
                    last.then_inc(b2_mm, 1)

            def facts_of(hot, q, e):
                for t in range(NT):
                    last = mm(PS[:, 7, q * 8:q * 8 + NR], hot[:, t], facts[:, t, e].rearrange("p a r -> p (a r)"),
                              t == 0, t == NT - 1)
                return last

            def next_facts(i, r, first):
                e = i * RING + r
                q = (r + RING - 1) % RING
                pe.wait_ge(oh_ready, e + RING)
                pe.wait_ge(idx_ready, e + (RING - 1))
                if first and r >= 1:
                    over_facts(0, over_pair(r - 1))
                facts_of(oh[:, q], q, bass.ds(e + (RING - 1), 1)).then_inc(idx_mm, 1)

            def hidden(i, r, first):
                e = i * RING + r
                pe.wait_ge(xgT_ready, e + 1)
                pe.wait_ge(ld_ring[r], i * 32 + 32)
                for m in range(NMC):
                    if not (first and r * NMC + m < 4):
                        pe.wait_ge(gelu_done, e * NMC + (m - 3))
                    for c in range(2):
                        last = mm(PS[:, (r * NMC + m) % 4, 0:CAP], ringw1[:, r, c, m * 128:(m + 1) * 128],
                                  xgT[:, r % 2, c], c == 0, c == 1)
                    last.then_inc(h_mm, 1)

            def tokens(i, r):
                pe.wait_ge(ld_xg[r], i * 16 + 16)
                for c in range(2):
                    last = pe.transpose(PS[0:HALF_D, 6, c * CAP:(c + 1) * CAP], xg[:, r, c * HALF_D:(c + 1) * HALF_D], ident)
                last.then_inc(xgT_mm, 1)

            def output(i, r, first):
                e = i * RING + r
                if not (first and r < 2):
                    pe.wait_ge(y_ready, e - 1)
                for m in range(NMC):
                    pe.wait_ge(gelu_done, e * NMC + (m + 1))
                    last = mm(PS[:, 4 + r % 2, 0:D], hT[:, r % 2, m], ringw2[:, r, m], m == 0, m == NMC - 1)
                last.then_inc(w2_done, 1)

            def experts(i, first=False, final=False):
                for r in range(RING):
                    hidden(i, r, first)
                    if r + 1 < RING:
                        tokens(i, r + 1)
                    elif not final:
                        tokens(i + 1, 0)
                    if not (final and r >= 1):
                        next_facts(i, r, first)
                    output(i, r, first)
                    if first and r < RING - 1:
                        if r == 0:
                            pe.wait_ge(eid_ready, 1)
                        for q in over_pair(r):
                            over_expert(0, q)
                    if final and r >= 2:
                        for q in over_half(r - 2):
                            over_tokens(0, q, True)

            experts_of = {}

            def over_expert(i, q):
                experts_of[q] = pe.value_load(eidi[0:1, bass.ds(i * OVER + q, 1)], min_val=0, max_val=NE - 1)

            def over_facts(i, tiles):
                pe.wait_ge(o_oh, i * OVER + (tiles[-1] + 1))
                for q in tiles:
                    last = facts_of(ooh[:, q], RING + q, bass.ds(experts_of[q], 1))
                if tiles[-1] == OVER - 1:
                    last.then_inc(o_idx_mm, 1)

            def over_tokens(i, q, first):
                pe.wait_ge(o_ld_xg[q], i * 16 + 16)
                if q >= 2:
                    pe.wait_ge(o_xgT, i * OVER + (q - 1))
                elif first and q == 0:
                    pe.wait_ge(xgT_ready, NE)
                elif first:
                    pe.wait_ge(idx_ready, NE)
                elif q == 1:
                    pe.wait_ge(o_idx, i + 1)
                for c in range(2):
                    last = pe.transpose(PS[0:HALF_D, 6 + q % 2, c * CAP:(c + 1) * CAP], oxg[:, q, c * HALF_D:(c + 1) * HALF_D], ident)
                last.then_inc(o_xgT_mm, 1)

            def over_tile(i, q, first):
                r = q % RING
                uses = 2 if r + RING < OVER else 1
                with pe.If(n_over > i * OVER + q):
                    pe.wait_ge(o_xgT, i * OVER + (q + 1))
                    pe.wait_ge(o_ld_ring[r], i * (32 * uses) + (64 if q >= RING else 32))
                    for m in range(NMC):
                        c4 = q * NMC + m
                        if not first or c4 >= 4:
                            pe.wait_ge(o_gelu, i * (OVER * NMC) + (c4 - 3))
                        elif c4 == 0:
                            pe.wait_ge(gelu_done, NE * NMC)
                        for c in range(2):
                            last = mm(PS[:, c4 % 4, 0:CAP], ringw1[:, r, c, m * 128:(m + 1) * 128], oxgT[:, q, c], c == 0, c == 1)
                        last.then_inc(o_h_mm, 1)
                    if first and q < 2:
                        pe.wait_ge(y_ready, NE)
                    else:
                        pe.wait_ge(o_y, i * OVER + (q - 1))
                    for m in range(NMC):
                        pe.wait_ge(o_gelu, i * (OVER * NMC) + (q * NMC + m + 1))
                        last = mm(PS[:, 4 + q % 2, 0:D], hT[:, q % 2, m], ringw2[:, r, m], m == 0, m == NMC - 1)
                    last.then_inc(o_w2, 1)

            pe.wait_ge(facts_ready, 3)
            pe.wait_ge(numbers_ready, 3)
            for e in range(RING - 1):
                if e == 0:
                    pe.wait_ge(combT_ready, 1)
                combine_bias(range(2 * e, 2 * e + 2))
                pe.wait_ge(oh_ready, e + 1)
                if e >= 1:
                    pe.wait_ge(idx_ready, e)
                facts_of(oh[:, e], e, slice(e, e + 1)).then_inc(idx_mm, 1)
            tokens(0, 0)
            pe.wait_ge(b2_read, 1)
            pe.wait_ge(cnt_read, 1)
            experts(0, first=True)
            n_over = over_count(pe)
            with pe.Fori(1, NE // RING - 1) as i:
                experts(i)
            experts(NE // RING - 1, final=True)
            for q in range(OVER):
                over_tile(0, q, True)
            with pe.Fori(1, OVER_ROUNDS) as i:
                with pe.If(n_over > i * OVER):
                    for q in range(OVER):
                        over_expert(i, q)
                    over_facts(i, range(OVER))
                    for q in range(OVER):
                        over_tokens(i, q, False)
                    for q in range(OVER):
                        over_tile(i, q, False)

        @block.scalar
        def _(act):
            act.wait_ge(ld_gb, 16)
            for g, (lo, hi) in enumerate(LOADS):
                act.wait_ge(ld_w[g], 16)
                for s in range(NSH):
                    if g >= 1:
                        act.wait_ge(bsum_ready, (g - 1) * NSH + s + 1)
                    for c in range(lo, hi):
                        k = GC_B + c * NSH + s
                        last = act.activation(bprod[:, s, c - lo], wsh_s[:, c, s], ACT.Identity, scale=gbs[:, k:k + 1])
                    last.then_inc(bprod_ready, 1)
                act.wait_ge(ld_x[g], 16)
                for c in range(lo, hi):
                    act.activation(xsq[:, c], x_s[:, c], ACT.Square, scale=gbs[:, GC_ROOT + c:GC_ROOT + c + 1]).then_inc(sq_ready, 1)
            act.wait_ge(ones_ready, 1)
            act.activation(warm[:], ones[0:1, 0:1], ACT.Silu).then_inc(warm_done, 1)

            def transposed(k):
                for h in range(2):
                    act.wait_ge(unT_mm, 2 * k + h + 1)
                    act.copy(unT[:, 0, h * HB:(h + 1) * HB], PS[0:HALF_D, h, 0:HB]).then_inc(unT_low, 1)

            transposed(0)

            def first_tap(j):
                act.wait_ge(win_mm, j + 1)
                k = PC_CONVW + j * KS + KS - 1
                act.activation(xc[:, j].rearrange("p (h n) -> p h n", h=2), PS[:, WIN_BANK[j]:WIN_BANK[j] + 2, 0:HB], ACT.Identity,
                               bias=par[:, PC_CONVB + j:PC_CONVB + j + 1], scale=par[:, k:k + 1]).then_inc(tap_ready, 1)

            def convolved(j):
                act.wait_ge(conv_done, j + 1)
                act.activation(xi[:, j], xc[:, j], ACT.Silu).then_inc(xi_ready, 1)

            def gate(j):
                act.wait_ge(win_mm, NJ + j + 1)
                act.activation(sres[:, j].rearrange("p (h n) -> p h n", h=2), PS[:, WIN_BANK[j]:WIN_BANK[j] + 2, 0:HB],
                               ACT.Silu).then_inc(gate_ready, 1)

            act.wait_ge(ld_par, 16)
            first_tap(0)
            first_tap(1)
            first_tap(2)
            convolved(0)
            gate(0)
            convolved(1)
            convolved(2)
            gate(1)
            gate(2)

            def exp_a_log(lo, hi):
                act.activation(av[:, 0, lo * NST:hi * NST], par[:, PC_ALOG + lo * NST:PC_ALOG + hi * NST], ACT.Exp).then_inc(aexp_ready, 1)

            exp_a_log(0, 1)
            for j in range(NJ):
                act.wait_ge(dl_mm, j + 1)
                act.activation(sp_en[:, j].rearrange("p (h n) -> p h n", h=2), PS[:, DL_BANK[j]:DL_BANK[j] + 2, 0:HB], ACT.Abs,
                               bias=par[:, PC_BDT + j:PC_BDT + j + 1]).then_inc(dl_read_act, 1)
            for j in range(NJ):
                act.wait_ge(dl_read_act, j + 1)
                act.activation(sp_en[:, j], sp_en[:, j], ACT.Exp, scale=-1.0).then_inc(en_ready, 1)
            for j in range(NJ):
                act.wait_ge(en_ready, j + 1)
                act.activation(sp_ln[:, j], sp_en[:, j], ACT.Ln, bias=1.0).then_inc(ln_ready, 1)
            exp_a_log(1, NJ)
            act.wait_ge(av_ready, 2)
            act.wait_ge(azero_ready, 2)
            act.wait_ge(ln_ready, NJ)
            act.wait_ge(corr_ready, NJ)
            act.wait_ge(spq_ready, NJ)

            s_view = rsum[:, :, 1:N + 1]
            d_view = delta.rearrange("p j (b l) -> p j b l", l=L)
            for s in range(STEPS):
                g, j, k = s // NJ, s % NJ, s % 2
                if s >= 2:
                    act.wait_ge(wg_ready, s - 1)
                if s == 1:
                    act.wait_ge(av_ready, 4)
                if s < NJ:
                    act.wait_ge(delta_ready, s + 1)
                    act.wait_ge(rsum_ready, s + 1)
                for n in range(NG):
                    q = j * NST + g * NG + n
                    act.activation(a_s[:, k, n, :, 1:L], d_view[:, j, :, 1:L], ACT.Exp, scale=av[:, 1, q:q + 1])
                    last = act.activation(th_s[:, k, n], s_view[:, j], ACT.Tanh, scale=av[:, 2, q:q + 1], bias=guard[:])
                last.then_inc(a_ready, 1)
            transposed(1)
            act.wait_ge(ex_in, 2)
            act.activation(ex, ex, ACT.Exp).then_inc(ex_out, 1)

            act.wait_ge(combT_mm, 1)
            act.copy(combT.rearrange("p (h n) -> p h n", h=2), PS[0:NE, 0:2, 0:HB]).then_inc(combT_ready, 1)

            def gelus(i, first):
                for r in range(RING):
                    e = i * RING + r
                    if not (first and r < 2):
                        act.wait_ge(w2_done, e - 1)
                    for m in range(NMC):
                        act.wait_ge(h_mm, e * NMC + (m + 1))
                        col = e * NMC + (PC_B1 + m)
                        act.activation(hT[:, r % 2, m], PS[:, (r * NMC + m) % 4, 0:CAP], ACT.Gelu,
                                       bias=par[:, bass.ds(col, 1)]).then_inc(gelu_done, 1)

            gelus(0, True)
            act.wait_ge(eid_ready, 1)
            n_over = over_count(act)
            with act.Fori(1, NE // RING) as i:
                gelus(i, False)

            def over_gelus(i, q, first):
                with act.If(n_over > i * OVER + q):
                    e = act.value_load(eidi[0:1, bass.ds(i * OVER + q, 1)], min_val=0, max_val=NE - 1)
                    if first and q < 2:
                        act.wait_ge(w2_done, NE - 1 + q)
                    else:
                        act.wait_ge(o_w2, i * OVER + (q - 1))
                    for m in range(NMC):
                        act.wait_ge(o_h_mm, i * (OVER * NMC) + (q * NMC + m + 1))
                        act.activation(hT[:, q % 2, m], PS[:, (q * NMC + m) % 4, 0:CAP], ACT.Gelu,
                                       bias=par[:, bass.ds(e * NMC + (PC_B1 + m), 1)]).then_inc(o_gelu, 1)

            for q in range(OVER):
                over_gelus(0, q, True)
            with act.Fori(1, OVER_ROUNDS) as i:
                with act.If(n_over > i * OVER):
                    for q in range(OVER):
                        over_gelus(i, q, False)

        @block.gpsimd
        def _(pool):
            step, settle = follower(pool, pool_own)
            pool.memset(ones[:], 1.0).then_inc(ones_ready, 1)
            pool.memset(zero_s[:], 0.0).then_inc(ones_ready, 1)
            step(pool.memset(bsum, 0.0))
            settle()
            for g, (lo, hi) in enumerate(LOADS):
                for s in range(NSH):
                    k = g * NSH + s
                    pool.wait_ge(bprod_ready, k + 1)
                    if k >= 1:
                        pool.wait_ge(bsum_ready, k)
                    pool.tensor_tensor(bsum[:, 0:hi - lo], bsum[:, 0:hi - lo], bprod[:, s, 0:hi - lo], ALU.add).then_inc(bsum_ready, 1)
            step(pool.memset(st[:, 64:64 + NT], -0.5))
            settle()
            def inverse_root(k, lo, hi):
                pool.wait_ge(var_ready, k + 1)
                pool.tensor_tensor(st[:, 32 + lo:32 + hi], st[:, 24 + lo:24 + hi], st[:, 64 + lo:64 + hi], ALU.pow).then_inc(rstd_ready, 1)

            inverse_root(0, 0, NT)
            inverse_root(1, 0, NT // 2)
            inverse_root(2, NT // 2, NT)
            pool.wait_ge(tok_mm, NT)
            pool.wait_ge(sq_mm, 1)
            pool.wait_ge(h_ready, NT)
            pool.memset(a_s[:, :, :, :, 0:1].rearrange("p a b c d -> p (a b) c d"), 0.0).then_inc(azero_ready, 1)
            pool.memset(guard[:], 0.5 * LOG_GUARD).then_inc(azero_ready, 1)
            step(pool.memset(mask[:], 1.0))
            settle()
            pool.memset(mask[:].rearrange("p (b l) -> p b l", l=L)[:, :, L - 1:L], 0.0).then_inc(azero_ready, 1)
            pool.wait_ge(ld_cst, 16)
            for c in range(2):
                pool.tensor_copy(facts[:, :, :, c], cst[0:TP, CC_TOK + c * NT:CC_TOK + (c + 1) * NT].unsqueeze(2)
                                 .to_broadcast([TP, NT, NE])).then_inc(numbers_ready, 1)
            pool.memset(facts[:, :, :, 2], 1.0).then_inc(numbers_ready, 1)
            pool.memset(ones_b[:], 1.0).then_inc(tri_ready, 1)
            pool.tensor_copy(tri_b[:], tri).then_inc(tri_ready, 1)

            for j in range(NJ):
                pool.wait_ge(en_ready, j + 1)
                pool.wait_ge(dl_read_dve, j + 1)
                pool.tensor_tensor(delta[:, j], delta[:, j], sp_en[:, j], ALU.add).then_inc(spq_ready, 1)

            def inputs(s):
                g, j, k = s // NJ, s % NJ, s % 2
                if s < NJ:
                    pool.wait_ge(delta_ready, j + 1)
                    pool.tensor_tensor(dx[:, j], delta[:, j], xi[:, j], ALU.mult).then_inc(dx_ready, 1)
                    pool.wait_ge(dx_ready, j + 1)
                if j == 0:
                    pool.wait_ge(b_ready[g % 2], 16 * (g // 2 + 1))
                if s >= 2:
                    pool.wait_ge(scan_done, s - 1)
                pool.tensor_tensor(t1_s[:, k], dx[:, j].unsqueeze(1).to_broadcast([128, NG, N]), bb_n[:, g % 2], ALU.mult).then_inc(t1_ready, 1)

            inputs(0)
            for s in range(STEPS):
                if s + 1 < STEPS:
                    inputs(s + 1)
                product(pool, s, PD, NG * N, p_pool)
            inverse_root(3, 0, NT // 2)
            inverse_root(4, NT // 2, NT)
            pool.wait_ge(spare_zero, 32)
            pool.wait_ge(xn_stored, 16)

            def gather(tile, col, done):
                pool.sem_inc(pool_turns, 1)
                pool.indirect_dma_start(tile, None, xn[:], bass.IndirectOffsetOnAxis(ap=idx[:, col:col + 1], axis=0)).then_inc(done, 16)

            def add(src, col, done):
                pool.sem_inc(pool_turns, 1)
                pool.indirect_dma_start(out[:], bass.IndirectOffsetOnAxis(ap=idx[:, col:col + 1], axis=0), src, None,
                                        compute_op=ALU.add).then_inc(done, 16)

            def expert_io(i, first=False, final=False):
                for r in range(RING):
                    e = i * RING + r
                    pool.wait_ge(y_ready, e + 1)
                    if not (first and r == 0):
                        pool.wait_ge(added, e * 16)
                    add(y_s[:, r % 2], r, added)
                    if not (final and r >= 1):
                        q = (r + RING - 1) % RING
                        pool.wait_ge(idx_ready, e + RING)
                        gather(xg[:, q], q, ld_xg[q])
                    if final and r < 2:
                        over_gathers(0, over_half(r))

            def over_gathers(i, tiles):
                pool.wait_ge(o_idx, i + 1)
                for q in tiles:
                    gather(oxg[:, q], RING + q, o_ld_xg[q])

            def over_adds(i, first):
                for q in range(OVER):
                    with pool.If(n_over > i * OVER + q):
                        pool.wait_ge(o_y, i * OVER + (q + 1))
                        if first and q == 0:
                            pool.wait_ge(added, 16 * NE)
                        add(y_s[:, q % 2], RING + q, o_added)
                        pool.wait_ge(o_added, i * (16 * OVER) + 16 * (q + 1))

            for e in range(RING - 1):
                pool.wait_ge(idx_ready, e + 1)
                gather(xg[:, e], e, ld_xg[e])
            pool.wait_ge(out_init, 16)
            expert_io(0, first=True)
            with pool.Fori(1, NE // RING - 1) as i:
                expert_io(i)
            pool.wait_ge(eid_ready, 1)
            n_over = over_count(pool)
            expert_io(NE // RING - 1, final=True)
            over_adds(0, True)
            with pool.Fori(1, OVER_ROUNDS) as i:
                with pool.If(n_over > i * OVER):
                    over_gathers(i, range(OVER))
                    over_adds(i, False)

        @block.vector
        def _(dve):
            step, settle = follower(dve, dve_own)
            ex2, var, rstd, nm = (st[:, 8:8 + NT], st[:, 24:24 + NT], st[:, 32:32 + NT], st[:, 40:40 + NT])

            dve.wait_ge(ld_gb, 16)
            dve.tensor_copy(weff[:, :, D], gbs[:, GC_CNT:GC_CNT + NKC]).then_inc(cnt_ready, 1)

            def sum_squares(lo, hi):
                for c in range(max(1, lo), hi):
                    dve.wait_ge(sq_ready, c + 1)
                    if c >= 2:
                        dve.wait_ge(sq_sum, c - 1)
                    dve.tensor_tensor(xsq[:, 0], xsq[:, 0], xsq[:, c], ALU.add).then_inc(sq_sum, 1)

            for g, (lo, hi) in enumerate(LOADS):
                dve.wait_ge(ld_w[g], 16)
                for s in range(NSH):
                    settle()
                    for c in range(lo, hi):
                        k = GC_G + c * NSH + s
                        if s == 0:
                            step(dve.tensor_scalar(weff[:, c, 0:D], wsh_s[:, c, 0], gbs[:, k:k + 1], None, ALU.mult))
                        else:
                            ins = dve.scalar_tensor_tensor(out=weff[:, c, 0:D], in0=wsh_s[:, c, s], scalar=gbs[:, k:k + 1],
                                                           in1=weff[:, c, 0:D], op0=ALU.mult, op1=ALU.add)
                            if s == NSH - 1:
                                ins.then_inc(weff_ready, 1)
                            else:
                                step(ins)
                if g >= 1:
                    sum_squares(*LOADS[g - 1])
            sum_squares(*LOADS[-1])
            def minus_mean(t):
                dve.wait_ge(tok_mm, t + 1)
                step(dve.tensor_scalar(nm[:, t:t + 1], PS[0:TP, t, D:D + 1], -1.0 / F, None, ALU.mult))

            dve.wait_ge(g_mm, 1)
            step(dve.tensor_copy(gcol, PS[0:TP, 6, 0:D]))
            minus_mean(0)
            for t in range(NT):
                settle()
                if t + 1 < NT:
                    minus_mean(t + 1)
                step(dve.scalar_tensor_tensor(out=u[:, t], in0=gcol, scalar=nm[:, t:t + 1], in1=PS[0:TP, t, 0:D], op0=ALU.mult, op1=ALU.add))
            step(dve.tensor_tensor(ex2, nm, nm, ALU.mult))
            dve.wait_ge(sq_mm, 1)
            settle()
            step(dve.scalar_tensor_tensor(out=var, in0=PS[0:TP, 7, D:D + NT], scalar=1.0 / F, in1=ex2, op0=ALU.mult, op1=ALU.subtract))
            settle()
            dve.tensor_scalar(var, var, TOK_EPS, None, ALU.add).then_inc(var_ready, 1)
            step(dve.tensor_copy(bb_s, PS[0:TP, 7, 0:D]))

            bst = st[:, 92:92 + 6 * NT].rearrange("p (t s) -> p t s", s=6)
            mv = st[:, 80:80 + 2 * NT].rearrange("p (t s) -> p t s", s=2)

            def layernorm(k, row, ready):
                for h in range(2):
                    tiles = range(h * NT // 2, (h + 1) * NT // 2)
                    row(tiles[0])
                    for t in tiles:
                        if t < tiles[-1]:
                            row(t + 1)
                        dve.wait_ge(ready, t + 1)
                        step(dve.bn_stats(bst[:, t], (h1, h2)[k][:, t]))
                    settle()
                    for t in tiles:
                        step(dve.bn_aggr(mv[:, t], bst[:, t]))
                    settle()
                    lo, hi = tiles[0], tiles[-1] + 1
                    dve.tensor_scalar(var[:, lo:hi], mv[:, lo:hi, 1], LN_EPS, None, ALU.add).then_inc(var_ready, 1)
                for h in range(2):
                    dve.wait_ge(rstd_ready, 2 * k + h + 2)
                    for t in range(h * NT // 2, (h + 1) * NT // 2):
                        dve.tensor_scalar(un[:, t], (h1, h2)[k][:, t], mv[:, t, 0:1], rstd[:, t:t + 1],
                                          ALU.subtract, ALU.mult).then_inc(un_ready, 1)
                for h in range(2):
                    dve.wait_ge(unT_mm, 2 * k + h + 1)
                    dve.tensor_copy(unT[:, 1, h * HB:(h + 1) * HB], PS[0:HALF_D, 2 + h, 0:HB]).then_inc(unT_high, 1)

            def embedding(t):
                dve.scalar_tensor_tensor(out=h1[:, t], in0=u[:, t], scalar=rstd[:, t:t + 1], in1=bb_s,
                                         op0=ALU.mult, op1=ALU.add).then_inc(h_ready, 1)

            dve.wait_ge(rstd_ready, 1)
            settle()
            layernorm(0, embedding, h_ready)
            dve.wait_ge(ld_par, 16)
            for j in range(NJ):
                dve.wait_ge(tap_ready, j + 1)
                for back in range(1, KS):
                    k = PC_CONVW + j * KS + KS - 1 - back
                    settle()
                    for h in range(2):
                        x_in = PS[:, WIN_BANK[j] + h, 0:HB].rearrange("p (b l) -> p b l", l=L)
                        x_out = xc[:, j, h * HB:(h + 1) * HB].rearrange("p (b l) -> p b l", l=L)
                        ins = dve.scalar_tensor_tensor(out=x_out[:, :, back:], in0=x_in[:, :, 0:L - back], scalar=par[:, k:k + 1],
                                                       in1=x_out[:, :, back:], op0=ALU.mult, op1=ALU.add)
                        if back < KS - 1 or h == 0:
                            step(ins)
                        else:
                            ins.then_inc(conv_done, 1)

            def skipped(j):
                dve.wait_ge(xi_ready, j + 1)
                dve.wait_ge(gate_ready, j + 1)
                dve.scalar_tensor_tensor(out=skip[:, j], in0=xi[:, j], scalar=par[:, PC_D + j:PC_D + j + 1], in1=sres[:, j],
                                         op0=ALU.mult, op1=ALU.mult).then_inc(skip_ready, 1)

            def scales(lo, hi, n):
                dve.wait_ge(aexp_ready, n)
                for k, f in ((1, -1.0), (2, -0.5)):
                    dve.tensor_scalar(av[:, k, lo * NST:hi * NST], av[:, 0, lo * NST:hi * NST], f, None, ALU.mult).then_inc(av_ready, 1)

            skipped(0)
            dve.wait_ge(xdbl_mm, 1)
            dve.tensor_copy(xdbl.rearrange("p (h n) -> p h n", h=2), PS[0:XW, 2:4, 0:HB]).then_inc(xdbl_ready, 1)
            skipped(1)
            scales(0, 1, 1)
            for j in range(NJ):
                dve.wait_ge(dl_read_act, j + 1)
                dve.tensor_scalar(delta[:, j].rearrange("p (h n) -> p h n", h=2), PS[:, DL_BANK[j]:DL_BANK[j] + 2, 0:HB],
                                  par[:, PC_BDT + j:PC_BDT + j + 1], 0.0, ALU.add, ALU.max).then_inc(dl_read_dve, 1)
            for j in range(NJ):
                dve.wait_ge(en_ready, j + 1)
                dve.tensor_scalar(dx[:, j], sp_en[:, j], 1.0, 1.0, ALU.add, ALU.subtract).then_inc(corr_ready, 1)
            skipped(2)
            dve.wait_ge(azero_ready, 3)
            for j in range(NJ):
                dve.wait_ge(ln_ready, j + 1)
                dve.wait_ge(corr_ready, j + 1)
                step(dve.tensor_tensor(dx[:, j], sp_ln[:, j], dx[:, j], ALU.subtract))
                settle()
                dve.wait_ge(spq_ready, j + 1)
                dve.tensor_tensor(delta[:, j], delta[:, j], dx[:, j], ALU.add).then_inc(delta_ready, 1)
                dve.wait_ge(delta_ready, j + 1)
                step(dve.tensor_tensor_scan(rsum[:, j, 0:N][:, ::-1], mask[:, 0:N][:, ::-1], delta[:, j][:, ::-1], 0.0, ALU.mult, ALU.add))
                settle()
                dve.memset(rsum[:, j, L:N + 1:L], 0.0).then_inc(rsum_ready, 1)
                if j == 0:
                    scales(1, NJ, 2)

            def guarded(s):
                k = s % 2
                dve.wait_ge(scan_done, s + 1)
                dve.scalar_tensor_tensor(out=w_s[:, k], in0=th_s[:, k], scalar=1.0, in1=w_s[:, k],
                                         op0=ALU.add, op1=ALU.mult).then_inc(wg_ready, 1)

            for s in range(STEPS + 1):
                k = s % 2
                if s >= 1:
                    guarded(s - 1)
                if s < STEPS:
                    dve.wait_ge(a_ready, s + 1)
                    dve.wait_ge(t1_ready, s + 1)
                    if s >= 2:
                        wait_product(dve, s - 2)
                    dve.tensor_tensor_scan(w_s[:, k].rearrange("p n l -> p (n l)"), a_s[:, k].rearrange("p n b l -> p (n b l)"),
                                           t1_s[:, k].rearrange("p n l -> p (n l)"), 0.0, ALU.mult, ALU.add).then_inc(scan_done, 1)
                if s >= 1:
                    product(dve, s - 1, 0, PD, p_dve)
            dve.wait_ge(p_used, STEPS)
            for j in range(NJ):
                dve.tensor_tensor(dx[:, j], PSF[:, 4 * 512 + j * N:4 * 512 + (j + 1) * N], sres[:, j], ALU.mult).then_inc(y2_ready, 1)

            def residual(t):
                dve.wait_ge(wout_mm, t // 2 + 1)
                dve.tensor_tensor(h2[:, t], PS[0:TP, t // 2, (t % 2) * D:(t % 2 + 1) * D], h1[:, t], ALU.add).then_inc(h2_ready, 1)

            layernorm(1, residual, h2_ready)

            def sets(v):
                return v[:, :, 0:G], v[:, :, G:].rearrange("p t (g e) -> p t g e", g=G)

            def per_set(v):
                return v[:, 0:NT], v[:, NT:].rearrange("p (t g) -> p t g", g=G)

            def spread(v):
                a, b = per_set(v)
                return a.unsqueeze(2).to_broadcast([TP, NT, G]), b.unsqueeze(3).to_broadcast([TP, NT, G, E])

            def flat(v):
                return v.rearrange("p t c -> p (t c)")

            def reduced(to, v, op):
                for o, x in zip(per_set(to), sets(v)):
                    step(dve.tensor_reduce(o, x, AX_X, op))

            def with_sets(to, v, m, op):
                for o, x, y in zip(sets(to), sets(v), spread(m)):
                    last = dve.tensor_tensor(o, x, y, op)
                    step(last) if to is not ex else last.then_inc(ex_in, 1)

            def best(k, v):
                reduced(mx[:, k], v, ALU.max)
                settle()
                with_sets(top[:, k], v, mx[:, k], ALU.is_equal)
                settle()
                step(dve.tensor_tensor_scan(flat(tie), cst[0:TP, CC_RST:CC_J], flat(top[:, k]), 0.0, ALU.mult, ALU.add))
                settle()
                if k == 0:
                    with_sets(ex, v, mx[:, 0], ALU.subtract)
                step(dve.scalar_tensor_tensor(out=flat(top[:, k]), in0=flat(tie), scalar=1.0, in1=flat(top[:, k]),
                                              op0=ALU.is_equal, op1=ALU.mult))
                settle()

            dve.wait_ge(rt_mm, 1)
            dve.wait_ge(ld_small, 16 * 5)
            step(dve.tensor_tensor(rl, PS[0:TP, 4, 0:NT * (G + NE)].rearrange("p (t c) -> p t c", t=NT),
                                   rbias[:].unsqueeze(1).to_broadcast([TP, NT, G + NE]), ALU.add))
            settle()
            best(0, rl)
            step(dve.scalar_tensor_tensor(out=flat(rl2), in0=flat(top[:, 0]), scalar=-1e30, in1=flat(rl), op0=ALU.mult, op1=ALU.add))
            settle()
            best(1, rl2)
            both = top[:, 0]
            step(dve.tensor_tensor(flat(both), flat(both), flat(top[:, 1]), ALU.add))
            settle()
            in_group, in_set = sets(both)
            dve.tensor_tensor(msk[:].rearrange("p t (g e) -> p t g e", g=G), in_set, in_group.unsqueeze(3).to_broadcast([TP, NT, G, E]),
                              ALU.mult).then_inc(msk_ready, 1)
            dve.wait_ge(ex_out, 1)
            step(dve.tensor_tensor(flat(ex), flat(ex), flat(both), ALU.mult))
            settle()
            reduced(sums, ex, ALU.add)
            settle()
            step(dve.reciprocal(sums, sums))
            settle()
            exg, exe = sets(ex)
            sum_e = per_set(sums)[1]
            step(dve.tensor_tensor(exg, exg, spread(sums)[0], ALU.mult))
            settle()
            step(dve.tensor_tensor(sum_e, sum_e, exg, ALU.mult))
            settle()
            dve.tensor_tensor(comb.rearrange("p t (g e) -> p t g e", g=G), exe, spread(sums)[1], ALU.mult).then_inc(comb_ready, 1)
            dve.wait_ge(msk_ready, 1)
            step(dve.tensor_scalar(posm, msk[:], 1e6, 1e6, ALU.mult, ALU.subtract))
            dve.wait_ge(comb_ready, 1)
            dve.tensor_copy(facts[:, :, :, 3], comb).then_inc(facts_ready, 1)
            dve.wait_ge(facts_ready, 1)
            step(dve.tensor_tensor(rest, comb, facts[:, :, :, 3], ALU.subtract))
            settle()
            dve.tensor_copy(facts[:, :, :, 4], rest).then_inc(facts_ready, 1)
            dve.wait_ge(facts_ready, 2)
            step(dve.tensor_tensor(rest, rest, facts[:, :, :, 4], ALU.subtract))
            settle()
            dve.tensor_copy(facts[:, :, :, 5], rest).then_inc(facts_ready, 1)
            dve.wait_ge(cnt_mm, 1)
            step(dve.tensor_tensor(posm, PS[0:TP, 5, 0:NT * NE].rearrange("p (t e) -> p t e", t=NT), posm, ALU.add))
            dve.tensor_copy(ov[:, 6], PS[:, 5, NT * NE:(NT + 1) * NE]).then_inc(cnt_read, 1)

            iota = cst[0:TP, CC_IOTA:CC_IOTA + CAP]

            def one_hot(o, pos):
                return dve.tensor_tensor(o, pos.to_broadcast([TP, NT, CAP]), iota.unsqueeze(1).to_broadcast([TP, NT, CAP]), ALU.is_equal)

            def slots(lo, hi, psum_lo, own, base):
                f = PS[:, 7, psum_lo * 8:(psum_lo + hi - lo) * 8].rearrange("p (q r) -> p q r", r=8)
                k = calc[:, lo:hi]
                dve.tensor_copy(k[:, :, 1:4], f[:, :, 1:4]).then_inc(own, 1)
                dve.wait_ge(own, base + 1)
                dve.scalar_tensor_tensor(out=k[:, :, 0:1], in0=f[:, :, 0:1], scalar=32.0, in1=k[:, :, 1:2],
                                         op0=ALU.mult, op1=ALU.add).then_inc(own, 1)
                dve.tensor_tensor(k[:, :, 3:4], f[:, :, 4:5], k[:, :, 3:4], ALU.add).then_inc(own, 1)
                dve.wait_ge(own, base + 3)
                dve.scalar_tensor_tensor(out=k[:, :, 0:1], in0=k[:, :, 2:3], scalar=cst[:, CC_SPARE + 1:CC_SPARE + 2],
                                         in1=k[:, :, 0:1], op0=ALU.mult, op1=ALU.add).then_inc(own, 1)
                dve.tensor_tensor(wgt[:, lo:hi].unsqueeze(2), f[:, :, 5:6], k[:, :, 3:4], ALU.add).then_inc(own, 1)
                dve.wait_ge(own, base + 5)
                return dve.tensor_scalar(idx[:, lo:hi].unsqueeze(2), k[:, :, 0:1], cst[:, CC_SPARE:CC_SPARE + 1], None, ALU.add)

            def first_hot(e):
                one_hot(oh[:, e], posm[:, :, e:e + 1]).then_inc(oh_ready, 1)

            def first_slots(e):
                dve.wait_ge(idx_mm, e + 1)
                slots(e, e + 1, e, slots_own, 5 * e).then_inc(idx_ready, 1)

            settle()
            first_hot(0)
            first_hot(1)
            first_slots(0)
            first_hot(2)
            first_slots(1)
            dve.wait_ge(b2_mm, 1)
            dve.tensor_tensor(h1[:].rearrange("p (a b) d -> p a b d", b=2), PS[0:TP, 2:5, 0:2 * D].rearrange("p a (b d) -> p a b d", b=2),
                              h2[:].rearrange("p (a b) d -> p a b d", b=2), ALU.add).then_inc(b2_read, 1)
            def token_copy(i, r, first):
                e = i * RING + r
                dve.wait_ge(xgT_mm, e + 1)
                dve.tensor_copy(xgT[:, r % 2], PS[0:HALF_D, 6, 0:2 * CAP].rearrange("p (c n) -> p c n", c=2)).then_inc(xgT_ready, 1)

            def output_copy(i, r, first):
                e = i * RING + r
                dve.wait_ge(w2_done, e + 1)
                if not (first and r < 2):
                    dve.wait_ge(added, (e - 1) * 16)
                dve.tensor_scalar(y_s[:, r % 2], PS[:, 4 + r % 2, 0:D], wgt[:, r:r + 1], None, ALU.mult).then_inc(y_ready, 1)

            def copies(i, first=False, final=False):
                for r in range(RING):
                    e = i * RING + r
                    if r + 1 < RING:
                        token_copy(i, r + 1, first)
                    elif not final:
                        token_copy(i + 1, 0, False)
                    if not final:
                        dve.wait_ge(idx_mm, e + 1)
                        pos = posm[:, :, e + RING:e + RING + 1] if first else posm[:, :, bass.ds(e + RING, 1)]
                        one_hot(oh[:, r], pos).then_inc(oh_ready, 1)
                    if first and r < RING - 1:
                        for q in over_pair(r):
                            over_hot(0, q)
                    output_copy(i, r, first)
                    if first and r == RING - 1:
                        over_slots(0, True)
                    if final and r >= 2:
                        for q in over_half(r - 2):
                            over_token_copy(0, q)
                    if not (final and r >= 1):
                        q = (r + RING - 1) % RING
                        dve.wait_ge(idx_mm, e + RING)
                        if not (first and r == 0):
                            dve.wait_ge(added, e * 16)
                        slots(q, q + 1, q, slots_own, (e + RING - 1) * 5).then_inc(idx_ready, 1)

            def over_hot(i, q):
                e = dve.value_load(eidi[0:1, bass.ds(i * OVER + q, 1)], min_val=0, max_val=NE - 1)
                dve.tensor_scalar(opos[:, q].unsqueeze(2), oposm[:, :, bass.ds(e, 1)], cst[0:TP, bass.ds(i * OVER + (CC_JC + q), 1)],
                                  None, ALU.subtract).then_inc(o_from, 1)
                dve.wait_ge(o_from, i * OVER + (q + 1))
                one_hot(ooh[:, q], opos[:, q].unsqueeze(2)).then_inc(o_oh, 1)

            def over_slots(i, first):
                dve.wait_ge(o_idx_mm, i + 1)
                if not first:
                    dve.wait_ge(o_added, i * (16 * OVER))
                slots(RING, RING + OVER, RING, o_own, i * 5).then_inc(o_idx, 1)

            def over_token_copy(i, q):
                dve.wait_ge(o_xgT_mm, i * OVER + (q + 1))
                dve.tensor_copy(oxgT[:, q], PS[0:HALF_D, 6 + q % 2, 0:2 * CAP].rearrange("p (c n) -> p c n", c=2)).then_inc(o_xgT, 1)

            def over_outputs(i, first):
                for q in range(OVER):
                    with dve.If(n_over > i * OVER + q):
                        dve.wait_ge(o_w2, i * OVER + (q + 1))
                        if first and q < 2:
                            dve.wait_ge(added, 16 * (NE - 1 + q))
                        else:
                            dve.wait_ge(o_added, i * (16 * OVER) + 16 * (q - 1))
                        dve.tensor_scalar(y_s[:, q % 2], PS[:, 4 + q % 2, 0:D], wgt[:, RING + q:RING + q + 1], None, ALU.mult).then_inc(o_y, 1)

            token_copy(0, 0, True)
            first_slots(2)
            first_hot(3)
            dve.wait_ge(cnt_read, 1)
            cnt = ov[:, 6]
            step(dve.tensor_scalar(ov[:, 0], cnt, float(CAP), None, ALU.is_gt))
            for q in range(2, (N + CAP - 1) // CAP):
                settle()
                step(dve.scalar_tensor_tensor(out=ov[:, 0], in0=cnt, scalar=float(q * CAP), in1=ov[:, 0], op0=ALU.is_gt, op1=ALU.add))
            step(dve.memset(ov[:, 1], 1.0))
            settle()
            step(dve.tensor_tensor_scan(ov[:, 2], ov[:, 1], ov[:, 0], 0.0, ALU.mult, ALU.add))
            settle()
            step(dve.tensor_tensor(ov[:, 3], ov[:, 2], ov[:, 0], ALU.subtract))
            step(dve.tensor_tensor(ofs, ov[:, 2].unsqueeze(1).to_broadcast([128, OVER_PAD, NE]),
                                   cst[:, CC_J:CC_J + OVER_PAD].unsqueeze(2).to_broadcast([128, OVER_PAD, NE]), ALU.is_le))
            settle()
            step(dve.tensor_scalar(ov[:, 4], ov[:, 3], float(CAP), float(CAP), ALU.mult, ALU.subtract))
            step(dve.tensor_reduce(ov[:, 5, 0:OVER_PAD], ofs, AX_X, ALU.add))
            step(dve.tensor_copy(ov[:, 5, OVER_PAD:OVER_PAD + 1], ov[:, 2, NE - 1:NE]))
            settle()
            step(dve.tensor_tensor(oposm, posm, ov[0:TP, 4].unsqueeze(1).to_broadcast([TP, NT, NE]), ALU.add))
            step(dve.tensor_scalar(ov[:, 5, 0:OVER_PAD], ov[:, 5, 0:OVER_PAD], float(NE - 1), None, ALU.min))
            settle()
            dve.tensor_copy(eidi[:], ov[:, 5, 0:OVER_PAD + 1]).then_inc(eid_ready, 1)

            dve.wait_ge(eid_ready, 1)
            n_over = over_count(dve)
            copies(0, first=True)
            with dve.Fori(1, NE // RING - 1) as i:
                copies(i)
            copies(NE // RING - 1, final=True)
            over_outputs(0, True)
            with dve.Fori(1, OVER_ROUNDS) as i:
                with dve.If(n_over > i * OVER):
                    for q in range(OVER):
                        over_hot(i, q)
                    over_slots(i, False)
                    for q in range(OVER):
                        over_token_copy(i, q)
                    over_outputs(i, False)


def _layouts(x, gamma, beta, W):
    xp = np.pad(x, ((0, 0), (1, 1), (1, 1), (0, 0)))
    rows = (np.arange(GRID) * PATCH)[:, None] + np.arange(WIN)[None, :]
    p = xp[:, rows][:, :, :, rows]
    p = p.transpose(2, 4, 5, 0, 1, 3).reshape(NKC, KC, N).transpose(1, 0, 2)
    moves = ((0, 0), (0, 1), (0, -1), (1, 0), (-1, 0))

    def place(a):
        a = a.reshape(PATCH, PATCH, NSH, CH, -1)
        o = np.zeros((NSH, WIN, WIN, CH, a.shape[-1]), a.dtype)
        for s, (dy, dx) in enumerate(moves):
            o[s, 1 - dy:1 - dy + PATCH, 1 - dx:1 - dx + PATCH] = a[:, :, s]
        o = o.reshape(NSH, NKC, KC, -1)
        return o.transpose(2, 1, 0, 3)

    cnt = place(np.ones((F, 1), np.float32)).sum(2)[:, :, 0]
    gb = np.concatenate([place(gamma).reshape(KC, -1), place(beta).reshape(KC, -1), cnt, np.sqrt(cnt)], 1)
    return p, place(W), gb


def _constants():
    c = np.zeros((128, CC_N), np.float32)
    c[:, CC_ID:CC_ID + 128] = np.eye(128)
    c[:, CC_HALF:CC_HALF + 128] = 0.5 * np.eye(128)
    c[:TP, CC_TRI:CC_TRI + TP] = np.triu(np.ones((TP, TP)), 1)
    c[:, CC_RST:CC_J] = 1.0
    c[:, CC_RST:CC_J].reshape(128, NT, G + NE)[:, :, [0] + [G + g * E for g in range(G)]] = 0.0
    c[:, CC_J:CC_J + OVER_PAD] = np.arange(OVER_PAD)
    c[:, CC_JC:CC_JC + OVER_PAD] = np.arange(OVER_PAD) * CAP
    c[:, CC_IOTA:CC_IOTA + CAP] = np.arange(CAP)
    number = np.arange(NT)[None, :] * TP + np.arange(TP)[:, None]
    c[:TP, CC_TOK:CC_TOK + NT] = number // 32
    c[:TP, CC_TOK + NT:CC_TOK + 2 * NT] = number % 32
    c[:, CC_SPARE] = N + np.arange(128)
    c[:, CC_SPARE + 1] = -c[:, CC_SPARE]
    return c


def kernel(**inputs):
    import numpy as _np
    import concourse.bacc as _bacc
    from concourse import mybir as _mybir
    from concourse.bass_utils import run_bass_kernel_spmd as _run

    v = {k: _np.asarray(a) for k, a in inputs.items()}

    def chunked(a):
        return a.reshape(NJ, 128, -1).transpose(1, 0, 2).reshape(128, -1)

    x_t, w_sh, gb = _layouts(v["x"], v["L0_tok_gamma"], v["L0_tok_beta"], v["L0_tok_W"])
    params = _np.concatenate(
        [chunked(v["L0_attn_" + k]) for k in ("conv_w", "conv_b", "b_dt", "A_log", "Dp", "W_x", "W_out")]
        + [v["L0_ffn_b1"].reshape(NE, NMC, 128).transpose(2, 0, 1).reshape(128, -1)], 1)
    rows = _np.concatenate([v["L0_tok_b"], v["L0_ffn_bg"], v["L0_ffn_bge"].reshape(-1)])[None]
    w_rt = _np.concatenate([v["L0_ffn_Wg"], v["L0_ffn_Wge"].transpose(1, 0, 2).reshape(D, NE)], 1)
    given = {"x_t": x_t, "w_sh": w_sh, "gb": gb, "consts": _constants(), "params": params, "rows": rows,
             "w_in": v["L0_attn_W_in"], "w_dt": v["L0_attn_W_dt"], "w_rt": w_rt,
             "w1": v["L0_ffn_W1"], "w2": v["L0_ffn_W2"], "b2": v["L0_ffn_b2"]}
    nc = _bacc.Bacc("TRN2", target_bir_lowering=False, num_devices=1)
    arrays, args = {}, []
    for name, a in given.items():
        a = _np.ascontiguousarray(a)
        arrays[f"in_{name}"] = a
        args.append(nc.dram_tensor(f"in_{name}", a.shape, _mybir.dt.from_np(a.dtype), kind="ExternalInput").ap())
    o = nc.dram_tensor("out_0", (N + CAP, D), _mybir.dt.float32, kind="ExternalOutput").ap()
    xn = nc.dram_tensor("xn", (N + CAP, D), _mybir.dt.float32).ap()
    bc = nc.dram_tensor("bc", (2 * NST, N), _mybir.dt.float32).ap()
    build_program(nc, *args, o, xn, bc)
    r = _run(nc, [arrays], core_ids=[0])
    return r.results[0]["out_0"][:N].reshape(BATCH, L, D)
```
